# Optimizing a Trainium2 kernel written in Bass

```python
import numpy as np
import jax
import jax.numpy as jnp

def _softmax(x, axis=-1):
    return jax.nn.softmax(x, axis=axis)

def _gelu(x):
    return jax.nn.gelu(x, approximate=True)

def _silu(x):
    return jax.nn.silu(x)

def _sigmoid(x):
    return jax.nn.sigmoid(x)

def _layernorm(x, axis=-1, eps=1e-05):
    m = jnp.mean(x, axis=axis, keepdims=True)
    v = jnp.var(x, axis=axis, keepdims=True)
    return (x - m) / jnp.sqrt(v + eps)

def _scatter_add(tgt, idx, src, axis=0):
    return tgt.at[idx].add(src)

def _segment_sum(src, seg, n):
    return jax.ops.segment_sum(src, seg, n)
kernel_name = 'mk_vit_tower_d1_tok_img1024_r4_512eac'

def setup_inputs(seed: int=0):
    np.random.seed(seed)
    _w = jnp.asarray

    def _rec_inputs():
        import jax
        import jax.numpy as jnp
        _rk = jax.random.key(seed)
        x = -0.00016672 + 0.999947 * jax.random.normal(jax.random.fold_in(_rk, 1), (64, 3, 96, 96), jnp.float32)
        return x
    x = _rec_inputs()

    def _L0_tok_setup():
        import jax, jax.numpy as jnp
        import numpy as np
        PATCH = 16

        def _patchify(x, p):
            B, C, H, W = x.shape
            nh, nw = (H // p, W // p)
            x = x.reshape(B, C, nh, p, nw, p)
            x = x.transpose(0, 2, 4, 1, 3, 5)
            return x.reshape(B, nh * nw, C * p * p)
        key = jax.random.key(seed)
        k1, k2, k3, k4, k5 = jax.random.split(key, 5)
        B, C, H = (64, 3, 96)
        d_model = 256
        p = PATCH
        num_patches = (H // p) ** 2
        in_dim = p * p * C
        x = jax.random.normal(k1, (B, C, H, H), dtype=jnp.float32)
        bound = 1.0 / np.sqrt(in_dim)
        W = jax.random.uniform(k2, (d_model, in_dim), dtype=jnp.float32, minval=-bound, maxval=bound)
        b = jax.random.uniform(k3, (d_model,), dtype=jnp.float32, minval=-bound, maxval=bound)
        cls_token = jax.random.normal(k4, (1, 1, d_model), dtype=jnp.float32)
        pos_enc = jax.random.normal(k5, (1, num_patches + 1, d_model), dtype=jnp.float32)
        return {'x': x, 'W': W, 'b': b, 'cls_token': cls_token, 'pos_enc': pos_enc}
    _L0_tok_all = _L0_tok_setup()
    _L0_tok_in = {k: v for k, v in _L0_tok_all.items() if k in ('W', 'b', 'cls_token', 'pos_enc')}
    del _L0_tok_all

    def _L0_attn_setup():
        import jax, jax.numpy as jnp
        import numpy as np
        DIM = 256
        N_HEADS = 16
        HEAD_DIM = DIM // N_HEADS
        HIDDEN = 704
        WINDOW_PER_SIDE = 128
        EPS = 1e-05
        THETA = 10000.0

        def rope_cos_sin(seqlen, head_dim):
            freqs = 1.0 / THETA ** (jnp.arange(0, head_dim, 2, dtype=jnp.float32) / head_dim)
            t = jnp.arange(seqlen, dtype=jnp.float32)
            ang = jnp.outer(t, freqs)
            return (jnp.cos(ang), jnp.sin(ang))

        def apply_rope(x, cos, sin):
            xr = x[..., 0::2]
            xi = x[..., 1::2]
            c = cos[None, :, None, :]
            s = sin[None, :, None, :]
            or_ = xr * c - xi * s
            oi_ = xr * s + xi * c
            return jnp.stack([or_, oi_], axis=-1).reshape(x.shape)

        def layernorm(x, g, b):
            mu = jnp.mean(x, axis=-1, keepdims=True)
            var = jnp.mean(jnp.square(x - mu), axis=-1, keepdims=True)
            return (x - mu) * jax.lax.rsqrt(var + EPS) * g + b

        def attention(x, wq, wk, wv, wo):
            b, s, _ = x.shape
            scale = HEAD_DIM ** (-0.5)
            q = (x @ wq).reshape(b, s, N_HEADS, HEAD_DIM)
            k = (x @ wk).reshape(b, s, N_HEADS, HEAD_DIM)
            v = (x @ wv).reshape(b, s, N_HEADS, HEAD_DIM)
            cos, sin = rope_cos_sin(s, HEAD_DIM)
            q = apply_rope(q, cos, sin)
            k = apply_rope(k, cos, sin)
            i = jnp.arange(s)[:, None]
            j = jnp.arange(s)[None, :]
            mask = (j <= i) & (i - j <= WINDOW_PER_SIDE)
            scores = jnp.einsum('bqhd,bkhd->bhqk', q, k) * scale
            scores = jnp.where(mask[None, None], scores, jnp.finfo(scores.dtype).min)
            probs = jax.nn.softmax(scores, axis=-1)
            out = jnp.einsum('bhqk,bkhd->bqhd', probs, v).reshape(b, s, -1)
            return out @ wo

        def ffn(x, w1, w2, w3):
            return jax.nn.silu(x @ w1) * (x @ w3) @ w2
        key = jax.random.key(seed)
        ks = jax.random.split(key, 9)
        sd = 0.02
        x = jax.random.normal(ks[0], (4, 512, DIM), dtype=jnp.float32)
        wq = jax.random.normal(ks[1], (DIM, DIM), dtype=jnp.float32) * sd
        wk = jax.random.normal(ks[2], (DIM, DIM), dtype=jnp.float32) * sd
        wv = jax.random.normal(ks[3], (DIM, DIM), dtype=jnp.float32) * sd
        wo = jax.random.normal(ks[4], (DIM, DIM), dtype=jnp.float32) * sd
        w1 = jax.random.normal(ks[5], (DIM, HIDDEN), dtype=jnp.float32) * sd
        w2 = jax.random.normal(ks[6], (HIDDEN, DIM), dtype=jnp.float32) * sd
        w3 = jax.random.normal(ks[7], (DIM, HIDDEN), dtype=jnp.float32) * sd
        ln1_g = jnp.ones((DIM,), jnp.float32)
        ln1_b = jnp.zeros((DIM,), jnp.float32)
        ln2_g = jnp.ones((DIM,), jnp.float32)
        ln2_b = jnp.zeros((DIM,), jnp.float32)
        return dict(x=x, wq=wq, wk=wk, wv=wv, wo=wo, w1=w1, w2=w2, w3=w3, ln1_g=ln1_g, ln1_b=ln1_b, ln2_g=ln2_g, ln2_b=ln2_b)
    _L0_attn_all = _L0_attn_setup()
    _L0_attn_in = {k: v for k, v in _L0_attn_all.items() if k in ('wq', 'wk', 'wv', 'wo', 'w1', 'w2', 'w3', 'ln1_g', 'ln1_b', 'ln2_g', 'ln2_b')}
    del _L0_attn_all

    def _L0_ffn_setup():
        import jax, jax.numpy as jnp
        import numpy as np
        B, S, H, F, E, K = (2, 512, 256, 1024, 8, 2)

        def _init_w(key, shape, fan_in):
            return jax.random.normal(key, shape, jnp.float32) * fan_in ** (-0.5)

        def _ffn(x, wi, bi, wo, bo):
            return jax.nn.selu(x @ wi + bi) @ wo + bo
        key = jax.random.key(seed)
        ks = jax.random.split(key, 6)
        return {'x': jax.random.normal(ks[0], (B, S, H), jnp.float32), 'gate_wi': _init_w(ks[1], (H, F), H), 'gate_bi': jnp.zeros((F,), jnp.float32), 'gate_wo': _init_w(ks[2], (F, H), F), 'gate_bo': jnp.zeros((H,), jnp.float32), 'exp_wi': _init_w(ks[3], (E, H, F), H), 'exp_bi': jnp.zeros((E, F), jnp.float32), 'exp_wo': _init_w(ks[4], (E, F, H), F), 'exp_bo': jnp.zeros((E, H), jnp.float32)}
    _L0_ffn_all = _L0_ffn_setup()
    _L0_ffn_in = {k: v for k, v in _L0_ffn_all.items() if k in ('gate_wi', 'gate_bi', 'gate_wo', 'gate_bo', 'exp_wi', 'exp_bi', 'exp_wo', 'exp_bo')}
    del _L0_ffn_all
    return {'x': x, 'L0_tok_W': _L0_tok_in['W'], 'L0_tok_b': _L0_tok_in['b'], 'L0_tok_cls_token': _L0_tok_in['cls_token'], 'L0_tok_pos_enc': _L0_tok_in['pos_enc'], 'L0_attn_wq': _L0_attn_in['wq'], 'L0_attn_wk': _L0_attn_in['wk'], 'L0_attn_wv': _L0_attn_in['wv'], 'L0_attn_wo': _L0_attn_in['wo'], 'L0_attn_w1': _L0_attn_in['w1'], 'L0_attn_w2': _L0_attn_in['w2'], 'L0_attn_w3': _L0_attn_in['w3'], 'L0_attn_ln1_g': _L0_attn_in['ln1_g'], 'L0_attn_ln1_b': _L0_attn_in['ln1_b'], 'L0_attn_ln2_g': _L0_attn_in['ln2_g'], 'L0_attn_ln2_b': _L0_attn_in['ln2_b'], 'L0_ffn_gate_wi': _L0_ffn_in['gate_wi'], 'L0_ffn_gate_bi': _L0_ffn_in['gate_bi'], 'L0_ffn_gate_wo': _L0_ffn_in['gate_wo'], 'L0_ffn_gate_bo': _L0_ffn_in['gate_bo'], 'L0_ffn_exp_wi': _L0_ffn_in['exp_wi'], 'L0_ffn_exp_bi': _L0_ffn_in['exp_bi'], 'L0_ffn_exp_wo': _L0_ffn_in['exp_wo'], 'L0_ffn_exp_bo': _L0_ffn_in['exp_bo']}

def reference(x, L0_tok_W, L0_tok_b, L0_tok_cls_token, L0_tok_pos_enc, L0_attn_wq, L0_attn_wk, L0_attn_wv, L0_attn_wo, L0_attn_w1, L0_attn_w2, L0_attn_w3, L0_attn_ln1_g, L0_attn_ln1_b, L0_attn_ln2_g, L0_attn_ln2_b, L0_ffn_gate_wi, L0_ffn_gate_bi, L0_ffn_gate_wo, L0_ffn_gate_bo, L0_ffn_exp_wi, L0_ffn_exp_bi, L0_ffn_exp_wo, L0_ffn_exp_bo):
    import jax
    import jax.numpy as jnp

    def _L0_tok_ref(x, W, b, cls_token, pos_enc):
        import jax, jax.numpy as jnp
        import numpy as np
        PATCH = 16

        def _patchify(x, p):
            B, C, H, W = x.shape
            nh, nw = (H // p, W // p)
            x = x.reshape(B, C, nh, p, nw, p)
            x = x.transpose(0, 2, 4, 1, 3, 5)
            return x.reshape(B, nh * nw, C * p * p)
        B = x.shape[0]
        patches = _patchify(x, PATCH)
        proj = jnp.einsum('bnf,df->bnd', patches, W) + b
        cls = jnp.broadcast_to(cls_token, (B, 1, cls_token.shape[-1]))
        out = jnp.concatenate([cls, proj], axis=1) + pos_enc
        return out

    def _L0_attn_ref(x, wq, wk, wv, wo, w1, w2, w3, ln1_g, ln1_b, ln2_g, ln2_b):
        import jax, jax.numpy as jnp
        import numpy as np
        DIM = 256
        N_HEADS = 16
        HEAD_DIM = DIM // N_HEADS
        HIDDEN = 704
        WINDOW_PER_SIDE = 128
        EPS = 1e-05
        THETA = 10000.0

        def rope_cos_sin(seqlen, head_dim):
            freqs = 1.0 / THETA ** (jnp.arange(0, head_dim, 2, dtype=jnp.float32) / head_dim)
            t = jnp.arange(seqlen, dtype=jnp.float32)
            ang = jnp.outer(t, freqs)
            return (jnp.cos(ang), jnp.sin(ang))

        def apply_rope(x, cos, sin):
            xr = x[..., 0::2]
            xi = x[..., 1::2]
            c = cos[None, :, None, :]
            s = sin[None, :, None, :]
            or_ = xr * c - xi * s
            oi_ = xr * s + xi * c
            return jnp.stack([or_, oi_], axis=-1).reshape(x.shape)

        def layernorm(x, g, b):
            mu = jnp.mean(x, axis=-1, keepdims=True)
            var = jnp.mean(jnp.square(x - mu), axis=-1, keepdims=True)
            return (x - mu) * jax.lax.rsqrt(var + EPS) * g + b

        def attention(x, wq, wk, wv, wo):
            b, s, _ = x.shape
            scale = HEAD_DIM ** (-0.5)
            q = (x @ wq).reshape(b, s, N_HEADS, HEAD_DIM)
            k = (x @ wk).reshape(b, s, N_HEADS, HEAD_DIM)
            v = (x @ wv).reshape(b, s, N_HEADS, HEAD_DIM)
            cos, sin = rope_cos_sin(s, HEAD_DIM)
            q = apply_rope(q, cos, sin)
            k = apply_rope(k, cos, sin)
            i = jnp.arange(s)[:, None]
            j = jnp.arange(s)[None, :]
            mask = (j <= i) & (i - j <= WINDOW_PER_SIDE)
            scores = jnp.einsum('bqhd,bkhd->bhqk', q, k) * scale
            scores = jnp.where(mask[None, None], scores, jnp.finfo(scores.dtype).min)
            probs = jax.nn.softmax(scores, axis=-1)
            out = jnp.einsum('bhqk,bkhd->bqhd', probs, v).reshape(b, s, -1)
            return out @ wo

        def ffn(x, w1, w2, w3):
            return jax.nn.silu(x @ w1) * (x @ w3) @ w2
        h = x + attention(layernorm(x, ln1_g, ln1_b), wq, wk, wv, wo)
        out = h + ffn(layernorm(h, ln2_g, ln2_b), w1, w2, w3)
        return out

    def _L0_ffn_ref(x, gate_wi, gate_bi, gate_wo, gate_bo, exp_wi, exp_bi, exp_wo, exp_bo):
        import jax, jax.numpy as jnp
        import numpy as np
        B, S, H, F, E, K = (2, 512, 256, 1024, 8, 2)

        def _init_w(key, shape, fan_in):
            return jax.random.normal(key, shape, jnp.float32) * fan_in ** (-0.5)

        def _ffn(x, wi, bi, wo, bo):
            return jax.nn.selu(x @ wi + bi) @ wo + bo
        Bb, Ss, Hh = x.shape
        xf = x.reshape(-1, Hh)
        gate_logits = _ffn(xf, gate_wi, gate_bi, gate_wo, gate_bo)
        topv, topi = jax.lax.top_k(gate_logits, K)
        topv = topv / jnp.sum(topv, axis=-1, keepdims=True)
        onehot = (topi[..., None] == jnp.arange(E)).astype(x.dtype)
        w = jnp.einsum('nk,nke->ne', topv, onehot)
        h = jax.nn.selu(jnp.einsum('nh,ehf->enf', xf, exp_wi) + exp_bi[:, None, :])
        out_e = jnp.einsum('enf,efh->enh', h, exp_wo) + exp_bo[:, None, :]
        out = jnp.einsum('enh,ne->nh', out_e, w)
        return out.reshape(Bb, Ss, Hh)
    h = _L0_tok_ref(x, L0_tok_W, L0_tok_b, L0_tok_cls_token, L0_tok_pos_enc)
    h = h + _L0_attn_ref(_layernorm(h, axis=-1), L0_attn_wq, L0_attn_wk, L0_attn_wv, L0_attn_wo, L0_attn_w1, L0_attn_w2, L0_attn_w3, L0_attn_ln1_g, L0_attn_ln1_b, L0_attn_ln2_g, L0_attn_ln2_b)
    h = h + _L0_ffn_ref(_layernorm(h, axis=-1), L0_ffn_gate_wi, L0_ffn_gate_bi, L0_ffn_gate_wo, L0_ffn_gate_bo, L0_ffn_exp_wi, L0_ffn_exp_bi, L0_ffn_exp_wo, L0_ffn_exp_bo)
    return h

_drawn_inputs = setup_inputs


def setup_inputs(seed=0):
    import zlib

    import numpy as np

    out = dict(_drawn_inputs(seed))
    spreads = {'L0_attn_ln1_g': (1.0, 0.6),
     'L0_attn_ln1_b': (0.0, 0.8),
     'L0_attn_ln2_g': (1.0, 0.6),
     'L0_attn_ln2_b': (0.0, 0.8),
     'L0_ffn_gate_bi': (0.0, 0.318),
     'L0_ffn_gate_bo': (0.0, 0.33),
     'L0_ffn_exp_bi': (0.0, 2.0),
     'L0_ffn_exp_bo': (0.0, 2.0)}
    factors = {'L0_tok_b': 2.67,
     'L0_attn_wq': 8.0,
     'L0_attn_wk': 8.0,
     'L0_attn_wv': 3.194,
     'L0_attn_wo': 2.938,
     'L0_attn_w1': 3.211,
     'L0_attn_w2': 3.223,
     'L0_attn_w3': 3.355,
     'L0_ffn_exp_wi': 2.765}
    for name, (base, spread) in spreads.items():
        noise = np.random.default_rng([zlib.crc32(name.encode()), seed]).standard_normal(out[name].shape)
        drawn = base * np.exp(spread * noise) if base else spread * noise
        out[name] = jnp.asarray(drawn.astype(out[name].dtype))
    for name, factor in factors.items():
        out[name] = (out[name] * factor).astype(out[name].dtype)
    return out
```

```python
from contextlib import ExitStack

import concourse.bass as bass
from concourse import mybir
import numpy as np

F32 = mybir.dt.float32
BF16 = mybir.dt.bfloat16
U32 = mybir.dt.uint32
ALU = mybir.AluOpType
ACT = mybir.ActivationFunctionType
AX = mybir.AxisListType

P = 128
IMAGES, CH, SIDE, PATCH = 64, 3, 96, 16
GRID = SIDE // PATCH
SEQ = GRID * GRID + 1
D = 256
DM = D // P
HEADS, HD = 16, 16
HIDDEN = 704
GLU = [min(P, HIDDEN - P * i) for i in range((HIDDEN + P - 1) // P)]
EXPERTS, FF = 8, 1024
FT = FF // P
PK = CH * PATCH * PATCH // P

GROUPS = 4
GI = IMAGES // GROUPS
GT = GI * SEQ
HALF = GT // 2
TILES = [(a, min(P, GT - a)) for a in range(0, GT, P)]
NT = len(TILES)
PAIRS = GI // 2
PITCH = 64
TOKENS = IMAGES * SEQ
SLOTS = 64
TURN = 4
CHUNKS = TOKENS // SLOTS
ROW = D + EXPERTS
LAMBDA, ALPHA = 1.0507009873554805, 1.6732632423543772
LA = LAMBDA * ALPHA
EPS = 1e-5
NEG = -1.0e30
PRIMED = 16

C_ID, C_TRI, C_MASK = 0, P, 2 * P
C_COS = C_MASK + 8 * SEQ
C_SIN = C_COS + NT * HD
C_IOTA = C_SIN + NT * HD
C_TOK = C_IOTA + NT * EXPERTS
C_HEAD = C_TOK + NT
C_PAR = C_HEAD + 4
C_PAD = C_PAR + 2
C_LNLA = C_PAD + SLOTS
C_ALL = C_LNLA + 1


def constants():
    c = np.zeros((P, C_ALL), np.float32)
    p = np.arange(P)
    c[:, C_ID:C_ID + P] = np.eye(P)
    c[:, C_TRI:C_TRI + P] = p[:, None] < p[None, :]
    key = np.tile(np.arange(SEQ), 8)
    c[:, C_MASK:C_MASK + 8 * SEQ] = np.where(key[None, :] <= (p % PITCH)[:, None], 0.0, NEG)
    freqs = (np.float32(1.0) / np.float32(10000.0) ** (np.arange(0, HD, 2, dtype=np.float32) / np.float32(HD))).astype(np.float32)
    for t, (a, n) in enumerate(TILES):
        ang = (((a + p) % SEQ).astype(np.float32)[:, None] * freqs[None, :]).astype(np.float32)
        c[:, C_COS + t * HD:C_COS + (t + 1) * HD] = np.repeat(np.cos(ang), 2, axis=1)
        s = np.repeat(np.sin(ang), 2, axis=1)
        s[:, 0::2] *= -1
        c[:, C_SIN + t * HD:C_SIN + (t + 1) * HD] = s
        c[:, C_IOTA + t * EXPERTS:C_IOTA + (t + 1) * EXPERTS] = np.where(p[:, None] < n, np.arange(EXPERTS)[None, :], -1)
        c[:, C_TOK + t] = a + p
    for j in range(4):
        c[:, C_HEAD + j] = (p // HD) % 4 == j
    for j in range(2):
        c[:, C_PAR + j] = (p // HD) % 2 == j
    c[:, C_PAD:C_PAD + SLOTS] = TOKENS + np.arange(SLOTS)[None, :]
    c[:, C_LNLA] = np.log(LA)
    return c


DENSE = [0, 1, 2, 3]
SCORE = [4, 6]


def attention_steps():
    for s in range(PAIRS + 3):
        if s < PAIRS:
            yield ("score", s)
        if 2 <= s < PAIRS + 2:
            yield ("turn", 2 * (s - 2))
            yield ("turn", 2 * (s - 2) + 1)
        if s >= 3:
            yield ("out", 2 * (s - 3))
            yield ("out", 2 * (s - 3) + 1)


GROUP_JOBS = (
    [("patch", i) for i in range(2 * PK)]
    + [("embed", i) for i in range(2 * DM)]
    + [("token", t) for t in range(NT)]
    + [("a1", t) for t in range(NT)]
    + [("qk", t) for t in range(NT)]
    + [("v", i) for i in range(PAIRS // 2)]
    + [("qkT", t) for t in range(NT)]
    + list(attention_steps())
    + [("wo", t) for t in range(NT)]
    + [("a2", t) for t in range(NT)]
    + [(k, n * len(GLU) + f) for n in range(2) for f in range(len(GLU)) for k in ("glu", "up")]
    + [("w2", t) for t in range(NT)]
    + [("y", t) for t in range(NT)]
    + [("gate", i) for i in range(2 * FT)]
    + [("logit", t) for t in range(NT)]
    + [("pos", 0)]
)
EXPERT_JOBS = [("xT", 0)] + [j for b in range(TURN) for j in [("mid", b)] + [("xT", b + 1)] * (b + 1 < TURN) + [("down", b)]]
SETUP_JOBS = [("wt", i) for i in range(PK)] + [("small", 0), ("posT", 0)]


class Banks:

    def __init__(self):
        self.uses = [0] * 8
        self.jobs = {}
        self.turn = 0
        self.scores = 0
        self.section("setup", SETUP_JOBS, 1)
        self.section("group", GROUP_JOBS, GROUPS)
        self.section("count", [("all", 0)], 1)
        self.section("expert", EXPERT_JOBS, 0)

    def section(self, name, jobs, times):
        base, count = list(self.uses), [0] * 8
        placed = {}
        for job in jobs:
            if job[0] in ("score", "small", "posT"):
                bank = SCORE[self.scores % 2]
                self.scores += 1
            else:
                bank = DENSE[self.turn % len(DENSE)]
                self.turn += 1
            placed[job] = (bank, count[bank])
            count[bank] += 1
        for job, (bank, before) in placed.items():
            self.jobs[(name,) + job] = (bank, base[bank] + before, count[bank])
        self.uses = [u + times * c for u, c in zip(base, count)]

    def bank(self, name, *job):
        return self.jobs[(name,) + job][0]

    def vacant(self, name, *job, g=0):
        bank, before, per = self.jobs[(name,) + job]
        return g * per + before

    def filled(self, name, *job, g=0):
        return self.vacant(name, *job, g=g) + 1

    emptied = filled


def build(nc, x, tok_W, tok_b, cls_token, pos_enc, wq, wk, wv, wo, w1, w2, w3, ln1_g, ln1_b, ln2_g, ln2_b,
          gate_wi, gate_bi, gate_wo, gate_bo, exp_wi, exp_bi, exp_wo, exp_bo, const, out):
    banks = Banks()
    ctx = ExitStack()
    with ctx:
        def sb(name, shape, dt=F32):
            return ctx.enter_context(nc.sbuf_tensor(name, shape, dt))

        def sem(name):
            return ctx.enter_context(nc.semaphore(name))

        rows = nc.dram_tensor("token_rows", [TOKENS + SLOTS, ROW], F32, kind="Internal").ap()
        lists = nc.dram_tensor("expert_lists", [EXPERTS * TOKENS, 1], U32, kind="Internal").ap()

        con = sb("con", [P, C_ALL])
        ident = con[:, C_ID:C_ID + P]
        tri = con[:, C_TRI:C_TRI + P]
        ident_bf = sb("ident_bf", [P, P], BF16)
        mask_bf = sb("mask_bf", [P, 8 * SEQ], BF16)
        ones = sb("ones", [P, P])
        small_rows = sb("small_rows", [P, P])
        small = sb("small", [P, P])
        WT = sb("WT", [P, PK, D])
        posT = sb("posT", [P, DM, SEQ])
        wqk_s = sb("wqk_s", [P, DM, 2 * D])
        wv_s = sb("wv_s", [P, DM, D])
        wo_s = sb("wo_s", [P, DM, D])
        w1_s = sb("w1_s", [P, DM, HIDDEN])
        w3_s = sb("w3_s", [P, DM, HIDDEN])
        w2_s = sb("w2_s", [P, len(GLU), D])
        gwi_s = sb("gwi_s", [P, DM, FF])
        gwo_s = sb("gwo_s", [P, FT, D])
        gbo_s = sb("gbo_s", [P, D])
        S_TB, S_CLS, S_G1, S_B1, S_G2, S_B2 = 0, 2, 4, 6, 8, 10
        S_GB = 12
        S_EB = S_GB + FT
        S_ROWS = S_EB + EXPERTS * FT
        gate_exp_bias = sb("gate_exp_bias", [P, FT])
        gate_lin_bias = sb("gate_lin_bias", [P, FT])

        XC = PATCH * SIDE
        arena = sb("arena", [P, 2 * XC + PK * GT])
        xin = arena[:, 0:2 * XC].rearrange("p (c n) -> p c n", c=2)
        xp = sb("xp", [P, 2, GRID, P])
        patch_area = arena[:, 2 * XC:2 * XC + PK * GT]
        patT = patch_area.rearrange("p (k n) -> p k n", k=PK)
        V = patch_area[:, 0:PAIRS * D].rearrange("p (i n) -> p i n", i=PAIRS)
        kx = patch_area[:, PAIRS * D:PAIRS * D + 2 * DM * 4 * 2 * SEQ].rearrange("p (b m h n) -> p b m h n", b=2, m=DM, h=4)
        h0T = sb("h0T", [P, DM, GT])
        h0 = sb("h0", [P, NT, D])
        u = sb("u", [P, NT, D])
        z = sb("z", [P, NT, D])
        stats = sb("stats", [P, NT, 6])
        mv = sb("mv", [P, NT, 2])
        rstd = sb("rstd", [P, NT])
        var_eps = sb("var_eps", [P, NT])
        minus_half = sb("minus_half", [P, NT])
        a1T = sb("a1T", [P, DM, GT])
        qk = sb("qk", [P, NT, 2 * D])
        swapped = sb("swapped", [P, 2, 2 * D])
        qT = sb("qT", [P, DM, GT + PITCH - SEQ])
        kT = sb("kT", [P, DM, GT])
        top = sb("top", [P, 2, 16])
        total = sb("total", [P, 2, 16])
        share = sb("share", [P, 2, 16])
        shifted = sb("shifted", [P, 2, 16 * SEQ])
        probs = sb("probs", [P, 3, 16, PITCH])
        probsT = sb("probsT", [P, 2, 2, 4 * P])
        a1P = probsT[:].rearrange("p b r n -> p (b r n)").rearrange("p (m n) -> p m n", m=DM)
        even = sb("even", [P, 2, DM, 2 * SEQ])
        attnT = sb("attnT", [P, DM, GT])
        h1 = u
        res = h0
        a2T = a1T
        th = sb("th", [P, 4, HALF])
        hidT = sb("hidT", [P, FT, GT])
        gT = hidT[:, 0:len(GLU), :]
        H2 = sb("H2", [P, NT, D])
        y = sb("y", [P, NT, ROW])
        yT = h0T
        qk_area = qk[:].rearrange("p t n -> p (t n)")
        ex, lin = (qk_area[:, i * 3 * HALF:(i + 1) * 3 * HALF].rearrange("p (b n) -> p b n", b=3) for i in range(2))
        logits = sb("logits", [P, 2, D])
        v8 = sb("v8", [P, NT, 8])
        i8 = sb("i8", [P, NT, 8], U32)
        idxf = sb("idxf", [P, 2, NT])
        vsum = sb("vsum", [P, NT, 1])
        vinv = sb("vinv", [P, NT, 1])
        wts = sb("wts", [P, NT, 2])
        pick = sb("pick", [P, 2, NT, EXPERTS])
        sel = sb("sel", [P, NT, EXPERTS])
        selcum = sb("selcum", [P, EXPERTS])
        selsum = sb("selsum", [P, EXPERTS])
        part = sb("part", [P, 2, NT, EXPERTS])
        place = sb("place", [P, 2, NT])
        dest = sb("dest", [P, 2, NT], U32)
        tokf = sb("tokf", [P, NT])
        tok = sb("tok", [P, NT], U32)
        hid_area = hidT[:].rearrange("p f n -> p (f n)")
        EW = DM * FF
        ewi = [a[:, 0:EW].rearrange("p (k n) -> p k n", k=DM) for a in (arena, hid_area)]
        ewo = [a[:, EW:2 * EW].rearrange("p (f n) -> p f n", f=FT) for a in (arena, hid_area)]
        most = sb("most", [P, 1])
        flag_u = sb("flag_u", [P, 1], U32)
        slot_tok = sb("slot_tok", [SLOTS, TURN], U32)
        pad_row = sb("pad_row", [P, SLOTS], U32)
        zero_rows = sb("zero_rows", [SLOTS, ROW])
        ebo = sb("ebo", [1, 2, D])
        xg = probs[:].rearrange("p a h n -> p (a h n)")[0:SLOTS, 0:TURN * ROW].rearrange("p (b n) -> p b n", b=TURN)
        xT = swapped[:].rearrange("p a n -> p (a n)")[:, 0:2 * DM * SLOTS].rearrange("p (b m n) -> p b m n", b=2, m=DM)
        ye = swapped[:].rearrange("p a n -> p (a n)")[0:SLOTS, 2 * DM * SLOTS:2 * DM * SLOTS + 2 * D].rearrange("p (b n) -> p b n", b=2)
        pre, ee, el = (qk[:, i, :].rearrange("p (f n) -> p f n", f=FT) for i in range(3))
        ehT = qk[:, 3:5, :].rearrange("p b (f n) -> p b f n", f=FT)
        ps = ctx.enter_context(nc.psum_tensor("ps", [P, 8, 512], F32))

        full = [sem(f"bank_filled{b}") for b in range(8)]
        free = [sem(f"bank_emptied{b}") for b in range(8)]
        waits_passed = sem("waits_passed")
        con_in = sem("con_in")
        weight_in = sem("weight_in")
        tokw_in = sem("tokw_in")
        small_in = sem("small_in")
        x_in = [sem(f"x_in{c}") for c in range(CH)]
        const_ready = sem("const_ready")
        setup_done = sem("setup_done")
        a_step = sem("vector_step_a")
        xp_ready = sem("xp_ready")
        var_ready = sem("var_ready")
        pool_step = sem("pool_step")
        rstd_ready = sem("rstd_ready")
        a1P_ready = sem("a1P_ready")
        z1_ready = sem("z1_ready")
        z2_ready = sem("z2_ready")
        y_ready = sem("y_ready")
        qk_ready = sem("qk_ready")
        kx_ready = sem("kx_ready")
        exp_ready = sem("exp_ready")
        share_ready = sem("share_ready")
        probs_ready = sem("probs_ready")
        even_ready = sem("even_ready")
        res_ready = sem("res_ready")
        th_ready = sem("th_ready")
        hid_ready = sem("hid_ready")
        sel_ready = sem("sel_ready")
        dest_ready = sem("dest_ready")
        h2_out = sem("h2_stored")
        row_out = sem("row_stored")
        list_out = sem("list_stored")
        flag_ready = sem("flag_ready")
        slots_in = [sem(f"slots_in{b}") for b in range(TURN)]
        gathered = [sem(f"rows_gathered{b}") for b in range(TURN)]
        ew_in = [sem(f"expert_weights_in{b}") for b in range(2)]
        pre_ready = sem("expert_pre_ready")
        act_ready = sem("expert_act_ready")
        added = [sem(f"expert_rows_added{b}") for b in range(TURN)]

        def bank(*job):
            return ps[:, banks.bank(*job), :]

        def full_of(eng, *job, g=0):
            eng.wait_ge(full[banks.bank(*job)], banks.filled(*job, g=g))

        def read_of(eng, *job, g=0):
            eng.wait_ge(free[banks.bank(*job)], banks.emptied(*job, g=g))

        def vacant_for(eng, *job, g=0):
            eng.wait_ge(free[banks.bank(*job)], banks.vacant(*job, g=g))

        def alone(eng):
            eng.sem_inc(waits_passed, 1)

        def filled(ins, *job):
            ins.then_inc(full[banks.bank(*job)], 1)

        def emptied(ins, *job):
            ins.then_inc(free[banks.bank(*job)], 1)

        def expert_passes(eng, body):
            with eng.Fori(0, EXPERTS // TURN) as i:
                body(0, i, i)
            eng.wait_ge(flag_ready, 1)
            more = eng.value_load(flag_u[0:1, 0:1], min_val=0, max_val=1)
            with eng.If(more > 0):
                with eng.Fori(1, CHUNKS) as c:
                    with eng.Fori(0, EXPERTS // TURN) as i:
                        body(c, i, c * (EXPERTS // TURN) + i)

        G = "group"
        x_rows = x.rearrange("b c (n r) w -> c b n (r w)", r=PATCH)
        out_rows = out

        block = ctx.enter_context(nc.Block())

        @block.sync
        def _(sp):
            sp.dma_start(con[:], const).then_inc(con_in, 16)
            sp.sem_inc(h2_out, PRIMED)
            wnat = patT.rearrange("p k n -> p (k n)")[:, 0:DM * PK * P].rearrange("p (m f) -> p m f", m=DM)
            sp.dma_start(wnat, tok_W.rearrange("(m p) f -> p m f", p=P)).then_inc(tokw_in, 16)
            for c in range(2):
                sp.dma_start(xin[0:GI * GRID, c, :], x_rows[c, 0:GI]).then_inc(x_in[c], 16)
            pos_nat = h0[0:SEQ, 0, :]
            sp.dma_start(pos_nat, pos_enc[0]).then_inc(small_in, 16)
            for at, v in ((S_TB, tok_b), (S_G1, ln1_g), (S_B1, ln1_b), (S_G2, ln2_g), (S_B2, ln2_b), (S_GB, gate_bi)):
                n = v.shape[0] // P
                sp.dma_start(small_rows[at:at + n, :], v.rearrange("(n p) -> n p", p=P)).then_inc(small_in, 16)
            sp.dma_start(small_rows[S_CLS:S_CLS + DM, :], cls_token[0, 0, :].rearrange("(n p) -> n p", p=P)).then_inc(small_in, 16)
            sp.dma_start(small_rows[S_EB:S_EB + EXPERTS * FT, :], exp_bi.rearrange("e (n p) -> (e n) p", p=P)).then_inc(small_in, 16)
            sp.dma_start(wqk_s[:, :, 0:D], wq.rearrange("(k p) n -> p k n", p=P)).then_inc(weight_in, 16)
            sp.dma_start(wqk_s[:, :, D:2 * D], wk.rearrange("(k p) n -> p k n", p=P)).then_inc(weight_in, 16)
            sp.dma_start(wv_s[:], wv.rearrange("(k p) n -> p k n", p=P)).then_inc(weight_in, 16)
            sp.dma_start(wo_s[:], wo.rearrange("(k p) n -> p k n", p=P)).then_inc(weight_in, 16)
            sp.dma_start(w1_s[:], w1.rearrange("(k p) n -> p k n", p=P)).then_inc(weight_in, 16)
            sp.dma_start(w3_s[:], w3.rearrange("(k p) n -> p k n", p=P)).then_inc(weight_in, 16)
            whole = HIDDEN // P
            sp.dma_start(w2_s[:, 0:whole, :], w2[0:whole * P].rearrange("(k p) n -> p k n", p=P)).then_inc(weight_in, 16)
            sp.dma_start(w2_s[0:GLU[-1], whole, :], w2[whole * P:HIDDEN]).then_inc(weight_in, 16)
            sp.dma_start(gwi_s[:], gate_wi.rearrange("(k p) n -> p k n", p=P)).then_inc(weight_in, 16)
            sp.dma_start(gwo_s[:], gate_wo.rearrange("(k p) n -> p k n", p=P)).then_inc(weight_in, 16)
            sp.dma_start(gbo_s[:], gate_bo.rearrange("(a n) -> a n", a=1).to_broadcast([P, D])).then_inc(weight_in, 16)
            with sp.Fori(0, GROUPS - 1) as g:
                sp.wait_ge(xp_ready, g * CH + 1)
                alone(sp)
                sp.dma_start(xin[0:GI * GRID, 0, :], x_rows[2, bass.ds(g * GI, GI)]).then_inc(x_in[2], 16)
                sp.wait_ge(xp_ready, g * CH + 2)
                alone(sp)
                sp.dma_start(xin[0:GI * GRID, 1, :], x_rows[1, bass.ds((g + 1) * GI, GI)]).then_inc(x_in[1], 16)
                sp.wait_ge(xp_ready, g * CH + 3)
                alone(sp)
                sp.dma_start(xin[0:GI * GRID, 0, :], x_rows[0, bass.ds((g + 1) * GI, GI)]).then_inc(x_in[0], 16)
            sp.wait_ge(xp_ready, (GROUPS - 1) * CH + 1)
            sp.dma_start(xin[0:GI * GRID, 0, :], x_rows[2, (GROUPS - 1) * GI:GROUPS * GI]).then_inc(x_in[2], 16)
            E = "expert"

            def load_expert(b, i):
                e = i * TURN + b
                sp.dma_start(ewi[b % 2], exp_wi[bass.ds(e, 1)].rearrange("a (k p) n -> p (a k) n", p=P)).then_inc(ew_in[b % 2], 16)
                sp.dma_start(ewo[b % 2], exp_wo[bass.ds(e, 1)].rearrange("a (f p) n -> p (a f) n", p=P)).then_inc(ew_in[b % 2], 16)
                sp.dma_start(ebo[:, b % 2, :], exp_bo[bass.ds(e, 1)]).then_inc(ew_in[b % 2], 16)

            def body(c, i, before):
                for b in range(TURN):
                    if b < 2:
                        full_of(sp, E, "down", b + 2, g=before - 1)
                    else:
                        full_of(sp, E, "down", b - 2, g=before)
                    alone(sp)
                    if b == 1:
                        full_of(sp, G, "logit", NT - 1, g=GROUPS - 1)
                    load_expert(b, i)
                    if b == 1:
                        sp.wait_ge(list_out, PRIMED + 16 * 2 * NT * GROUPS)
                        for s in range(TURN):
                            at = sp.snap((i * TURN + s) * TOKENS + c * SLOTS)
                            sp.wait_ge(added[s], PRIMED + 16 * before)
                            alone(sp)
                            sp.dma_start(slot_tok[:, s:s + 1], lists[bass.ds(at, SLOTS), :]).then_inc(slots_in[s], 16)
            full_of(sp, G, "out", 2 * PAIRS - 1, g=GROUPS - 1)
            expert_passes(sp, body)
            sp.wait_ge(h2_out, PRIMED + 16 * NT * GROUPS)
            sp.wait_ge(row_out, PRIMED + 16 * NT * GROUPS)

        @block.tensor
        def _(pe):
            def turn_tiles(job, src, g):
                for t, (a, n) in enumerate(TILES):
                    vacant_for(pe, G, job, t, g=g)
                    ready = {"a1": z1_ready, "a2": z2_ready, "y": y_ready}[job]
                    pe.wait_ge(ready, g * NT + t + 1)
                    for m in range(DM):
                        mm = pe.transpose(bank(G, job, t)[:, m * P:m * P + n], src[0:n, t, m * P:(m + 1) * P], ident[0:n, 0:n])
                    filled(mm, G, job, t)

            pe.wait_ge(con_in, 16)
            pe.wait_ge(tokw_in, 16)
            wnat = patT.rearrange("p k n -> p (k n)")[:, 0:DM * PK * P].rearrange("p (m f) -> p m f", m=DM)
            for k in range(PK):
                vacant_for(pe, "setup", "wt", k)
                for m in range(DM):
                    mm = pe.transpose(bank("setup", "wt", k)[:, m * P:(m + 1) * P], wnat[:, m, k * P:(k + 1) * P], ident)
                filled(mm, "setup", "wt", k)
            pe.wait_ge(small_in, 16 * 9)
            vacant_for(pe, "setup", "small", 0)
            filled(pe.transpose(bank("setup", "small", 0)[:, 0:S_ROWS], small_rows[0:S_ROWS, :], ident[0:S_ROWS, 0:S_ROWS]), "setup", "small", 0)
            vacant_for(pe, "setup", "posT", 0)
            for m in range(DM):
                mm = pe.transpose(bank("setup", "posT", 0)[:, m * SEQ:(m + 1) * SEQ], h0[0:SEQ, 0, m * P:(m + 1) * P], ident[0:SEQ, 0:SEQ])
            filled(mm, "setup", "posT", 0)
            pe.wait_ge(setup_done, 2)

            with pe.Fori(0, GROUPS) as g:
                for i in range(2 * PK):
                    k, side = i // 2, i % 2
                    c, upper = k // 2, k % 2
                    if i % 4 == 0:
                        pe.wait_ge(xp_ready, g * CH + c + 1)
                    vacant_for(pe, G, "patch", i, g=g)
                    for j in range(3):
                        mm = pe.transpose(bank(G, "patch", i)[:, j * GI * GRID:(j + 1) * GI * GRID], xp[0:GI * GRID, upper, 3 * side + j, :],
                                          ident[0:GI * GRID, 0:GI * GRID])
                    filled(mm, G, "patch", i)
                for i in range(2 * DM):
                    n, m = i // DM, i % DM
                    vacant_for(pe, G, "embed", i, g=g)
                    if i == 0:
                        for j in range(2 * PK - 4, 2 * PK):
                            read_of(pe, G, "patch", j, g=g)
                    for k in range(PK):
                        mm = pe.matmul(bank(G, "embed", i)[:, 0:HALF], WT[:, k, m * P:(m + 1) * P], patT[:, k, n * HALF:(n + 1) * HALF],
                                       start=(k == 0), stop=(k == PK - 1))
                    filled(mm, G, "embed", i)
                for t, (a, n) in enumerate(TILES):
                    vacant_for(pe, G, "token", t, g=g)
                    for i in range(2 * DM if t >= 2 else DM):
                        if t in (0, 2):
                            read_of(pe, G, "embed", i, g=g)
                    for m in range(DM):
                        mm = pe.transpose(bank(G, "token", t)[0:n, m * P:(m + 1) * P], h0T[:, m, a:a + n], ident)
                    filled(mm, G, "token", t)
                turn_tiles("a1", z, g)
                pe.wait_ge(weight_in, 16 * 11)
                for t, (a, n) in enumerate(TILES):
                    vacant_for(pe, G, "qk", t, g=g)
                    read_of(pe, G, "a1", t, g=g)
                    for k in range(DM):
                        mm = pe.matmul(bank(G, "qk", t)[0:n, :], a1T[:, k, a:a + n], wqk_s[:, k, :], start=(k == 0), stop=(k == DM - 1))
                    filled(mm, G, "qk", t)
                for i in range(PAIRS // 2):
                    vacant_for(pe, G, "v", i, g=g)
                    pe.wait_ge(a1P_ready, g + 1)
                    for j in range(2):
                        a = (2 * i + j) * P
                        for k in range(DM):
                            mm = pe.matmul(bank(G, "v", i)[:, j * D:(j + 1) * D], a1P[:, k, a:a + P], wv_s[:, k, :],
                                           start=(k == 0), stop=(k == DM - 1))
                    filled(mm, G, "v", i)
                for t, (a, n) in enumerate(TILES):
                    vacant_for(pe, G, "qkT", t, g=g)
                    pe.wait_ge(qk_ready, g * NT + t + 1)
                    for m in range(2 * DM):
                        mm = pe.transpose(bank(G, "qkT", t)[:, m * P:m * P + n], qk[0:n, t, m * P:(m + 1) * P], ident[0:n, 0:n])
                    filled(mm, G, "qkT", t)
                for kind, i in attention_steps():
                    vacant_for(pe, G, kind, i, g=g)
                    if kind == "score":
                        pe.wait_ge(kx_ready, g * PAIRS + i + 1)
                        for r in range(2):
                            b = ps[:, banks.bank(G, "score", i) + r, 0:8 * SEQ]
                            pe.matmul(b, ident_bf[:], mask_bf[:], start=True, stop=False, skip_group_check=True)
                            for m in range(DM):
                                for j in range(2):
                                    a = (2 * i + j) * SEQ
                                    mm = pe.matmul(b.rearrange("p (h n) -> p h n", h=4)[PITCH * m:PITCH * (m + 1), :, j * SEQ:(j + 1) * SEQ],
                                                   qT[64 * r:64 * r + 64, m, a:a + PITCH], kx[64 * r:64 * r + 64, i % 2, m, :, j * SEQ:(j + 1) * SEQ],
                                                   start=False, stop=True, skip_group_check=True)
                    elif kind == "turn":
                        p, r = i // 2, i % 2
                        pe.wait_ge(probs_ready, g * PAIRS + p + 1)
                        for j in range(4):
                            src = probs[:, p % 3, (4 * r + j) * 2:(4 * r + j) * 2 + 2, :].rearrange("p a n -> p (a n)")
                            mm = pe.transpose(bank(G, kind, i)[:, j * P:(j + 1) * P], src, ident)
                    else:
                        pair, j = i // 2, i % 2
                        if j == 0:
                            for r in range(2):
                                read_of(pe, G, "turn", 2 * pair + r, g=g)
                        if i == 0:
                            for v in range(PAIRS // 2):
                                read_of(pe, G, "v", v, g=g)
                        alone(pe)
                        b = bank(G, kind, i)[:, 0:2 * 2 * SEQ].rearrange("p (m e c) -> p m e c", m=DM, e=2)
                        for m in range(DM):
                            for q in range(4):
                                r, s = q // 2, q % 2
                                pT = probsT[64 * j:64 * j + SEQ, pair % 2, r, :].rearrange("p (h n) -> p h n", h=4)
                                mm = pe.matmul(b[32 * q:32 * q + 32, m, :, :],
                                               V[64 * j:64 * j + SEQ, pair, m * P + 32 * q:m * P + 32 * q + 32],
                                               pT[:, 2 * s:2 * s + 2, PITCH * m:PITCH * m + SEQ], start=True, stop=True,
                                               skip_group_check=True)
                    filled(mm, G, kind, i)
                for t, (a, n) in enumerate(TILES):
                    vacant_for(pe, G, "wo", t, g=g)
                    if t == 0:
                        for i in (2 * PAIRS - 2, 2 * PAIRS - 1):
                            read_of(pe, G, "out", i, g=g)
                    for k in range(DM):
                        mm = pe.matmul(bank(G, "wo", t)[0:n, 0:D], attnT[:, k, a:a + n], wo_s[:, k, :], start=(k == 0), stop=(k == DM - 1))
                    filled(mm, G, "wo", t)
                turn_tiles("a2", z, g)
                for i in range(2 * len(GLU)):
                    n, f = i // len(GLU), i % len(GLU)
                    for kind, w in (("glu", w1_s), ("up", w3_s)):
                        vacant_for(pe, G, kind, i, g=g)
                        if kind == "glu" and f == 0:
                            for t in (range(3), range(3, NT))[n]:
                                read_of(pe, G, "a2", t, g=g)
                        for k in range(DM):
                            mm = pe.matmul(bank(G, kind, i)[0:GLU[f], 0:HALF], w[:, k, f * P:f * P + GLU[f]], a2T[:, k, n * HALF:(n + 1) * HALF],
                                           start=(k == 0), stop=(k == DM - 1))
                        filled(mm, G, kind, i)
                for t, (a, n) in enumerate(TILES):
                    vacant_for(pe, G, "w2", t, g=g)
                    if t in (0, 2):
                        hi = len(GLU) if t == 0 else 2 * len(GLU)
                        for j in range(hi - len(GLU), hi):
                            read_of(pe, G, "up", j, g=g)
                    for f, h in enumerate(GLU):
                        mm = pe.matmul(bank(G, "w2", t)[0:n, 0:D], gT[0:h, f, a:a + n], w2_s[0:h, f, :], start=(f == 0), stop=(f == len(GLU) - 1))
                    filled(mm, G, "w2", t)
                turn_tiles("y", y, g)
                for i in range(2 * FT):
                    n, f = i // FT, i % FT
                    vacant_for(pe, G, "gate", i, g=g)
                    if f == 0:
                        for t in (range(3), range(3, NT))[n]:
                            read_of(pe, G, "y", t, g=g)
                    for k in range(DM):
                        mm = pe.matmul(bank(G, "gate", i)[:, 0:HALF], gwi_s[:, k, f * P:(f + 1) * P], yT[:, k, n * HALF:(n + 1) * HALF],
                                       start=(k == 0), stop=(k == DM - 1))
                    filled(mm, G, "gate", i)
                for t, (a, n) in enumerate(TILES):
                    vacant_for(pe, G, "logit", t, g=g)
                    if t in (0, 2):
                        pe.wait_ge(hid_ready, g * 2 * FT + (FT if t == 0 else 2 * FT))
                    for f in range(FT):
                        mm = pe.matmul(bank(G, "logit", t)[0:n, 0:D], hidT[:, f, a:a + n], gwo_s[:, f, :], start=(f == 0), stop=(f == FT - 1))
                    filled(mm, G, "logit", t)
                vacant_for(pe, G, "pos", 0, g=g)
                pe.wait_ge(sel_ready, g + 1)
                before = bank(G, "pos", 0)[:, 0:NT * EXPERTS].rearrange("p (t e) -> p t e", e=EXPERTS)
                pe.matmul(before, tri, sel[:], start=True, stop=False, skip_group_check=True)
                for back in range(1, NT):
                    pe.matmul(before[:, back:NT, :], ones[:], sel[:, 0:NT - back, :], start=False, stop=False, skip_group_check=True)
                filled(pe.matmul(before, ones[:], selcum[:].rearrange("p (a e) -> p a e", a=1).to_broadcast([P, NT, EXPERTS]),
                                 start=False, stop=True, skip_group_check=True), G, "pos", 0)

            vacant_for(pe, "count", "all", 0)
            pe.wait_ge(dest_ready, GROUPS)
            filled(pe.matmul(bank("count", "all", 0)[:, 0:EXPERTS], ones[:], selcum[:], start=True, stop=True), "count", "all", 0)

            def body(c, i, before):
                E = "expert"

                def turn_rows(b):
                    pe.wait_ge(gathered[b], 16 * (before + 1))
                    vacant_for(pe, E, "xT", b, g=before)
                    alone(pe)
                    for m in range(DM):
                        mm = pe.transpose(bank(E, "xT", b)[:, m * SLOTS:(m + 1) * SLOTS], xg[:, b, m * P:(m + 1) * P], ident[0:SLOTS, 0:SLOTS])
                    filled(mm, E, "xT", b)

                turn_rows(0)
                for b in range(TURN):
                    pe.wait_ge(ew_in[b % 2], 48 * (before * (TURN // 2) + b // 2 + 1))
                    read_of(pe, E, "xT", b, g=before)
                    vacant_for(pe, E, "mid", b, g=before)
                    for f in range(FT):
                        for k in range(DM):
                            mm = pe.matmul(bank(E, "mid", b)[:, f * SLOTS:(f + 1) * SLOTS], ewi[b % 2][:, k, f * P:(f + 1) * P], xT[:, b % 2, k, :],
                                           start=(k == 0), stop=(k == DM - 1))
                    filled(mm, E, "mid", b)
                    if b + 1 < TURN:
                        turn_rows(b + 1)
                    vacant_for(pe, E, "down", b, g=before)
                    pe.wait_ge(act_ready, before * TURN + b + 1)
                    down = bank(E, "down", b)[0:SLOTS, 0:D]
                    pe.matmul(down, ones[0:1, 0:SLOTS], ebo[:, b % 2, :], start=True, stop=False)
                    for f in range(FT):
                        mm = pe.matmul(down, ehT[:, b % 2, f, :], ewo[b % 2][:, f, :], start=False, stop=(f == FT - 1))
                    filled(mm, E, "down", b)
            expert_passes(pe, body)

        @block.scalar
        def _(act):
            def turned(job, dst, g, scale=None, bias=None):
                for t, (a, n) in enumerate(TILES):
                    full_of(act, G, job, t, g=g)
                    if scale is None:
                        last = act.activation(dst[:, :, a:a + n], bank(G, job, t)[:, 0:DM * P].rearrange("p (m n) -> p m n", m=DM)[:, :, 0:n], ACT.Copy)
                    else:
                        for m in range(DM):
                            last = act.activation(dst[:, m, a:a + n], bank(G, job, t)[:, m * P:m * P + n], ACT.Identity,
                                                  scale=small[:, scale + m:scale + m + 1], bias=small[:, bias + m:bias + m + 1])
                    emptied(last, G, job, t)

            for k in range(PK):
                full_of(act, "setup", "wt", k)
                emptied(act.activation(WT[:, k, :], bank("setup", "wt", k)[:, 0:D], ACT.Copy), "setup", "wt", k)

            with act.Fori(0, GROUPS) as g:
                act.wait_ge(setup_done, 2)
                for i in range(2 * PK):
                    k, side = i // 2, i % 2
                    full_of(act, G, "patch", i, g=g)
                    dst = patT[:, k, :].rearrange("p (b s) -> p b s", s=SEQ)[:, :, 1:SEQ].rearrange("p b (n w) -> p b n w", w=GRID)
                    src = bank(G, "patch", i)[:, 0:3 * GI * GRID].rearrange("p (w b n) -> p w b n", w=3, b=GI)
                    for j in range(3):
                        last = act.activation(dst[:, :, :, 3 * side + j], src[:, j, :, :], ACT.Copy)
                    emptied(last, G, "patch", i)
                for t, (a, n) in enumerate(TILES):
                    full_of(act, G, "token", t, g=g)
                    emptied(act.activation(h0[0:n, t, :], bank(G, "token", t)[0:n, 0:D], ACT.Copy), G, "token", t)
                turned("a1", a1T, g, S_G1, S_B1)
                for i in range(PAIRS // 2):
                    full_of(act, G, "v", i, g=g)
                    emptied(act.activation(V[:, 2 * i:2 * i + 2, :].rearrange("p a n -> p (a n)"), bank(G, "v", i), ACT.Copy), G, "v", i)
                for t, (a, n) in enumerate(TILES):
                    full_of(act, G, "qkT", t, g=g)
                    src = bank(G, "qkT", t).rearrange("p (m n) -> p m n", m=2 * DM)
                    act.activation(qT[:, :, a:a + n], src[:, 0:DM, 0:n], ACT.Copy, scale=float(HD) ** -0.5)
                    emptied(act.activation(kT[:, :, a:a + n], src[:, DM:2 * DM, 0:n], ACT.Copy), G, "qkT", t)
                for s in range(PAIRS + 3):
                    if s < PAIRS:
                        read_of(act, G, "score", s, g=g)
                        if s >= 3:
                            full_of(act, G, "turn", 2 * (s - 3) + 1, g=g)
                        act.activation(probs[:, s % 3, :, 0:SEQ], shifted[:, s % 2, :].rearrange("p (h n) -> p h n", n=SEQ),
                                       ACT.Exp).then_inc(exp_ready, 1)
                    if 2 <= s < PAIRS + 2:
                        for r in range(2):
                            i = 2 * (s - 2) + r
                            full_of(act, G, "turn", i, g=g)
                            emptied(act.activation(probsT[:, (s - 2) % 2, r, :], bank(G, "turn", i), ACT.Copy), G, "turn", i)
                    if s >= 3:
                        i = s - 3
                        full_of(act, G, "out", 2 * i + 1, g=g)
                        if i >= 2:
                            read_of(act, G, "out", 2 * (i - 2) + 1, g=g)
                        b = banks.bank(G, "out", 2 * i)
                        assert banks.bank(G, "out", 2 * i + 1) == b + 1
                        src = ps[:, b:b + 2, 0:2 * 2 * SEQ].rearrange("p j (m e c) -> p m j e c", m=DM, e=2)
                        act.activation(even[:, i % 2, :, :].rearrange("p m (j c) -> p m j c", j=2), src[:, :, :, 0, :], ACT.Copy, scale=con[:, C_PAR:C_PAR + 1]).then_inc(even_ready, 1)
                turned("a2", a2T, g, S_G2, S_B2)
                for i in range(2 * len(GLU)):
                    f = i % len(GLU)
                    full_of(act, G, "glu", i, g=g)
                    if i >= 4:
                        read_of(act, G, "up", i - 4, g=g)
                    act.activation(th[0:GLU[f], i % 4, :], bank(G, "glu", i)[0:GLU[f], 0:HALF], ACT.Tanh, scale=0.5).then_inc(th_ready, 1)
                turned("y", yT, g)
                for t, (a, n) in enumerate(TILES):
                    act.dma_start(out_rows[bass.ds(g * GT + a, n), :], H2[0:n, t, :]).then_inc(h2_out, 16)
                for i in range(2 * FT):
                    f = i % FT
                    full_of(act, G, "gate", i, g=g)
                    if i >= 3:
                        act.wait_ge(hid_ready, g * 2 * FT + i - 2)
                    act.activation(ex[:, i % 3, :], bank(G, "gate", i)[:, 0:HALF], ACT.Exp, bias=gate_exp_bias[:, f:f + 1])
                    act.activation(lin[:, i % 3, :], bank(G, "gate", i)[:, 0:HALF], ACT.Relu, scale=LAMBDA,
                                   bias=gate_lin_bias[:, f:f + 1]).then_inc(free[banks.bank(G, "gate", i)], 1)

            def body(c, i, before):
                E = "expert"
                for b in range(TURN):
                    full_of(act, E, "xT", b, g=before)
                    emptied(act.activation(xT[:, b % 2, :, :].rearrange("p m n -> p (m n)"), bank(E, "xT", b)[:, 0:DM * SLOTS], ACT.Copy), E, "xT", b)
                    read_of(act, E, "mid", b, g=before)
                    act.activation(ee, pre, ACT.Exp, bias=con[:, C_LNLA:C_LNLA + 1])
                    act.activation(el, pre, ACT.Relu, scale=LAMBDA).then_inc(pre_ready, 1)
            expert_passes(act, body)

        @block.gpsimd
        def _(pool):
            pool.memset(ones[:], 1.0).then_inc(const_ready, 1)
            pool.memset(zero_rows[:], 0.0).then_inc(const_ready, 1)
            pool.memset(probs[:], 0.0)
            pool.memset(probsT[:], 0.0)
            pool.memset(qT[:, :, GT:], 0.0)
            pool.memset(selcum[:], 0.0)
            pool.memset(minus_half[:], -0.5)
            pool.memset(v8[:], 1.0)
            pool.memset(i8[:], 0)
            pool.wait_ge(con_in, 16)
            pool.tensor_copy(ident_bf[:], ident)
            pool.tensor_copy(mask_bf[:], con[:, C_MASK:C_MASK + 8 * SEQ]).then_inc(setup_done, 1)
            pool.wait_ge(const_ready, 3)
            quarter = EXPERTS * CHUNKS // 4
            pool.dma_start(lists.rearrange("(q c s) o -> q c (s o)", s=SLOTS, c=4),
                           pad_row[0:quarter, :].rearrange("q (a s) -> q a s", a=1).to_broadcast([quarter, 4, SLOTS])).then_inc(list_out, 16)
            pool.dma_start(rows[TOKENS:TOKENS + SLOTS, :], zero_rows[:]).then_inc(row_out, 16)
            pad = SLOTS // TURN
            for b in range(TURN):
                pool.dma_start(out_rows[TOKENS + b * pad:TOKENS + (b + 1) * pad, :], zero_rows[0:pad, 0:D]).then_inc(added[b], 16)

            def inverse_deviation(which, g):
                pool.wait_ge(var_ready, g * 4 + which + 1)
                alone(pool)
                pool.tensor_scalar(var_eps[:], mv[:, :, 1], EPS, None, ALU.add).then_inc(pool_step, 1)
                pool.wait_ge(pool_step, g * 4 + which + 1)
                pool.tensor_tensor(rstd[:], var_eps[:], minus_half[:], ALU.pow).then_inc(rstd_ready, 1)

            with pool.Fori(0, GROUPS) as g:
                for c in range(CH):
                    pool.wait_ge(x_in[c], 16 * (g + 1))
                    if c:
                        full_of(pool, G, "patch", 4 * c - 1, g=g)
                    alone(pool)
                    for upper in range(2):
                        last = pool.tensor_copy(xp[0:GI * GRID, upper, :, :].rearrange("p w (r x) -> p r w x", x=PATCH),
                                                xin[0:GI * GRID, c % 2, upper * 8 * SIDE:(upper + 1) * 8 * SIDE].rearrange("p (r w x) -> p r w x", w=GRID, x=PATCH))
                    last.then_inc(xp_ready, 1)
                inverse_deviation(0, g)
                inverse_deviation(1, g)
                for t in range(NT):
                    read_of(pool, G, "a1", t, g=g)
                alone(pool)
                pool.tensor_copy(a1P.rearrange("p m (i n) -> p m i n", n=PITCH)[:, :, :, 0:SEQ],
                                 a1T[:].rearrange("p m (i n) -> p m i n", n=SEQ)).then_inc(a1P_ready, 1)
                for t, (a, n) in enumerate(TILES):
                    read_of(pool, G, "qk", t, g=g)
                    pool.tensor_tensor(qk[0:n, t, :], qk[0:n, t, :], swapped[0:n, t % 2, :], ALU.add).then_inc(qk_ready, 1)
                for s in range(PAIRS + 1):
                    if s < PAIRS:
                        last_tile = min(NT - 1, ((s + 1) * 2 * SEQ - 1) // P)
                        read_of(pool, G, "qkT", last_tile, g=g)
                        if s >= 2:
                            full_of(pool, G, "score", s - 2, g=g)
                        for m in range(DM):
                            last = pool.tensor_tensor(
                                kx[:, s % 2, m, :, :],
                                kT[:, m:m + 1, s * 2 * SEQ:(s + 1) * 2 * SEQ].to_broadcast([P, 4, 2 * SEQ]),
                                con[:, C_HEAD:C_HEAD + 4].rearrange("p (h a) -> p h a", a=1).to_broadcast([P, 4, 2 * SEQ]), ALU.mult)
                        last.then_inc(kx_ready, 1)
                    if s >= 1:
                        p = s - 1
                        pool.wait_ge(share_ready, g * PAIRS + p + 1)
                        pool.tensor_tensor(probs[:, p % 3, :, 0:SEQ], probs[:, p % 3, :, 0:SEQ],
                                           share[:, p % 2, :].rearrange("p (h a) -> p h a", a=1).to_broadcast([P, 16, SEQ]),
                                           ALU.mult).then_inc(probs_ready, 1)
                inverse_deviation(2, g)
                for t, (a, n) in enumerate(TILES):
                    read_of(pool, G, "wo", t, g=g)
                    pool.tensor_tensor(res[0:n, t, :], h0[0:n, t, :], h1[0:n, t, :], ALU.add).then_inc(res_ready, 1)
                inverse_deviation(3, g)
                pool.wait_ge(dest_ready, g + 1)
                pool.wait_ge(list_out, PRIMED)
                for t, (a, n) in enumerate(TILES):
                    pool.dma_start(rows[bass.ds(g * GT + a, n), :], y[0:n, t, :]).then_inc(row_out, 16)
                    for k in range(2):
                        pool.indirect_dma_start(out=lists, out_offset=bass.IndirectOffsetOnAxis(ap=dest[0:n, k, t:t + 1], axis=0),
                                                in_=tok[0:n, t:t + 1], in_offset=None, bounds_check=EXPERTS * TOKENS - 1,
                                                oob_is_err=False).then_inc(list_out, 16)

            pool.wait_ge(row_out, PRIMED + 16 * NT * GROUPS)
            pool.wait_ge(h2_out, PRIMED + 16 * NT * GROUPS)

            def body(c, i, before):
                E = "expert"
                for b in range(TURN):
                    pool.wait_ge(slots_in[b], 16 * (before + 1))
                    alone(pool)
                    pool.indirect_dma_start(out=xg[:, b, :], out_offset=None, in_=rows,
                                            in_offset=bass.IndirectOffsetOnAxis(ap=slot_tok[:, b:b + 1], axis=0)).then_inc(gathered[b], 16)
                for b in range(TURN):
                    read_of(pool, E, "down", b, g=before)
                    if b:
                        pool.wait_ge(added[b - 1], PRIMED + 16 * (before + 1))
                    else:
                        pool.wait_ge(added[TURN - 1], PRIMED + 16 * before)
                    alone(pool)
                    pool.indirect_dma_start(out=out_rows, out_offset=bass.IndirectOffsetOnAxis(ap=slot_tok[:, b:b + 1], axis=0),
                                            in_=ye[:, b % 2, :], in_offset=None, compute_op=ALU.add).then_inc(added[b], 16)
                for b in range(TURN):
                    pool.wait_ge(added[b], PRIMED + 16 * (before + 1))
            expert_passes(pool, body)

        @block.vector
        def _(dve):
            class Chain:
                def __init__(self, g, per):
                    self.g, self.per, self.n = g, per, 0

                def step(self, ins):
                    ins.then_inc(a_step, 1)
                    self.n += 1

                def wait(self):
                    dve.wait_ge(a_step, self.g * self.per + self.n)

            PER = 36

            def norm(which, dst, src, chain, ready, g):
                for t, (a, n) in enumerate(TILES):
                    last = dve.bn_stats(stats[0:n, t, :], src[0:n, t, :])
                chain.step(last)
                chain.wait()
                alone(dve)
                for t, (a, n) in enumerate(TILES):
                    last = dve.bn_aggr(mv[0:n, t, :], stats[0:n, t, :])
                last.then_inc(var_ready, 1)
                dve.wait_ge(rstd_ready, g * 4 + which + 1)
                for t, (a, n) in enumerate(TILES):
                    ins = dve.tensor_scalar(dst[0:n, t, 0:D], src[0:n, t, :], mv[0:n, t, 0:1], rstd[0:n, t:t + 1], ALU.subtract, ALU.mult)
                    if ready is not None:
                        ins.then_inc(ready, 1)
                if ready is None:
                    chain.step(ins)
                    chain.wait()

            dve.memset(mv[:], 1.0)
            dve.wait_ge(con_in, 16)
            dve.tensor_copy(tokf[:], con[:, C_TOK:C_TOK + NT])
            dve.tensor_copy(pad_row[:], con[:, C_PAD:C_PAD + SLOTS]).then_inc(const_ready, 1)
            full_of(dve, "setup", "small", 0)
            dve.tensor_copy(small[:, 0:S_ROWS], bank("setup", "small", 0)[:, 0:S_ROWS]).then_inc(free[banks.bank("setup", "small", 0)], 1)
            read_of(dve, "setup", "small", 0)
            dve.tensor_scalar(gate_exp_bias[:], small[:, S_GB:S_GB + FT], con[:, C_LNLA:C_LNLA + 1], None, ALU.add)
            dve.tensor_scalar(gate_lin_bias[:], small[:, S_GB:S_GB + FT], LAMBDA, None, ALU.mult)
            full_of(dve, "setup", "posT", 0)
            for m in range(DM):
                src = bank("setup", "posT", 0)[:, m * SEQ:(m + 1) * SEQ]
                dve.tensor_scalar(posT[:, m, 1:SEQ], src[:, 1:SEQ], small[:, S_TB + m:S_TB + m + 1], None, ALU.add)
                last = dve.tensor_scalar(posT[:, m, 0:1], src[:, 0:1], small[:, S_CLS + m:S_CLS + m + 1], None, ALU.add)
            emptied(last, "setup", "posT", 0)
            read_of(dve, "setup", "wt", PK - 1)
            dve.memset(patT.rearrange("p k (b s) -> p k b s", s=SEQ)[:, :, :, 0], 0.0).then_inc(setup_done, 1)

            with dve.Fori(0, GROUPS) as g:
                ch = Chain(g, PER)
                for i in range(2 * DM):
                    n, m = i // DM, i % DM
                    full_of(dve, G, "embed", i, g=g)
                    dst = h0T[:, m, n * HALF:(n + 1) * HALF].rearrange("p (b s) -> p b s", s=SEQ)
                    src = bank(G, "embed", i)[:, 0:HALF].rearrange("p (b s) -> p b s", s=SEQ)
                    dve.tensor_copy(dst[:, :, 0:1], posT[:, m:m + 1, 0:1].to_broadcast([P, GI // 2, 1]))
                    emptied(dve.tensor_tensor(dst[:, :, 1:SEQ], src[:, :, 1:SEQ],
                                              posT[:, m:m + 1, 1:SEQ].to_broadcast([P, GI // 2, SEQ - 1]), ALU.add), G, "embed", i)
                for t in range(NT):
                    read_of(dve, G, "token", t, g=g)
                norm(0, u, h0, ch, None, g)
                norm(1, z, u, ch, z1_ready, g)
                for t, (a, n) in enumerate(TILES):
                    full_of(dve, G, "qk", t, g=g)
                    if t >= 2:
                        dve.wait_ge(qk_ready, g * NT + t - 1)
                    src = bank(G, "qk", t)[0:n, :].rearrange("p (h c) -> p h c", c=HD)
                    heads = 2 * HEADS

                    def table(at):
                        return con[0:n, at + t * HD:at + (t + 1) * HD].rearrange("p (a c) -> p a c", a=1)
                    dve.tensor_tensor(qk[0:n, t, :].rearrange("p (h c) -> p h c", c=HD), src, table(C_COS).to_broadcast([n, heads, HD]), ALU.mult)
                    for e in range(2):
                        ins = dve.tensor_tensor(swapped[0:n, t % 2, :].rearrange("p (h c) -> p h c", c=HD)[:, :, e::2], src[:, :, 1 - e::2],
                                                table(C_SIN)[:, :, e::2].to_broadcast([n, heads, HD // 2]), ALU.mult)
                    emptied(ins, G, "qk", t)
                for s in range(PAIRS + 3):
                    if s < PAIRS:
                        full_of(dve, G, "score", s, g=g)
                        b = banks.bank(G, "score", s)
                        src = ps[:, b:b + 2, 0:8 * SEQ].rearrange("p r (h n) -> p r h n", n=SEQ)
                        mx = top[:, s % 2, :].rearrange("p (r h) -> p r h", r=2)
                        ch.step(dve.tensor_reduce(mx, src, AX.X, ALU.max))
                        ch.wait()
                        emptied(dve.tensor_tensor(shifted[:, s % 2, :].rearrange("p (r h n) -> p r h n", r=2, n=SEQ), src,
                                                  mx.rearrange("p r (h a) -> p r h a", a=1).to_broadcast([P, 2, 8, SEQ]), ALU.subtract),
                                G, "score", s)
                    if 1 <= s <= PAIRS:
                        p = s - 1
                        dve.wait_ge(exp_ready, g * PAIRS + p + 1)
                        ch.step(dve.tensor_reduce(total[:, p % 2, :], probs[:, p % 3, :, 0:SEQ], AX.X, ALU.add))
                        ch.wait()
                        dve.reciprocal(share[:, p % 2, :], total[:, p % 2, :]).then_inc(share_ready, 1)
                    if s >= 3:
                        i = s - 3
                        dve.wait_ge(even_ready, g * PAIRS + i + 1)
                        for j in range(2):
                            src = bank(G, "out", 2 * i + j)[:, 0:2 * 2 * SEQ].rearrange("p (m e c) -> p m e c", m=DM, e=2)
                            a = (2 * i + j) * SEQ
                            emptied(dve.scalar_tensor_tensor(attnT[:, :, a:a + SEQ], src[:, :, 1, :], con[:, C_PAR + 1:C_PAR + 2],
                                                             even[:, i % 2, :, j * SEQ:(j + 1) * SEQ], ALU.mult, ALU.add), G, "out", 2 * i + j)
                for t, (a, n) in enumerate(TILES):
                    full_of(dve, G, "wo", t, g=g)
                    emptied(dve.tensor_tensor(h1[0:n, t, :], bank(G, "wo", t)[0:n, 0:D], u[0:n, t, :], ALU.add), G, "wo", t)
                for t in range(NT):
                    read_of(dve, G, "wo", t, g=g)
                norm(2, z, h1, ch, z2_ready, g)
                for i in range(2 * len(GLU)):
                    n, f = i // len(GLU), i % len(GLU)
                    h = GLU[f]
                    dve.wait_ge(th_ready, g * 2 * len(GLU) + i + 1)
                    full_of(dve, G, "up", i, g=g)
                    emptied(dve.scalar_tensor_tensor(th[0:h, i % 4, :], th[0:h, i % 4, :], 1.0, bank(G, "glu", i)[0:h, 0:HALF], ALU.add, ALU.mult), G, "glu", i)
                    read_of(dve, G, "glu", i, g=g)
                    emptied(dve.scalar_tensor_tensor(gT[0:h, f, n * HALF:(n + 1) * HALF], th[0:h, i % 4, :], 0.5, bank(G, "up", i)[0:h, 0:HALF], ALU.mult, ALU.mult), G, "up", i)
                dve.wait_ge(h2_out, PRIMED + g * NT * 16)
                for t in range(NT):
                    dve.wait_ge(res_ready, g * NT + t + 1)
                    a, n = TILES[t]
                    full_of(dve, G, "w2", t, g=g)
                    emptied(dve.tensor_tensor(H2[0:n, t, :], bank(G, "w2", t)[0:n, 0:D], res[0:n, t, :], ALU.add), G, "w2", t)
                    read_of(dve, G, "w2", t, g=g)
                dve.wait_ge(row_out, PRIMED + g * NT * 16)
                norm(3, y, H2, ch, y_ready, g)
                for i in range(2 * FT):
                    n, f = i // FT, i % FT
                    read_of(dve, G, "gate", i, g=g)
                    dve.scalar_tensor_tensor(hidT[:, f, n * HALF:(n + 1) * HALF], ex[:, i % 3, :], LA, lin[:, i % 3, :], ALU.subtract, ALU.min).then_inc(hid_ready, 1)
                for t, (a, n) in enumerate(TILES):
                    full_of(dve, G, "logit", t, g=g)
                    emptied(dve.tensor_tensor(logits[0:n, t % 2, :], bank(G, "logit", t)[0:n, 0:D], gbo_s[0:n, :], ALU.add), G, "logit", t)
                    read_of(dve, G, "logit", t, g=g)
                    alone(dve)
                    ch.step(dve.max(v8[0:n, t, :], logits[0:n, t % 2, :]))
                    ch.wait()
                    alone(dve)
                    ins = dve.max_index(i8[0:n, t, :], v8[0:n, t, :], logits[0:n, t % 2, :])
                ch.step(ins)
                ch.wait()
                dve.tensor_copy(idxf[:].rearrange("p k t -> p t k"), i8[:, :, 0:2])
                ch.step(dve.tensor_tensor(vsum[:], v8[:, :, 0:1], v8[:, :, 1:2], ALU.add))
                ch.wait()
                ch.step(dve.reciprocal(vinv[:], vsum[:]))
                iota = con[:, C_IOTA:C_IOTA + NT * EXPERTS].rearrange("p (t e) -> p t e", e=EXPERTS)
                for k in range(2):
                    ins = dve.tensor_tensor(pick[:, k, :, :], iota, idxf[:, k, :].rearrange("p (t a) -> p t a", a=1).to_broadcast([P, NT, EXPERTS]), ALU.is_equal)
                ch.step(ins)
                ch.wait()
                ch.step(dve.tensor_tensor(wts[:], v8[:, :, 0:2], vinv[:].to_broadcast([P, NT, 2]), ALU.mult))
                dve.tensor_tensor(sel[:], pick[:, 0, :, :], pick[:, 1, :, :], ALU.add).then_inc(sel_ready, 1)
                ch.wait()
                for k in range(2):
                    ins = dve.tensor_tensor(part[:, k, :, :], pick[:, k, :, :], wts[:, :, k:k + 1].to_broadcast([P, NT, EXPERTS]), ALU.mult)
                ch.step(ins)
                ch.wait()
                ch.step(dve.tensor_tensor(y[:, :, D:ROW], part[:, 0, :, :], part[:, 1, :, :], ALU.add))
                ch.wait()
                full_of(dve, G, "pos", 0, g=g)
                before = bank(G, "pos", 0)[:, 0:NT * EXPERTS].rearrange("p (t e) -> p t e", e=EXPERTS)
                for k in range(2):
                    ins = dve.tensor_tensor(part[:, k, :, :], pick[:, k, :, :], before, ALU.mult)
                emptied(ins, G, "pos", 0)
                read_of(dve, G, "pos", 0, g=g)
                ch.step(dve.tensor_reduce(place[:], part[:], AX.X, ALU.add))
                ch.step(dve.tensor_reduce(selsum[:], sel[:].rearrange("p t e -> p e t"), AX.X, ALU.add))
                ch.wait()
                dve.wait_ge(list_out, PRIMED + g * 2 * NT * 16)
                dve.tensor_tensor(selcum[:], selcum[:], selsum[:], ALU.add)
                dve.tensor_copy(tok[:], tokf[:])
                ch.step(dve.scalar_tensor_tensor(dest[:], idxf[:], float(TOKENS), place[:], ALU.mult, ALU.add))
                ch.wait()
                dve.tensor_scalar(tokf[:], tokf[:], float(GT), None, ALU.add).then_inc(dest_ready, 1)
                assert ch.n == PER, ch.n


            full_of(dve, "count", "all", 0)
            dve.tensor_reduce(most[:], bank("count", "all", 0)[:, 0:EXPERTS], AX.X, ALU.max).then_inc(free[banks.bank("count", "all", 0)], 1)
            read_of(dve, "count", "all", 0)
            dve.tensor_scalar(flag_u[:], most[:], float(SLOTS), None, ALU.is_gt).then_inc(flag_ready, 1)

            def body(c, i, before):
                E = "expert"
                for b in range(TURN):
                    full_of(dve, E, "mid", b, g=before)
                    bias = small[:, bass.ds(i * (TURN * FT) + S_EB + b * FT, FT)].rearrange("p (f a) -> p f a", a=1)
                    emptied(dve.tensor_tensor(pre, bank(E, "mid", b)[:, 0:FT * SLOTS].rearrange("p (f n) -> p f n", f=FT),
                                              bias.to_broadcast([P, FT, SLOTS]), ALU.add), E, "mid", b)
                    dve.wait_ge(pre_ready, before * TURN + b + 1)
                    dve.scalar_tensor_tensor(ehT[:, b % 2, :, :], ee, LA, el, ALU.subtract, ALU.min).then_inc(act_ready, 1)
                    full_of(dve, E, "down", b, g=before)
                    if b >= 2:
                        dve.wait_ge(added[b - 2], PRIMED + 16 * (before + 1))
                    else:
                        dve.wait_ge(added[b + 2], PRIMED + 16 * before)
                    emptied(dve.tensor_scalar(ye[:, b % 2, :], bank(E, "down", b)[0:SLOTS, 0:D],
                                              xg[:, b, bass.ds(i * TURN + D + b, 1)], None, ALU.mult), E, "down", b)
            expert_passes(dve, body)


_INS = ['x', 'L0_tok_W', 'L0_tok_b', 'L0_tok_cls_token', 'L0_tok_pos_enc', 'L0_attn_wq', 'L0_attn_wk', 'L0_attn_wv', 'L0_attn_wo',
        'L0_attn_w1', 'L0_attn_w2', 'L0_attn_w3', 'L0_attn_ln1_g', 'L0_attn_ln1_b', 'L0_attn_ln2_g', 'L0_attn_ln2_b',
        'L0_ffn_gate_wi', 'L0_ffn_gate_bi', 'L0_ffn_gate_wo', 'L0_ffn_gate_bo', 'L0_ffn_exp_wi', 'L0_ffn_exp_bi', 'L0_ffn_exp_wo', 'L0_ffn_exp_bo']


def kernel(**inputs):
    import numpy as _np
    import concourse.bacc as _bacc
    from concourse import mybir as _mybir
    from concourse.bass_utils import run_bass_kernel_spmd as _run

    nc = _bacc.Bacc("TRN2", target_bir_lowering=False, num_devices=1)
    arrays, args = {}, []
    for name in _INS:
        a = _np.ascontiguousarray(inputs[name])
        arrays[f"in_{name}"] = a
        args.append(nc.dram_tensor(f"in_{name}", a.shape, _mybir.dt.from_np(a.dtype), kind="ExternalInput").ap())
    arrays["const"] = constants()
    args.append(nc.dram_tensor("const", arrays["const"].shape, F32, kind="ExternalInput").ap())
    args.append(nc.dram_tensor("out_0", (TOKENS + SLOTS, D), F32, kind="ExternalOutput").ap())
    build(nc, *args)
    r = _run(nc, [arrays], core_ids=[0])
    return r.results[0]["out_0"][:TOKENS].reshape(IMAGES, SEQ, D)
```

```python
from contextlib import ExitStack

import concourse.bass as bass
from concourse import mybir
import numpy as np

F32 = mybir.dt.float32
BF16 = mybir.dt.bfloat16
U32 = mybir.dt.uint32
ALU = mybir.AluOpType
ACT = mybir.ActivationFunctionType
AX = mybir.AxisListType

P = 128
IMAGES, CH, SIDE, PATCH = 64, 3, 96, 16
GRID = SIDE // PATCH
SEQ = GRID * GRID + 1
D = 256
DM = D // P
HEADS, HD = 16, 16
HIDDEN = 704
GLU = [min(P, HIDDEN - P * i) for i in range((HIDDEN + P - 1) // P)]
EXPERTS, FF = 8, 1024
FT = FF // P
PK = CH * PATCH * PATCH // P

GROUPS = 4
GI = IMAGES // GROUPS
GT = GI * SEQ
HALF = GT // 2
TILES = [(a, min(P, GT - a)) for a in range(0, GT, P)]
NT = len(TILES)
BATCHES = (range(0, 3), range(3, NT))
PAIRS = GI // 2
PITCH = 64
TOKENS = IMAGES * SEQ
SLOTS = 64
TURN = 4
CHUNKS = TOKENS // SLOTS
ROW = D + EXPERTS
LAMBDA, ALPHA = 1.0507009873554805, 1.6732632423543772
LA = LAMBDA * ALPHA
EPS = 1e-5
NEG = -1.0e30
STORES = 2
PRIMED = 16

C_ID, C_TRI, C_MASK = 0, P, 2 * P
C_COS = C_MASK + 8 * SEQ
C_SIN = C_COS + NT * HD
C_IOTA = C_SIN + NT * HD
C_TOK = C_IOTA + NT * EXPERTS
C_HEAD = C_TOK + NT
C_PAR = C_HEAD + 4
C_PAD = C_PAR + 2
C_LNLA = C_PAD + SLOTS
C_ALL = C_LNLA + 1


def constants():
    c = np.zeros((P, C_ALL), np.float32)
    p = np.arange(P)
    c[:, C_ID:C_ID + P] = np.eye(P)
    c[:, C_TRI:C_TRI + P] = p[:, None] < p[None, :]
    key = np.tile(np.arange(SEQ), 8)
    c[:, C_MASK:C_MASK + 8 * SEQ] = np.where(key[None, :] <= (p % PITCH)[:, None], 0.0, NEG)
    freqs = (np.float32(1.0) / np.float32(10000.0) ** (np.arange(0, HD, 2, dtype=np.float32) / np.float32(HD))).astype(np.float32)
    for t, (a, n) in enumerate(TILES):
        ang = (((a + p) % SEQ).astype(np.float32)[:, None] * freqs[None, :]).astype(np.float32)
        c[:, C_COS + t * HD:C_COS + (t + 1) * HD] = np.repeat(np.cos(ang), 2, axis=1)
        s = np.repeat(np.sin(ang), 2, axis=1)
        s[:, 0::2] *= -1
        c[:, C_SIN + t * HD:C_SIN + (t + 1) * HD] = s
        c[:, C_IOTA + t * EXPERTS:C_IOTA + (t + 1) * EXPERTS] = np.where(p[:, None] < n, np.arange(EXPERTS)[None, :], -1)
        c[:, C_TOK + t] = a + p
    for j in range(4):
        c[:, C_HEAD + j] = (p // HD) % 4 == j
    for j in range(2):
        c[:, C_PAR + j] = (p // HD) % 2 == j
    c[:, C_PAD:C_PAD + SLOTS] = TOKENS + np.arange(SLOTS)[None, :]
    c[:, C_LNLA] = np.log(LA)
    return c


DENSE = [0, 1, 2, 3]
SCORE = [4, 6]


PATCH_STEPS = range(0, CH)
EMBED_STEPS = (4, 7)


def attention_steps(front):
    for s in range(PAIRS + 3):
        if s < PAIRS:
            yield ("score", s)
        if front and s in PATCH_STEPS:
            for i in range(4 * s, 4 * s + 4):
                yield ("patch", i)
        if front and s in EMBED_STEPS:
            yield ("embed", EMBED_STEPS.index(s))
        if 2 <= s < PAIRS + 2:
            yield ("turn", 2 * (s - 2))
            yield ("turn", 2 * (s - 2) + 1)
        if s >= 3:
            yield ("out", 2 * (s - 3))
            yield ("out", 2 * (s - 3) + 1)


def each_tile(kind):
    return [(kind, t) for t in range(NT)]


def back_jobs(front):
    def halves(turned, kinds, per):
        return [j for n in range(2) for j in [(turned, t) for t in BATCHES[n]] + [(k, n * per + f) for f in range(per) for k in kinds]]
    return (
        list(attention_steps(front)) + each_tile("wo") + [("embed", i) for i in range(len(EMBED_STEPS), 2 * DM)] * front
        + halves("a2", ("glu", "up"), len(GLU)) + each_tile("w2") + each_tile("token") * front + halves("y", ("gate",), FT) + each_tile("logit")
        + (each_tile("a1") + each_tile("qk") + [("v", i) for i in range(PAIRS // 2)]) * front + [("pos", 0)] + each_tile("qkT") * front
    )


FIRST_JOBS = (
    [("patch", i) for i in range(2 * PK)] + [("embed", i) for i in range(2 * DM)] + each_tile("token") + each_tile("a1") + each_tile("qk")
    + [("v", i) for i in range(PAIRS // 2)] + each_tile("qkT")
)
EXPERT_JOBS = [("xT", 0)] + [j for b in range(TURN) for j in [("mid", b)] + [("xT", b + 1)] * (b + 1 < TURN) + [("down", b)]]
SETUP_JOBS = [("wt", i) for i in range(PK)] + [("small", 0), ("posT", 0)]


class Banks:

    def __init__(self):
        self.uses = [0] * 8
        self.jobs = {}
        self.turn = 0
        self.scores = 0
        self.section("setup", SETUP_JOBS, 1)
        self.section("first", FIRST_JOBS, 1)
        self.section("loop", back_jobs(True), GROUPS - 1)
        self.section("last", back_jobs(False), 1)
        self.section("count", [("all", 0)], 1)
        self.section("expert", EXPERT_JOBS, 0)

    def section(self, name, jobs, times):
        base, count = list(self.uses), [0] * 8
        placed = {}
        for job in jobs:
            if job[0] in ("score", "small", "posT"):
                bank = SCORE[self.scores % 2]
                self.scores += 1
            else:
                if job[0] == "out" and job[1] % 2 == 0:
                    self.turn += self.turn % 2
                bank = DENSE[self.turn % len(DENSE)]
                self.turn += 1
            placed[job] = (bank, count[bank])
            count[bank] += 1
        for job, (bank, before) in placed.items():
            self.jobs[(name,) + job] = (bank, base[bank] + before, count[bank])
        self.uses = [u + times * c for u, c in zip(base, count)]

    def bank(self, name, *job):
        return self.jobs[(name,) + job][0]

    def vacant(self, name, *job, g=0):
        bank, before, per = self.jobs[(name,) + job]
        return g * per + before

    def filled(self, name, *job, g=0):
        return self.vacant(name, *job, g=g) + 1

    emptied = filled


def build(nc, x, tok_W, tok_b, cls_token, pos_enc, wq, wk, wv, wo, w1, w2, w3, ln1_g, ln1_b, ln2_g, ln2_b,
          gate_wi, gate_bi, gate_wo, gate_bo, exp_wi, exp_bi, exp_wo, exp_bo, const, out):
    banks = Banks()
    ctx = ExitStack()
    with ctx:
        def sb(name, shape, dt=F32):
            return ctx.enter_context(nc.sbuf_tensor(name, shape, dt))

        def sem(name):
            return ctx.enter_context(nc.semaphore(name))

        rows = nc.dram_tensor("token_rows", [TOKENS + SLOTS, ROW], F32, kind="Internal").ap()
        lists = nc.dram_tensor("expert_lists", [EXPERTS * TOKENS, 1], U32, kind="Internal").ap()

        con = sb("con", [P, C_ALL])
        ident = con[:, C_ID:C_ID + P]
        tri = con[:, C_TRI:C_TRI + P]
        ident_bf = sb("ident_bf", [P, P], BF16)
        mask_bf = sb("mask_bf", [P, 8 * SEQ], BF16)
        ones = sb("ones", [P, P])
        small_rows = sb("small_rows", [P, P])
        small = sb("small", [P, P])
        WT = sb("WT", [P, PK, D])
        posT = sb("posT", [P, DM, SEQ])
        wqk_s = sb("wqk_s", [P, DM, 2 * D])
        wv_s = sb("wv_s", [P, DM, D])
        wo_s = sb("wo_s", [P, DM, D])
        w1_s = sb("w1_s", [P, DM, HIDDEN])
        w3_s = sb("w3_s", [P, DM, HIDDEN])
        w2_s = sb("w2_s", [P, len(GLU), D])
        gwi_s = sb("gwi_s", [P, DM, FF])
        gwo_s = sb("gwo_s", [P, FT, D])
        gbo_s = sb("gbo_s", [P, D])
        S_TB, S_CLS, S_G1, S_B1, S_G2, S_B2 = 0, 2, 4, 6, 8, 10
        S_GB = 12
        S_EB = S_GB + FT
        S_ROWS = S_EB + EXPERTS * FT
        gate_exp_bias = sb("gate_exp_bias", [P, FT])
        gate_lin_bias = sb("gate_lin_bias", [P, FT])

        XC = PATCH * SIDE
        EW = DM * FF
        VN, KN = PAIRS * D, 2 * DM * 4 * 2 * SEQ
        arena = sb("arena", [P, 2 * XC + VN + KN])
        xin = arena[:, 0:2 * XC].rearrange("p (c n) -> p c n", c=2)
        V = arena[:, 2 * XC:2 * XC + VN].rearrange("p (i n) -> p i n", i=PAIRS)
        kx = arena[:, 2 * XC + VN:].rearrange("p (b m h n) -> p b m h n", b=2, m=DM, h=4)
        xp = sb("xp", [P, 2, GRID, P])
        hidT = sb("hidT", [P, FT, GT])
        gT = hidT[:, 0:len(GLU), :]
        patT = hidT[:, 0:PK, :]
        h0T = sb("h0T", [P, DM, GT])
        h0 = sb("h0", [P, NT, D])
        u = sb("u", [P, NT, D])
        z = sb("z", [P, NT, D])
        stats = sb("stats", [P, NT, 6])
        mv = sb("mv", [P, NT, 2])
        rstd = sb("rstd", [P, NT])
        var_eps = sb("var_eps", [P, NT])
        minus_half = sb("minus_half", [P, NT])
        a1T = sb("a1T", [P, DM, GT])
        qk = sb("qk", [P, NT, 2 * D])
        swapped = sb("swapped", [P, 2, 2 * D])
        qT = sb("qT", [P, DM, GT + PITCH - SEQ])
        kT = sb("kT", [P, DM, GT])
        top = sb("top", [P, 2, 16])
        total = sb("total", [P, 2, 16])
        share = sb("share", [P, 2, 16])
        shifted = sb("shifted", [P, 2, 16 * SEQ])
        probs = sb("probs", [P, 3, 16, PITCH])
        probsT = sb("probsT", [P, 2, 2, 4 * P])
        a1P = probsT[:].rearrange("p b r n -> p (b r n)").rearrange("p (m n) -> p m n", m=DM)
        even = sb("even", [P, 2, DM, 2 * SEQ])
        attnT = sb("attnT", [P, DM, GT])
        h1 = u
        res = h0
        a2T = a1T
        th = sb("th", [P, 4, HALF])
        H2 = sb("H2", [P, NT, D])
        y = sb("y", [P, NT, ROW])
        yT = a1T
        qk_area = qk[:].rearrange("p t n -> p (t n)")
        ex, lin = (qk_area[:, i * 3 * HALF:(i + 1) * 3 * HALF].rearrange("p (b n) -> p b n", b=3) for i in range(2))
        logits = sb("logits", [P, 2, D])
        v8 = sb("v8", [P, NT, 8])
        i8 = sb("i8", [P, NT, 8], U32)
        idxf = sb("idxf", [P, 2, NT])
        vsum = sb("vsum", [P, NT, 1])
        vinv = sb("vinv", [P, NT, 1])
        wts = sb("wts", [P, NT, 2])
        pick = sb("pick", [P, 2, NT, EXPERTS])
        sel = sb("sel", [P, NT, EXPERTS])
        selcum = sb("selcum", [P, EXPERTS])
        selsum = sb("selsum", [P, EXPERTS])
        part = sb("part", [P, 2, NT, EXPERTS])
        place = sb("place", [P, 2, NT])
        dest = sb("dest", [P, 2, NT], U32)
        tokf = sb("tokf", [P, NT])
        tok = sb("tok", [P, NT], U32)
        hid_area = hidT[:].rearrange("p f n -> p (f n)")
        ewi = [a[:, 0:EW].rearrange("p (k n) -> p k n", k=DM) for a in (arena, hid_area)]
        ewo = [a[:, EW:2 * EW].rearrange("p (f n) -> p f n", f=FT) for a in (arena, hid_area)]
        most = sb("most", [P, 1])
        flag_u = sb("flag_u", [P, 1], U32)
        slot_tok = sb("slot_tok", [SLOTS, TURN], U32)
        pad_row = sb("pad_row", [P, SLOTS], U32)
        zero_rows = sb("zero_rows", [SLOTS, ROW])
        ebo = sb("ebo", [1, 2, D])
        xg = probs[:].rearrange("p a h n -> p (a h n)")[0:SLOTS, 0:TURN * ROW].rearrange("p (b n) -> p b n", b=TURN)
        xT = swapped[:].rearrange("p a n -> p (a n)")[:, 0:2 * DM * SLOTS].rearrange("p (b m n) -> p b m n", b=2, m=DM)
        ye = swapped[:].rearrange("p a n -> p (a n)")[0:SLOTS, 2 * DM * SLOTS:2 * DM * SLOTS + 2 * D].rearrange("p (b n) -> p b n", b=2)
        pre, ee, el = (qk[:, i, :].rearrange("p (f n) -> p f n", f=FT) for i in range(3))
        ehT = qk[:, 3:5, :].rearrange("p b (f n) -> p b f n", f=FT)
        ps = ctx.enter_context(nc.psum_tensor("ps", [P, 8, 512], F32))

        full = [sem(f"bank_filled{b}") for b in range(8)]
        free = [sem(f"bank_emptied{b}") for b in range(8)]
        waits_passed = sem("waits_passed")
        con_in = sem("con_in")
        weight_in = sem("weight_in")
        tokw_in = sem("tokw_in")
        small_in = sem("small_in")
        x_in = [sem(f"x_in{c}") for c in range(CH)]
        const_ready = sem("const_ready")
        setup_done = sem("setup_done")
        a_step = sem("vector_step_a")
        xp_ready = sem("xp_ready")
        var_ready = sem("var_ready")
        pool_step = sem("pool_step")
        rstd_ready = sem("rstd_ready")
        a1P_ready = sem("a1P_ready")
        z1_ready = sem("z1_ready")
        z2_ready = sem("z2_ready")
        y_ready = sem("y_ready")
        qk_ready = sem("qk_ready")
        kx_ready = sem("kx_ready")
        kT_ready = sem("kT_ready")
        exp_ready = sem("exp_ready")
        share_ready = sem("share_ready")
        probs_ready = sem("probs_ready")
        even_ready = sem("even_ready")
        res_ready = sem("res_ready")
        th_ready = sem("th_ready")
        hid_ready = sem("hid_ready")
        sel_ready = sem("sel_ready")
        weights_ready = sem("weights_ready")
        dest_ready = sem("dest_ready")
        h2_out = sem("h2_stored")
        row_out = sem("row_stored")
        list_out = sem("list_stored")
        flag_ready = sem("flag_ready")
        slots_in = [sem(f"slots_in{b}") for b in range(TURN)]
        gathered = [sem(f"rows_gathered{b}") for b in range(TURN)]
        ew_in = [sem(f"expert_weights_in{b}") for b in range(2)]
        pre_ready = sem("expert_pre_ready")
        act_ready = sem("expert_act_ready")
        added = [sem(f"expert_rows_added{b}") for b in range(TURN)]

        def bank(*job):
            return ps[:, banks.bank(*job), :]

        def turns_of(job, g):
            return g if job[0] in ("loop", "expert") else 0

        def full_of(eng, *job, g=0):
            eng.wait_ge(full[banks.bank(*job)], banks.filled(*job, g=turns_of(job, g)))

        def read_of(eng, *job, g=0):
            eng.wait_ge(free[banks.bank(*job)], banks.emptied(*job, g=turns_of(job, g)))

        def all_read(eng, S, kind, indices, g=0):
            last = {banks.bank(S, kind, i): i for i in indices}
            alone(eng)
            for i in last.values():
                read_of(eng, S, kind, i, g=g)

        def vacant_for(eng, *job, g=0):
            eng.wait_ge(free[banks.bank(*job)], banks.vacant(*job, g=turns_of(job, g)))

        def alone(eng):
            eng.sem_inc(waits_passed, 1)

        def filled(ins, *job):
            ins.then_inc(full[banks.bank(*job)], 1)

        def emptied(ins, *job):
            ins.then_inc(free[banks.bank(*job)], 1)

        def expert_passes(eng, body):
            with eng.Fori(0, EXPERTS // TURN) as i:
                body(0, i, i)
            eng.wait_ge(flag_ready, 1)
            more = eng.value_load(flag_u[0:1, 0:1], min_val=0, max_val=1)
            with eng.If(more > 0):
                with eng.Fori(1, CHUNKS) as c:
                    with eng.Fori(0, EXPERTS // TURN) as i:
                        body(c, i, c * (EXPERTS // TURN) + i)

        LAST = GROUPS - 1

        def section(g):
            return "last" if isinstance(g, int) and g == LAST else "loop"

        x_rows = x.rearrange("b c (n r) w -> c b n (r w)", r=PATCH)
        out_rows = out

        block = ctx.enter_context(nc.Block())

        @block.sync
        def _(sp):
            sp.dma_start(con[:], const).then_inc(con_in, 16)
            sp.sem_inc(h2_out, PRIMED)
            wnat = patT.rearrange("p k n -> p (k n)")[:, 0:DM * PK * P].rearrange("p (m f) -> p m f", m=DM)
            sp.dma_start(wnat, tok_W.rearrange("(m p) f -> p m f", p=P)).then_inc(tokw_in, 16)
            for c in range(2):
                sp.dma_start(xin[0:GI * GRID, c, :], x_rows[c, 0:GI]).then_inc(x_in[c], 16)
            pos_nat = h0[0:SEQ, 0, :]
            sp.dma_start(pos_nat, pos_enc[0]).then_inc(small_in, 16)
            for at, v in ((S_TB, tok_b), (S_G1, ln1_g), (S_B1, ln1_b), (S_G2, ln2_g), (S_B2, ln2_b), (S_GB, gate_bi)):
                n = v.shape[0] // P
                sp.dma_start(small_rows[at:at + n, :], v.rearrange("(n p) -> n p", p=P)).then_inc(small_in, 16)
            sp.dma_start(small_rows[S_CLS:S_CLS + DM, :], cls_token[0, 0, :].rearrange("(n p) -> n p", p=P)).then_inc(small_in, 16)
            sp.dma_start(small_rows[S_EB:S_EB + EXPERTS * FT, :], exp_bi.rearrange("e (n p) -> (e n) p", p=P)).then_inc(small_in, 16)
            sp.dma_start(wqk_s[:, :, 0:D], wq.rearrange("(k p) n -> p k n", p=P)).then_inc(weight_in, 16)
            sp.dma_start(wqk_s[:, :, D:2 * D], wk.rearrange("(k p) n -> p k n", p=P)).then_inc(weight_in, 16)
            sp.dma_start(wv_s[:], wv.rearrange("(k p) n -> p k n", p=P)).then_inc(weight_in, 16)
            sp.dma_start(wo_s[:], wo.rearrange("(k p) n -> p k n", p=P)).then_inc(weight_in, 16)
            sp.dma_start(w1_s[:], w1.rearrange("(k p) n -> p k n", p=P)).then_inc(weight_in, 16)
            sp.dma_start(w3_s[:], w3.rearrange("(k p) n -> p k n", p=P)).then_inc(weight_in, 16)
            whole = HIDDEN // P
            sp.dma_start(w2_s[:, 0:whole, :], w2[0:whole * P].rearrange("(k p) n -> p k n", p=P)).then_inc(weight_in, 16)
            sp.dma_start(w2_s[0:GLU[-1], whole, :], w2[whole * P:HIDDEN]).then_inc(weight_in, 16)
            sp.dma_start(gwi_s[:], gate_wi.rearrange("(k p) n -> p k n", p=P)).then_inc(weight_in, 16)
            sp.dma_start(gwo_s[:], gate_wo.rearrange("(k p) n -> p k n", p=P)).then_inc(weight_in, 16)
            sp.dma_start(gbo_s[:], gate_bo.rearrange("(a n) -> a n", a=1).to_broadcast([P, D])).then_inc(weight_in, 16)
            sp.wait_ge(const_ready, 3)
            sp.dma_start(rows[TOKENS:TOKENS + SLOTS, :], zero_rows[:]).then_inc(row_out, 16)
            def load_patches(g, more):
                sp.wait_ge(xp_ready, g * CH + 1)
                alone(sp)
                sp.dma_start(xin[0:GI * GRID, 0, :], x_rows[2, bass.ds(g * GI, GI)]).then_inc(x_in[2], 16)
                if more:
                    sp.wait_ge(xp_ready, g * CH + 2)
                    alone(sp)
                    sp.dma_start(xin[0:GI * GRID, 1, :], x_rows[1, bass.ds((g + 1) * GI, GI)]).then_inc(x_in[1], 16)
                    sp.wait_ge(xp_ready, g * CH + 3)
                    alone(sp)
                    sp.dma_start(xin[0:GI * GRID, 0, :], x_rows[0, bass.ds((g + 1) * GI, GI)]).then_inc(x_in[0], 16)

            def store(dst, src, g, done):
                whole = NT - 1
                a, n = TILES[whole]
                sp.dma_start(dst[bass.ds(g * GT, whole * P), :].rearrange("(t p) d -> p t d", p=P), src[:, 0:whole, :]).then_inc(done, 16)
                sp.dma_start(dst[bass.ds(g * GT + a, n), :], src[0:n, whole, :]).then_inc(done, 16)

            def store_group(g):
                for t in range(NT):
                    read_of(sp, section(g), "w2", t, g=g)
                    alone(sp)
                store(out_rows, H2, g, h2_out)
                sp.wait_ge(weights_ready, g + 1)
                alone(sp)
                store(rows, y, g, row_out)

            load_patches(0, True)
            with sp.Fori(0, GROUPS - 2) as g:
                load_patches(g + 1, True)
                store_group(g)
            load_patches(LAST, False)
            store_group(LAST - 1)
            full_of(sp, "last", "out", 2 * PAIRS - 1, g=0)
            store_group(LAST)
            E = "expert"

            def load_expert(b, i):
                e = i * TURN + b
                sp.dma_start(ewi[b % 2], exp_wi[bass.ds(e, 1)].rearrange("a (k p) n -> p (a k) n", p=P)).then_inc(ew_in[b % 2], 16)
                sp.dma_start(ewo[b % 2], exp_wo[bass.ds(e, 1)].rearrange("a (f p) n -> p (a f) n", p=P)).then_inc(ew_in[b % 2], 16)
                sp.dma_start(ebo[:, b % 2, :], exp_bo[bass.ds(e, 1)]).then_inc(ew_in[b % 2], 16)

            def body(c, i, before):
                for b in range(TURN):
                    if b < 2:
                        full_of(sp, E, "down", b + 2, g=before - 1)
                    else:
                        full_of(sp, E, "down", b - 2, g=before)
                    alone(sp)
                    if b == 1:
                        full_of(sp, "last", "logit", NT - 1)
                    load_expert(b, i)
                    if b == 1:
                        sp.wait_ge(list_out, PRIMED + 16 * 2 * NT * (GROUPS + 1))
                        for s in range(TURN):
                            at = sp.snap((i * TURN + s) * TOKENS + c * SLOTS)
                            sp.wait_ge(added[s], PRIMED + 16 * before)
                            alone(sp)
                            sp.dma_start(slot_tok[:, s:s + 1], lists[bass.ds(at, SLOTS), :]).then_inc(slots_in[s], 16)
            expert_passes(sp, body)
            sp.wait_ge(h2_out, PRIMED + 16 * STORES * GROUPS)
            sp.wait_ge(row_out, PRIMED + 16 * STORES * GROUPS)

        @block.tensor
        def _(pe):
            def turn_tiles(S, job, src, g, f, tiles=range(NT)):
                for t in tiles:
                    a, n = TILES[t]
                    vacant_for(pe, S, job, t, g=g)
                    ready = {"a1": z1_ready, "a2": z2_ready, "y": y_ready}[job]
                    pe.wait_ge(ready, f * NT + t + 1)
                    for m in range(DM):
                        mm = pe.transpose(bank(S, job, t)[:, m * P:m * P + n], src[0:n, t, m * P:(m + 1) * P], ident[0:n, 0:n])
                    filled(mm, S, job, t)

            pe.wait_ge(con_in, 16)
            pe.wait_ge(tokw_in, 16)
            wnat = patT.rearrange("p k n -> p (k n)")[:, 0:DM * PK * P].rearrange("p (m f) -> p m f", m=DM)
            for k in range(PK):
                vacant_for(pe, "setup", "wt", k)
                for m in range(DM):
                    mm = pe.transpose(bank("setup", "wt", k)[:, m * P:(m + 1) * P], wnat[:, m, k * P:(k + 1) * P], ident)
                filled(mm, "setup", "wt", k)
            pe.wait_ge(small_in, 16 * 9)
            vacant_for(pe, "setup", "small", 0)
            filled(pe.transpose(bank("setup", "small", 0)[:, 0:S_ROWS], small_rows[0:S_ROWS, :], ident[0:S_ROWS, 0:S_ROWS]), "setup", "small", 0)
            vacant_for(pe, "setup", "posT", 0)
            for m in range(DM):
                mm = pe.transpose(bank("setup", "posT", 0)[:, m * SEQ:(m + 1) * SEQ], h0[0:SEQ, 0, m * P:(m + 1) * P], ident[0:SEQ, 0:SEQ])
            filled(mm, "setup", "posT", 0)
            pe.wait_ge(setup_done, 2)

            def patch(S, g, f, i):
                k, side = i // 2, i % 2
                c, upper = k // 2, k % 2
                if i % 4 == 0:
                    pe.wait_ge(xp_ready, f * CH + c + 1)
                vacant_for(pe, S, "patch", i, g=g)
                for j in range(3):
                    mm = pe.transpose(bank(S, "patch", i)[:, j * GI * GRID:(j + 1) * GI * GRID], xp[0:GI * GRID, upper, 3 * side + j, :],
                                      ident[0:GI * GRID, 0:GI * GRID])
                filled(mm, S, "patch", i)

            def embed(S, g, i):
                n, m = i // DM, i % DM
                vacant_for(pe, S, "embed", i, g=g)
                if i == 0:
                    all_read(pe, S, "patch", range(2 * PK), g)
                for k in range(PK):
                    mm = pe.matmul(bank(S, "embed", i)[:, 0:HALF], WT[:, k, m * P:(m + 1) * P], patT[:, k, n * HALF:(n + 1) * HALF],
                                   start=(k == 0), stop=(k == PK - 1))
                filled(mm, S, "embed", i)

            def tokens(S, g):
                for t, (a, n) in enumerate(TILES):
                    vacant_for(pe, S, "token", t, g=g)
                    if t in (0, 2):
                        all_read(pe, S, "embed", range(2 * DM if t else DM), g)
                    for m in range(DM):
                        mm = pe.transpose(bank(S, "token", t)[0:n, m * P:(m + 1) * P], h0T[:, m, a:a + n], ident)
                    filled(mm, S, "token", t)

            def project(S, g, f):
                turn_tiles(S, "a1", z, g, f)
                pe.wait_ge(weight_in, 16 * 11)
                for t, (a, n) in enumerate(TILES):
                    vacant_for(pe, S, "qk", t, g=g)
                    read_of(pe, S, "a1", t, g=g)
                    for k in range(DM):
                        mm = pe.matmul(bank(S, "qk", t)[0:n, :], a1T[:, k, a:a + n], wqk_s[:, k, :], start=(k == 0), stop=(k == DM - 1))
                    filled(mm, S, "qk", t)
                for i in range(PAIRS // 2):
                    vacant_for(pe, S, "v", i, g=g)
                    pe.wait_ge(a1P_ready, f + 1)
                    for j in range(2):
                        a = (2 * i + j) * P
                        for k in range(DM):
                            mm = pe.matmul(bank(S, "v", i)[:, j * D:(j + 1) * D], a1P[:, k, a:a + P], wv_s[:, k, :],
                                           start=(k == 0), stop=(k == DM - 1))
                    filled(mm, S, "v", i)

            def turn_queries(S, g, f):
                for t, (a, n) in enumerate(TILES):
                    vacant_for(pe, S, "qkT", t, g=g)
                    pe.wait_ge(qk_ready, f * NT + t + 1)
                    for m in range(2 * DM):
                        mm = pe.transpose(bank(S, "qkT", t)[:, m * P:m * P + n], qk[0:n, t, m * P:(m + 1) * P], ident[0:n, 0:n])
                    filled(mm, S, "qkT", t)
                all_read(pe, S, "qkT", range(NT), g)

            def position(S, g):
                vacant_for(pe, S, "pos", 0, g=g)
                pe.wait_ge(sel_ready, g + 1)
                before = bank(S, "pos", 0)[:, 0:NT * EXPERTS].rearrange("p (t e) -> p t e", e=EXPERTS)
                pe.matmul(before, tri, sel[:], start=True, stop=False, skip_group_check=True)
                for back in range(1, NT):
                    pe.matmul(before[:, back:NT, :], ones[:], sel[:, 0:NT - back, :], start=False, stop=False, skip_group_check=True)
                filled(pe.matmul(before, ones[:], selcum[:].rearrange("p (a e) -> p a e", a=1).to_broadcast([P, NT, EXPERTS]),
                                 start=False, stop=True, skip_group_check=True), S, "pos", 0)

            def back(S, g, front):
                for kind, i in attention_steps(front):
                    if kind == "patch":
                        patch(S, g, g + 1, i)
                        continue
                    if kind == "embed":
                        embed(S, g, i)
                        continue
                    vacant_for(pe, S, kind, i, g=g)
                    if kind == "score":
                        pe.wait_ge(kx_ready, g * PAIRS + i + 1)
                        for r in range(2):
                            b = ps[:, banks.bank(S, "score", i) + r, 0:8 * SEQ]
                            pe.matmul(b, ident_bf[:], mask_bf[:], start=True, stop=False, skip_group_check=True)
                            for m in range(DM):
                                for j in range(2):
                                    a = (2 * i + j) * SEQ
                                    mm = pe.matmul(b.rearrange("p (h n) -> p h n", h=4)[PITCH * m:PITCH * (m + 1), :, j * SEQ:(j + 1) * SEQ],
                                                   qT[64 * r:64 * r + 64, m, a:a + PITCH], kx[64 * r:64 * r + 64, i % 2, m, :, j * SEQ:(j + 1) * SEQ],
                                                   start=False, stop=True, skip_group_check=True)
                    elif kind == "turn":
                        p, r = i // 2, i % 2
                        pe.wait_ge(probs_ready, g * PAIRS + p + 1)
                        for j in range(4):
                            src = probs[:, p % 3, (4 * r + j) * 2:(4 * r + j) * 2 + 2, :].rearrange("p a n -> p (a n)")
                            mm = pe.transpose(bank(S, kind, i)[:, j * P:(j + 1) * P], src, ident)
                    else:
                        pair, j = i // 2, i % 2
                        if j == 0:
                            all_read(pe, S, "turn", (2 * pair, 2 * pair + 1), g)
                        alone(pe)
                        b = bank(S, kind, i)[:, 0:2 * 2 * SEQ].rearrange("p (m e c) -> p m e c", m=DM, e=2)
                        for m in range(DM):
                            for q in range(4):
                                r, s = q // 2, q % 2
                                pT = probsT[64 * j:64 * j + SEQ, pair % 2, r, :].rearrange("p (h n) -> p h n", h=4)
                                mm = pe.matmul(b[32 * q:32 * q + 32, m, :, :],
                                               V[64 * j:64 * j + SEQ, pair, m * P + 32 * q:m * P + 32 * q + 32],
                                               pT[:, 2 * s:2 * s + 2, PITCH * m:PITCH * m + SEQ], start=True, stop=True,
                                               skip_group_check=True)
                    filled(mm, S, kind, i)
                for t, (a, n) in enumerate(TILES):
                    vacant_for(pe, S, "wo", t, g=g)
                    if t == 0:
                        all_read(pe, S, "out", range(2 * PAIRS), g)
                    for k in range(DM):
                        mm = pe.matmul(bank(S, "wo", t)[0:n, 0:D], attnT[:, k, a:a + n], wo_s[:, k, :], start=(k == 0), stop=(k == DM - 1))
                    filled(mm, S, "wo", t)
                if front:
                    for i in range(len(EMBED_STEPS), 2 * DM):
                        embed(S, g, i)
                for i in range(2 * len(GLU)):
                    n, f = i // len(GLU), i % len(GLU)
                    if f == 0:
                        turn_tiles(S, "a2", z, g, g, BATCHES[n])
                    for kind, w in (("glu", w1_s), ("up", w3_s)):
                        vacant_for(pe, S, kind, i, g=g)
                        if kind == "glu" and f == 0:
                            all_read(pe, S, "a2", BATCHES[n], g)
                        for k in range(DM):
                            mm = pe.matmul(bank(S, kind, i)[0:GLU[f], 0:HALF], w[:, k, f * P:f * P + GLU[f]], a2T[:, k, n * HALF:(n + 1) * HALF],
                                           start=(k == 0), stop=(k == DM - 1))
                        filled(mm, S, kind, i)
                for t, (a, n) in enumerate(TILES):
                    vacant_for(pe, S, "w2", t, g=g)
                    if t in (0, 2):
                        all_read(pe, S, "up", range(len(GLU)) if t == 0 else range(len(GLU), 2 * len(GLU)), g)
                    for f, h in enumerate(GLU):
                        mm = pe.matmul(bank(S, "w2", t)[0:n, 0:D], gT[0:h, f, a:a + n], w2_s[0:h, f, :], start=(f == 0), stop=(f == len(GLU) - 1))
                    filled(mm, S, "w2", t)
                if front:
                    tokens(S, g)
                for i in range(2 * FT):
                    n, f = i // FT, i % FT
                    if f == 0:
                        turn_tiles(S, "y", y, g, g, BATCHES[n])
                    vacant_for(pe, S, "gate", i, g=g)
                    if f == 0:
                        all_read(pe, S, "y", BATCHES[n], g)
                    for k in range(DM):
                        mm = pe.matmul(bank(S, "gate", i)[:, 0:HALF], gwi_s[:, k, f * P:(f + 1) * P], yT[:, k, n * HALF:(n + 1) * HALF],
                                       start=(k == 0), stop=(k == DM - 1))
                    filled(mm, S, "gate", i)
                for t, (a, n) in enumerate(TILES):
                    vacant_for(pe, S, "logit", t, g=g)
                    if t in (0, 2):
                        pe.wait_ge(hid_ready, g * 2 * FT + (FT if t == 0 else 2 * FT))
                    for f in range(FT):
                        mm = pe.matmul(bank(S, "logit", t)[0:n, 0:D], hidT[:, f, a:a + n], gwo_s[:, f, :], start=(f == 0), stop=(f == FT - 1))
                    filled(mm, S, "logit", t)
                if front:
                    project(S, g, g + 1)
                position(S, g)
                if front:
                    turn_queries(S, g, g + 1)

            for i in range(2 * PK):
                patch("first", 0, 0, i)
            for i in range(2 * DM):
                embed("first", 0, i)
            tokens("first", 0)
            project("first", 0, 0)
            turn_queries("first", 0, 0)
            with pe.Fori(0, LAST) as g:
                back("loop", g, True)
            back("last", LAST, False)

            vacant_for(pe, "count", "all", 0)
            pe.wait_ge(dest_ready, GROUPS + 1)
            filled(pe.matmul(bank("count", "all", 0)[:, 0:EXPERTS], ones[:], selcum[:], start=True, stop=True), "count", "all", 0)

            def body(c, i, before):
                E = "expert"

                def turn_rows(b):
                    pe.wait_ge(gathered[b], 16 * (before + 1))
                    vacant_for(pe, E, "xT", b, g=before)
                    alone(pe)
                    for m in range(DM):
                        mm = pe.transpose(bank(E, "xT", b)[:, m * SLOTS:(m + 1) * SLOTS], xg[:, b, m * P:(m + 1) * P], ident[0:SLOTS, 0:SLOTS])
                    filled(mm, E, "xT", b)

                turn_rows(0)
                for b in range(TURN):
                    pe.wait_ge(ew_in[b % 2], 48 * (before * (TURN // 2) + b // 2 + 1))
                    read_of(pe, E, "xT", b, g=before)
                    vacant_for(pe, E, "mid", b, g=before)
                    for f in range(FT):
                        for k in range(DM):
                            mm = pe.matmul(bank(E, "mid", b)[:, f * SLOTS:(f + 1) * SLOTS], ewi[b % 2][:, k, f * P:(f + 1) * P], xT[:, b % 2, k, :],
                                           start=(k == 0), stop=(k == DM - 1))
                    filled(mm, E, "mid", b)
                    if b + 1 < TURN:
                        turn_rows(b + 1)
                    vacant_for(pe, E, "down", b, g=before)
                    pe.wait_ge(act_ready, before * TURN + b + 1)
                    down = bank(E, "down", b)[0:SLOTS, 0:D]
                    pe.matmul(down, ones[0:1, 0:SLOTS], ebo[:, b % 2, :], start=True, stop=False)
                    for f in range(FT):
                        mm = pe.matmul(down, ehT[:, b % 2, f, :], ewo[b % 2][:, f, :], start=False, stop=(f == FT - 1))
                    filled(mm, E, "down", b)
            expert_passes(pe, body)

        @block.scalar
        def _(act):
            def turned(S, job, dst, g, scale=None, bias=None, tiles=range(NT)):
                for t in tiles:
                    a, n = TILES[t]
                    full_of(act, S, job, t, g=g)
                    if scale is None:
                        last = act.activation(dst[:, :, a:a + n], bank(S, job, t)[:, 0:DM * P].rearrange("p (m n) -> p m n", m=DM)[:, :, 0:n], ACT.Copy)
                    else:
                        for m in range(DM):
                            last = act.activation(dst[:, m, a:a + n], bank(S, job, t)[:, m * P:m * P + n], ACT.Identity,
                                                  scale=small[:, scale + m:scale + m + 1], bias=small[:, bias + m:bias + m + 1])
                    emptied(last, S, job, t)

            for k in range(PK):
                full_of(act, "setup", "wt", k)
                emptied(act.activation(WT[:, k, :], bank("setup", "wt", k)[:, 0:D], ACT.Copy), "setup", "wt", k)

            def pixels(S, g, f, c):
                act.wait_ge(x_in[c], 16 * (f + 1))
                if c:
                    full_of(act, S, "patch", 4 * c - 1, g=g)
                for upper in range(2):
                    last = act.activation(xp[0:GI * GRID, upper, :, :].rearrange("p w (r x) -> p r w x", x=PATCH),
                                          xin[0:GI * GRID, c % 2, upper * 8 * SIDE:(upper + 1) * 8 * SIDE].rearrange("p (r w x) -> p r w x", w=GRID, x=PATCH),
                                          ACT.Copy)
                last.then_inc(xp_ready, 1)

            def patch(S, g, i):
                k, side = i // 2, i % 2
                full_of(act, S, "patch", i, g=g)
                dst = patT[:, k, :].rearrange("p (b s) -> p b s", s=SEQ)[:, :, 1:SEQ].rearrange("p b (n w) -> p b n w", w=GRID)
                src = bank(S, "patch", i)[:, 0:3 * GI * GRID].rearrange("p (w b n) -> p w b n", w=3, b=GI)
                for j in range(3):
                    last = act.activation(dst[:, :, :, 3 * side + j], src[:, j, :, :], ACT.Copy)
                emptied(last, S, "patch", i)

            def tokens(S, g):
                for t, (a, n) in enumerate(TILES):
                    full_of(act, S, "token", t, g=g)
                    if S == "loop":
                        read_of(act, S, "w2", t, g=g)
                    emptied(act.activation(h0[0:n, t, :], bank(S, "token", t)[0:n, 0:D], ACT.Copy), S, "token", t)

            def project(S, g):
                turned(S, "a1", a1T, g, S_G1, S_B1)
                for i in range(PAIRS // 2):
                    full_of(act, S, "v", i, g=g)
                    emptied(act.activation(V[:, 2 * i:2 * i + 2, :].rearrange("p a n -> p (a n)"), bank(S, "v", i), ACT.Copy), S, "v", i)
                for t, (a, n) in enumerate(TILES):
                    full_of(act, S, "qkT", t, g=g)
                    src = bank(S, "qkT", t).rearrange("p (m n) -> p m n", m=2 * DM)
                    act.activation(kT[:, :, a:a + n], src[:, DM:2 * DM, 0:n], ACT.Copy).then_inc(kT_ready, 1)
                    emptied(act.activation(qT[:, :, a:a + n], src[:, 0:DM, 0:n], ACT.Copy, scale=float(HD) ** -0.5), S, "qkT", t)

            def back(S, g, front):
                if front:
                    pixels(S, g, g + 1, 0)
                for s in range(PAIRS + 3):
                    if s < PAIRS:
                        read_of(act, S, "score", s, g=g)
                        if s >= 3:
                            full_of(act, S, "turn", 2 * (s - 3) + 1, g=g)
                        act.activation(probs[:, s % 3, :, 0:SEQ], shifted[:, s % 2, :].rearrange("p (h n) -> p h n", n=SEQ),
                                       ACT.Exp).then_inc(exp_ready, 1)
                    if front and s in PATCH_STEPS:
                        for i in range(4 * s, 4 * s + 4):
                            patch(S, g, i)
                        if s + 1 < CH:
                            pixels(S, g, g + 1, s + 1)
                    if 2 <= s < PAIRS + 2:
                        for r in range(2):
                            i = 2 * (s - 2) + r
                            full_of(act, S, "turn", i, g=g)
                            emptied(act.activation(probsT[:, (s - 2) % 2, r, :], bank(S, "turn", i), ACT.Copy), S, "turn", i)
                    if s >= 3:
                        i = s - 3
                        full_of(act, S, "out", 2 * i + 1, g=g)
                        if i >= 2:
                            read_of(act, S, "out", 2 * (i - 2) + 1, g=g)
                        b = banks.bank(S, "out", 2 * i)
                        assert banks.bank(S, "out", 2 * i + 1) == b + 1
                        src = ps[:, b:b + 2, 0:2 * 2 * SEQ].rearrange("p j (m e c) -> p m j e c", m=DM, e=2)
                        act.activation(even[:, i % 2, :, :].rearrange("p m (j c) -> p m j c", j=2), src[:, :, :, 0, :], ACT.Copy, scale=con[:, C_PAR:C_PAR + 1]).then_inc(even_ready, 1)
                for i in range(2 * len(GLU)):
                    f = i % len(GLU)
                    if f == 0:
                        turned(S, "a2", a2T, g, S_G2, S_B2, BATCHES[i // len(GLU)])
                    full_of(act, S, "glu", i, g=g)
                    if i >= 4:
                        read_of(act, S, "up", i - 4, g=g)
                    act.activation(th[0:GLU[f], i % 4, :], bank(S, "glu", i)[0:GLU[f], 0:HALF], ACT.Tanh, scale=0.5).then_inc(th_ready, 1)
                if front:
                    tokens(S, g)
                for i in range(2 * FT):
                    f = i % FT
                    if f == 0:
                        turned(S, "y", yT, g, tiles=BATCHES[i // FT])
                    full_of(act, S, "gate", i, g=g)
                    if i >= 3:
                        act.wait_ge(hid_ready, g * 2 * FT + i - 2)
                    act.activation(ex[:, i % 3, :], bank(S, "gate", i)[:, 0:HALF], ACT.Exp, bias=gate_exp_bias[:, f:f + 1])
                    act.activation(lin[:, i % 3, :], bank(S, "gate", i)[:, 0:HALF], ACT.Relu, scale=LAMBDA,
                                   bias=gate_lin_bias[:, f:f + 1]).then_inc(free[banks.bank(S, "gate", i)], 1)
                if front:
                    project(S, g)

            act.wait_ge(setup_done, 2)
            for c in range(CH):
                pixels("first", 0, 0, c)
                for i in range(4 * c, 4 * c + 4):
                    patch("first", 0, i)
            tokens("first", 0)
            project("first", 0)
            with act.Fori(0, LAST) as g:
                back("loop", g, True)
            back("last", LAST, False)

            def body(c, i, before):
                E = "expert"
                for b in range(TURN):
                    full_of(act, E, "xT", b, g=before)
                    emptied(act.activation(xT[:, b % 2, :, :].rearrange("p m n -> p (m n)"), bank(E, "xT", b)[:, 0:DM * SLOTS], ACT.Copy), E, "xT", b)
                    read_of(act, E, "mid", b, g=before)
                    act.activation(ee, pre, ACT.Exp, bias=con[:, C_LNLA:C_LNLA + 1])
                    act.activation(el, pre, ACT.Relu, scale=LAMBDA).then_inc(pre_ready, 1)
            expert_passes(act, body)

        @block.gpsimd
        def _(pool):
            pool.memset(ones[:], 1.0).then_inc(const_ready, 1)
            pool.memset(zero_rows[:], 0.0).then_inc(const_ready, 1)
            pool.memset(probs[:], 0.0)
            pool.memset(probsT[:], 0.0)
            pool.memset(qT[:, :, GT:], 0.0)
            pool.memset(selcum[:], 0.0)
            pool.memset(minus_half[:], -0.5)
            pool.memset(v8[:], 1.0)
            pool.memset(i8[:], 0)
            pool.wait_ge(con_in, 16)
            pool.tensor_copy(ident_bf[:], ident)
            pool.tensor_copy(mask_bf[:], con[:, C_MASK:C_MASK + 8 * SEQ]).then_inc(setup_done, 1)
            pool.wait_ge(const_ready, 3)
            quarter = EXPERTS * CHUNKS // 4
            pool.dma_start(lists.rearrange("(q c s) o -> q c (s o)", s=SLOTS, c=4),
                           pad_row[0:quarter, :].rearrange("q (a s) -> q a s", a=1).to_broadcast([quarter, 4, SLOTS])).then_inc(list_out, 16)
            pad = SLOTS // TURN
            for b in range(TURN):
                pool.dma_start(out_rows[TOKENS + b * pad:TOKENS + (b + 1) * pad, :], zero_rows[0:pad, 0:D]).then_inc(added[b], 16)

            def inverse_deviation(which, g):
                for b, tiles in enumerate(BATCHES):
                    done = (g * 4 + which) * 2 + b + 1
                    own = slice(tiles[0], tiles[-1] + 1)
                    pool.wait_ge(var_ready, done)
                    alone(pool)
                    pool.tensor_scalar(var_eps[:, own], mv[:, own, 1], EPS, None, ALU.add).then_inc(pool_step, 1)
                    pool.wait_ge(pool_step, done)
                    pool.tensor_tensor(rstd[:, own], var_eps[:, own], minus_half[:, own], ALU.pow).then_inc(rstd_ready, 1)

            def project(S, g, f):
                for t in range(NT):
                    read_of(pool, S, "a1", t, g=g)
                alone(pool)
                pool.tensor_copy(a1P.rearrange("p m (i n) -> p m i n", n=PITCH)[:, :, :, 0:SEQ],
                                 a1T[:].rearrange("p m (i n) -> p m i n", n=SEQ)).then_inc(a1P_ready, 1)
                for t, (a, n) in enumerate(TILES):
                    read_of(pool, S, "qk", t, g=g)
                    pool.tensor_tensor(qk[0:n, t, :], qk[0:n, t, :], swapped[0:n, t % 2, :], ALU.add).then_inc(qk_ready, 1)

            def spread_keys(S, g, i):
                last_tile = min(NT - 1, ((i + 1) * 2 * SEQ - 1) // P)
                pool.wait_ge(kT_ready, g * NT + last_tile + 1)
                if i >= 2:
                    full_of(pool, S, "score", i - 2, g=g)
                for m in range(DM):
                    last = pool.tensor_tensor(
                        kx[:, i % 2, m, :, :],
                        kT[:, m:m + 1, i * 2 * SEQ:(i + 1) * 2 * SEQ].to_broadcast([P, 4, 2 * SEQ]),
                        con[:, C_HEAD:C_HEAD + 4].rearrange("p (h a) -> p h a", a=1).to_broadcast([P, 4, 2 * SEQ]), ALU.mult)
                last.then_inc(kx_ready, 1)

            def list_tile(t):
                n = TILES[t][1]
                for k in range(2):
                    pool.indirect_dma_start(out=lists, out_offset=bass.IndirectOffsetOnAxis(ap=dest[0:n, k, t:t + 1], axis=0),
                                            in_=tok[0:n, t:t + 1], in_offset=None, bounds_check=EXPERTS * TOKENS - 1,
                                            oob_is_err=False).then_inc(list_out, 16)

            def back(S, g, front):
                spread_keys(S, g, 0)
                for s in range(PAIRS):
                    if s + 1 < PAIRS:
                        spread_keys(S, g, s + 1)
                    pool.wait_ge(share_ready, g * PAIRS + s + 1)
                    pool.tensor_tensor(probs[:, s % 3, :, 0:SEQ], probs[:, s % 3, :, 0:SEQ],
                                       share[:, s % 2, :].rearrange("p (h a) -> p h a", a=1).to_broadcast([P, 16, SEQ]),
                                       ALU.mult).then_inc(probs_ready, 1)
                    if s == 2:
                        pool.wait_ge(dest_ready, g + 1)
                        alone(pool)
                        pool.wait_ge(list_out, PRIMED)
                    if 2 <= s < 2 + NT:
                        list_tile(s - 2)
                inverse_deviation(2, g)
                for t, (a, n) in enumerate(TILES):
                    read_of(pool, S, "wo", t, g=g)
                    pool.tensor_tensor(res[0:n, t, :], h0[0:n, t, :], h1[0:n, t, :], ALU.add).then_inc(res_ready, 1)
                inverse_deviation(3, g)
                if front:
                    inverse_deviation(4, g)
                    inverse_deviation(5, g)
                    project(S, g, g + 1)

            inverse_deviation(0, 0)
            inverse_deviation(1, 0)
            project("first", 0, 0)
            with pool.Fori(0, LAST) as g:
                back("loop", g, True)
            back("last", LAST, False)
            pool.wait_ge(dest_ready, GROUPS + 1)
            for t in range(NT):
                list_tile(t)

            pool.wait_ge(row_out, PRIMED + 16 * STORES * GROUPS)
            pool.wait_ge(h2_out, PRIMED + 16 * STORES * GROUPS)

            def body(c, i, before):
                E = "expert"
                for b in range(TURN):
                    pool.wait_ge(slots_in[b], 16 * (before + 1))
                    alone(pool)
                    pool.indirect_dma_start(out=xg[:, b, :], out_offset=None, in_=rows,
                                            in_offset=bass.IndirectOffsetOnAxis(ap=slot_tok[:, b:b + 1], axis=0)).then_inc(gathered[b], 16)
                for b in range(TURN):
                    read_of(pool, E, "down", b, g=before)
                    if b:
                        pool.wait_ge(added[b - 1], PRIMED + 16 * (before + 1))
                    else:
                        pool.wait_ge(added[TURN - 1], PRIMED + 16 * before)
                    alone(pool)
                    pool.indirect_dma_start(out=out_rows, out_offset=bass.IndirectOffsetOnAxis(ap=slot_tok[:, b:b + 1], axis=0),
                                            in_=ye[:, b % 2, :], in_offset=None, compute_op=ALU.add).then_inc(added[b], 16)
                for b in range(TURN):
                    pool.wait_ge(added[b], PRIMED + 16 * (before + 1))
            expert_passes(pool, body)

        @block.vector
        def _(dve):
            class Chain:
                def __init__(self, before):
                    self.before, self.n = before, 0

                def step(self, ins):
                    ins.then_inc(a_step, 1)
                    self.n += 1

                def wait(self):
                    dve.wait_ge(a_step, self.before + self.n)

            FIRST_STEPS, LOOP_STEPS = 5, 39

            def norm(which, dst, src, chain, ready, g, product=None):
                def statistics(t):
                    n = TILES[t][1]
                    return dve.bn_stats(stats[0:n, t, :], src[0:n, t, :])

                def variances(tiles):
                    for t in tiles:
                        if product is None:
                            last = statistics(t)
                            continue
                        product[0](t)
                        if t > tiles[0]:
                            product[1](t - 1)
                            statistics(t - 1)
                    if product is not None:
                        product[1](t)
                        last = statistics(t)
                    chain.step(last)
                    chain.wait()
                    alone(dve)
                    for t in tiles:
                        n = TILES[t][1]
                        last = dve.bn_aggr(mv[0:n, t, :], stats[0:n, t, :])
                    last.then_inc(var_ready, 1)

                for b, tiles in enumerate(BATCHES):
                    if product is None:
                        if b == 0:
                            variances(BATCHES[0])
                            variances(BATCHES[1])
                    else:
                        variances(tiles)
                    dve.wait_ge(rstd_ready, (g * 4 + which) * 2 + b + 1)
                    for t in tiles:
                        n = TILES[t][1]
                        ins = dve.tensor_scalar(dst[0:n, t, 0:D], src[0:n, t, :], mv[0:n, t, 0:1], rstd[0:n, t:t + 1], ALU.subtract, ALU.mult)
                        if ready is not None:
                            ins.then_inc(ready, 1)
                if ready is None:
                    chain.step(ins)
                    chain.wait()

            dve.memset(mv[:], 1.0)
            dve.memset(tok[:], 0)
            dve.memset(dest[:], EXPERTS * TOKENS).then_inc(dest_ready, 1)
            dve.wait_ge(con_in, 16)
            dve.tensor_copy(tokf[:], con[:, C_TOK:C_TOK + NT])
            dve.tensor_copy(pad_row[:], con[:, C_PAD:C_PAD + SLOTS]).then_inc(const_ready, 1)
            full_of(dve, "setup", "small", 0)
            dve.tensor_copy(small[:, 0:S_ROWS], bank("setup", "small", 0)[:, 0:S_ROWS]).then_inc(free[banks.bank("setup", "small", 0)], 1)
            read_of(dve, "setup", "small", 0)
            dve.tensor_scalar(gate_exp_bias[:], small[:, S_GB:S_GB + FT], con[:, C_LNLA:C_LNLA + 1], None, ALU.add)
            dve.tensor_scalar(gate_lin_bias[:], small[:, S_GB:S_GB + FT], LAMBDA, None, ALU.mult)
            full_of(dve, "setup", "posT", 0)
            for m in range(DM):
                src = bank("setup", "posT", 0)[:, m * SEQ:(m + 1) * SEQ]
                dve.tensor_scalar(posT[:, m, 1:SEQ], src[:, 1:SEQ], small[:, S_TB + m:S_TB + m + 1], None, ALU.add)
                last = dve.tensor_scalar(posT[:, m, 0:1], src[:, 0:1], small[:, S_CLS + m:S_CLS + m + 1], None, ALU.add)
            emptied(last, "setup", "posT", 0)
            read_of(dve, "setup", "wt", PK - 1)
            dve.memset(patT.rearrange("p k (b s) -> p k b s", s=SEQ)[:, :, :, 0], 0.0).then_inc(setup_done, 1)

            def embed(S, g, i):
                n, m = i // DM, i % DM
                full_of(dve, S, "embed", i, g=g)
                dst = h0T[:, m, n * HALF:(n + 1) * HALF].rearrange("p (b s) -> p b s", s=SEQ)
                src = bank(S, "embed", i)[:, 0:HALF].rearrange("p (b s) -> p b s", s=SEQ)
                dve.tensor_copy(dst[:, :, 0:1], posT[:, m:m + 1, 0:1].to_broadcast([P, GI // 2, 1]))
                emptied(dve.tensor_tensor(dst[:, :, 1:SEQ], src[:, :, 1:SEQ],
                                          posT[:, m:m + 1, 1:SEQ].to_broadcast([P, GI // 2, SEQ - 1]), ALU.add), S, "embed", i)

            def rotate(S, g, f):
                for t, (a, n) in enumerate(TILES):
                    full_of(dve, S, "qk", t, g=g)
                    if t >= 2:
                        dve.wait_ge(qk_ready, f * NT + t - 1)
                    src = bank(S, "qk", t)[0:n, :].rearrange("p (h c) -> p h c", c=HD)
                    heads = 2 * HEADS

                    def table(at):
                        return con[0:n, at + t * HD:at + (t + 1) * HD].rearrange("p (a c) -> p a c", a=1)
                    dve.tensor_tensor(qk[0:n, t, :].rearrange("p (h c) -> p h c", c=HD), src, table(C_COS).to_broadcast([n, heads, HD]), ALU.mult)
                    for e in range(2):
                        ins = dve.tensor_tensor(swapped[0:n, t % 2, :].rearrange("p (h c) -> p h c", c=HD)[:, :, e::2], src[:, :, 1 - e::2],
                                                table(C_SIN)[:, :, e::2].to_broadcast([n, heads, HD // 2]), ALU.mult)
                    emptied(ins, S, "qk", t)

            def hidden(S, g, half):
                for i in range(half * FT, (half + 1) * FT):
                    n, f = i // FT, i % FT
                    read_of(dve, S, "gate", i, g=g)
                    dve.scalar_tensor_tensor(hidT[:, f, n * HALF:(n + 1) * HALF], ex[:, i % 3, :], LA, lin[:, i % 3, :], ALU.subtract, ALU.min).then_inc(hid_ready, 1)

            def back(S, g, front):
                ch = Chain(FIRST_STEPS + g * LOOP_STEPS)
                for s in range(PAIRS + 3):
                    if s < PAIRS:
                        full_of(dve, S, "score", s, g=g)
                        b = banks.bank(S, "score", s)
                        src = ps[:, b:b + 2, 0:8 * SEQ].rearrange("p r (h n) -> p r h n", n=SEQ)
                        mx = top[:, s % 2, :].rearrange("p (r h) -> p r h", r=2)
                        ch.step(dve.tensor_reduce(mx, src, AX.X, ALU.max))
                        ch.wait()
                        emptied(dve.tensor_tensor(shifted[:, s % 2, :].rearrange("p (r h n) -> p r h n", r=2, n=SEQ), src,
                                                  mx.rearrange("p r (h a) -> p r h a", a=1).to_broadcast([P, 2, 8, SEQ]), ALU.subtract),
                                S, "score", s)
                        dve.wait_ge(exp_ready, g * PAIRS + s + 1)
                        ch.step(dve.tensor_reduce(total[:, s % 2, :], probs[:, s % 3, :, 0:SEQ], AX.X, ALU.add))
                        ch.wait()
                        dve.reciprocal(share[:, s % 2, :], total[:, s % 2, :]).then_inc(share_ready, 1)
                    if front and s in EMBED_STEPS:
                        embed(S, g, EMBED_STEPS.index(s))
                    if s >= 3:
                        i = s - 3
                        dve.wait_ge(even_ready, g * PAIRS + i + 1)
                        for j in range(2):
                            src = bank(S, "out", 2 * i + j)[:, 0:2 * 2 * SEQ].rearrange("p (m e c) -> p m e c", m=DM, e=2)
                            a = (2 * i + j) * SEQ
                            emptied(dve.scalar_tensor_tensor(attnT[:, :, a:a + SEQ], src[:, :, 1, :], con[:, C_PAR + 1:C_PAR + 2],
                                                             even[:, i % 2, :, j * SEQ:(j + 1) * SEQ], ALU.mult, ALU.add), S, "out", 2 * i + j)
                def attention_sum(t):
                    n = TILES[t][1]
                    full_of(dve, S, "wo", t, g=g)
                    emptied(dve.tensor_tensor(h1[0:n, t, :], bank(S, "wo", t)[0:n, 0:D], u[0:n, t, :], ALU.add), S, "wo", t)
                norm(2, z, h1, ch, z2_ready, g, (attention_sum, lambda t: read_of(dve, S, "wo", t, g=g)))
                if front:
                    for i in range(len(EMBED_STEPS), 2 * DM):
                        embed(S, g, i)
                for i in range(2 * len(GLU)):
                    n, f = i // len(GLU), i % len(GLU)
                    h = GLU[f]
                    dve.wait_ge(th_ready, g * 2 * len(GLU) + i + 1)
                    full_of(dve, S, "up", i, g=g)
                    emptied(dve.scalar_tensor_tensor(th[0:h, i % 4, :], th[0:h, i % 4, :], 1.0, bank(S, "glu", i)[0:h, 0:HALF], ALU.add, ALU.mult), S, "glu", i)
                    read_of(dve, S, "glu", i, g=g)
                    emptied(dve.scalar_tensor_tensor(gT[0:h, f, n * HALF:(n + 1) * HALF], th[0:h, i % 4, :], 0.5, bank(S, "up", i)[0:h, 0:HALF], ALU.mult, ALU.mult), S, "up", i)
                dve.wait_ge(h2_out, PRIMED + g * STORES * 16)
                dve.wait_ge(row_out, PRIMED + g * STORES * 16)

                def unit_sum(t):
                    n = TILES[t][1]
                    dve.wait_ge(res_ready, g * NT + t + 1)
                    full_of(dve, S, "w2", t, g=g)
                    emptied(dve.tensor_tensor(H2[0:n, t, :], bank(S, "w2", t)[0:n, 0:D], res[0:n, t, :], ALU.add), S, "w2", t)
                norm(3, y, H2, ch, y_ready, g, (unit_sum, lambda t: read_of(dve, S, "w2", t, g=g)))
                if front:
                    for t in range(NT):
                        read_of(dve, S, "token", t, g=g)
                    norm(4, u, h0, ch, None, g)
                hidden(S, g, 0)
                if front:
                    norm(5, z, u, ch, z1_ready, g)
                hidden(S, g, 1)
                for t, (a, n) in enumerate(TILES):
                    full_of(dve, S, "logit", t, g=g)
                    emptied(dve.tensor_tensor(logits[0:n, t % 2, :], bank(S, "logit", t)[0:n, 0:D], gbo_s[0:n, :], ALU.add), S, "logit", t)
                    read_of(dve, S, "logit", t, g=g)
                    alone(dve)
                    ch.step(dve.max(v8[0:n, t, :], logits[0:n, t % 2, :]))
                    ch.wait()
                    alone(dve)
                    ins = dve.max_index(i8[0:n, t, :], v8[0:n, t, :], logits[0:n, t % 2, :])
                ch.step(ins)
                ch.wait()
                if front:
                    rotate(S, g, g + 1)
                dve.tensor_copy(idxf[:].rearrange("p k t -> p t k"), i8[:, :, 0:2])
                ch.step(dve.tensor_tensor(vsum[:], v8[:, :, 0:1], v8[:, :, 1:2], ALU.add))
                ch.wait()
                ch.step(dve.reciprocal(vinv[:], vsum[:]))
                iota = con[:, C_IOTA:C_IOTA + NT * EXPERTS].rearrange("p (t e) -> p t e", e=EXPERTS)
                for k in range(2):
                    ins = dve.tensor_tensor(pick[:, k, :, :], iota, idxf[:, k, :].rearrange("p (t a) -> p t a", a=1).to_broadcast([P, NT, EXPERTS]), ALU.is_equal)
                ch.step(ins)
                ch.wait()
                ch.step(dve.tensor_tensor(wts[:], v8[:, :, 0:2], vinv[:].to_broadcast([P, NT, 2]), ALU.mult))
                dve.tensor_tensor(sel[:], pick[:, 0, :, :], pick[:, 1, :, :], ALU.add).then_inc(sel_ready, 1)
                ch.wait()
                for k in range(2):
                    ins = dve.tensor_tensor(part[:, k, :, :], pick[:, k, :, :], wts[:, :, k:k + 1].to_broadcast([P, NT, EXPERTS]), ALU.mult)
                ch.step(ins)
                ch.wait()
                dve.tensor_tensor(y[:, :, D:ROW], part[:, 0, :, :], part[:, 1, :, :], ALU.add).then_inc(weights_ready, 1)
                dve.wait_ge(weights_ready, g + 1)
                full_of(dve, S, "pos", 0, g=g)
                before = bank(S, "pos", 0)[:, 0:NT * EXPERTS].rearrange("p (t e) -> p t e", e=EXPERTS)
                for k in range(2):
                    ins = dve.tensor_tensor(part[:, k, :, :], pick[:, k, :, :], before, ALU.mult)
                emptied(ins, S, "pos", 0)
                read_of(dve, S, "pos", 0, g=g)
                ch.step(dve.tensor_reduce(place[:], part[:], AX.X, ALU.add))
                ch.step(dve.tensor_reduce(selsum[:], sel[:].rearrange("p t e -> p e t"), AX.X, ALU.add))
                ch.wait()
                dve.wait_ge(list_out, PRIMED + (g + 1) * 2 * NT * 16)
                dve.tensor_tensor(selcum[:], selcum[:], selsum[:], ALU.add)
                dve.tensor_copy(tok[:], tokf[:])
                ch.step(dve.scalar_tensor_tensor(dest[:], idxf[:], float(TOKENS), place[:], ALU.mult, ALU.add))
                ch.wait()
                dve.tensor_scalar(tokf[:], tokf[:], float(GT), None, ALU.add).then_inc(dest_ready, 1)
                assert not front or ch.n == LOOP_STEPS, ch.n

            for i in range(2 * DM):
                embed("first", 0, i)
            for t in range(NT):
                read_of(dve, "first", "token", t)
            ch = Chain(0)
            norm(0, u, h0, ch, None, 0)
            norm(1, z, u, ch, z1_ready, 0)
            assert ch.n == FIRST_STEPS, ch.n
            rotate("first", 0, 0)
            with dve.Fori(0, LAST) as g:
                back("loop", g, True)
            back("last", LAST, False)

            full_of(dve, "count", "all", 0)
            dve.tensor_reduce(most[:], bank("count", "all", 0)[:, 0:EXPERTS], AX.X, ALU.max).then_inc(free[banks.bank("count", "all", 0)], 1)
            read_of(dve, "count", "all", 0)
            dve.tensor_scalar(flag_u[:], most[:], float(SLOTS), None, ALU.is_gt).then_inc(flag_ready, 1)

            def body(c, i, before):
                E = "expert"
                for b in range(TURN):
                    full_of(dve, E, "mid", b, g=before)
                    bias = small[:, bass.ds(i * (TURN * FT) + S_EB + b * FT, FT)].rearrange("p (f a) -> p f a", a=1)
                    emptied(dve.tensor_tensor(pre, bank(E, "mid", b)[:, 0:FT * SLOTS].rearrange("p (f n) -> p f n", f=FT),
                                              bias.to_broadcast([P, FT, SLOTS]), ALU.add), E, "mid", b)
                    dve.wait_ge(pre_ready, before * TURN + b + 1)
                    dve.scalar_tensor_tensor(ehT[:, b % 2, :, :], ee, LA, el, ALU.subtract, ALU.min).then_inc(act_ready, 1)
                    full_of(dve, E, "down", b, g=before)
                    if b >= 2:
                        dve.wait_ge(added[b - 2], PRIMED + 16 * (before + 1))
                    else:
                        dve.wait_ge(added[b + 2], PRIMED + 16 * before)
                    emptied(dve.tensor_scalar(ye[:, b % 2, :], bank(E, "down", b)[0:SLOTS, 0:D],
                                              xg[:, b, bass.ds(i * TURN + D + b, 1)], None, ALU.mult), E, "down", b)
            expert_passes(dve, body)


_INS = ['x', 'L0_tok_W', 'L0_tok_b', 'L0_tok_cls_token', 'L0_tok_pos_enc', 'L0_attn_wq', 'L0_attn_wk', 'L0_attn_wv', 'L0_attn_wo',
        'L0_attn_w1', 'L0_attn_w2', 'L0_attn_w3', 'L0_attn_ln1_g', 'L0_attn_ln1_b', 'L0_attn_ln2_g', 'L0_attn_ln2_b',
        'L0_ffn_gate_wi', 'L0_ffn_gate_bi', 'L0_ffn_gate_wo', 'L0_ffn_gate_bo', 'L0_ffn_exp_wi', 'L0_ffn_exp_bi', 'L0_ffn_exp_wo', 'L0_ffn_exp_bo']


def kernel(**inputs):
    import numpy as _np
    import concourse.bacc as _bacc
    from concourse import mybir as _mybir
    from concourse.bass_utils import run_bass_kernel_spmd as _run

    nc = _bacc.Bacc("TRN2", target_bir_lowering=False, num_devices=1)
    arrays, args = {}, []
    for name in _INS:
        a = _np.ascontiguousarray(inputs[name])
        arrays[f"in_{name}"] = a
        args.append(nc.dram_tensor(f"in_{name}", a.shape, _mybir.dt.from_np(a.dtype), kind="ExternalInput").ap())
    arrays["const"] = constants()
    args.append(nc.dram_tensor("const", arrays["const"].shape, F32, kind="ExternalInput").ap())
    args.append(nc.dram_tensor("out_0", (TOKENS + SLOTS, D), F32, kind="ExternalOutput").ap())
    build(nc, *args)
    r = _run(nc, [arrays], core_ids=[0])
    return r.results[0]["out_0"][:TOKENS].reshape(IMAGES, SEQ, D)
```

```python
from contextlib import ExitStack

import concourse.bass as bass
from concourse import mybir
import numpy as np

F32 = mybir.dt.float32
BF16 = mybir.dt.bfloat16
U32 = mybir.dt.uint32
ALU = mybir.AluOpType
ACT = mybir.ActivationFunctionType
AX = mybir.AxisListType

P = 128
IMAGES, CH, SIDE, PATCH = 64, 3, 96, 16
GRID = SIDE // PATCH
SEQ = GRID * GRID + 1
D = 256
DM = D // P
HEADS, HD = 16, 16
HIDDEN = 704
GLU = [min(P, HIDDEN - P * i) for i in range((HIDDEN + P - 1) // P)]
EXPERTS, FF = 8, 1024
FT = FF // P
PK = CH * PATCH * PATCH // P

GROUPS = 4
GI = IMAGES // GROUPS
GT = GI * SEQ
HALF = GT // 2
TILES = [(a, min(P, GT - a)) for a in range(0, GT, P)]
NT = len(TILES)
BATCHES = (range(0, 3), range(3, NT))
PAIRS = GI // 2
PITCH = 64
TOKENS = IMAGES * SEQ
SLOTS = 64
EBUFS = 4
CHUNKS = TOKENS // SLOTS
ROW = D + EXPERTS
LAMBDA, ALPHA = 1.0507009873554805, 1.6732632423543772
LA = LAMBDA * ALPHA
EPS = 1e-5
NEG = -1.0e30
STORES = 2
PRIMED = 16

C_ID, C_TRI, C_MASK = 0, P, 2 * P
C_COS = C_MASK + 8 * SEQ
C_SIN = C_COS + NT * HD
C_IOTA = C_SIN + NT * HD
C_TOK = C_IOTA + NT * EXPERTS
C_HEAD = C_TOK + NT
C_PAR = C_HEAD + 4
C_PAD = C_PAR + 2
C_LNLA = C_PAD + SLOTS
C_ALL = C_LNLA + 1


def constants():
    c = np.zeros((P, C_ALL), np.float32)
    p = np.arange(P)
    c[:, C_ID:C_ID + P] = np.eye(P)
    c[:, C_TRI:C_TRI + P] = p[:, None] < p[None, :]
    key = np.tile(np.arange(SEQ), 8)
    c[:, C_MASK:C_MASK + 8 * SEQ] = np.where(key[None, :] <= (p % PITCH)[:, None], 0.0, NEG)
    freqs = (np.float32(1.0) / np.float32(10000.0) ** (np.arange(0, HD, 2, dtype=np.float32) / np.float32(HD))).astype(np.float32)
    for t, (a, n) in enumerate(TILES):
        ang = (((a + p) % SEQ).astype(np.float32)[:, None] * freqs[None, :]).astype(np.float32)
        c[:, C_COS + t * HD:C_COS + (t + 1) * HD] = np.repeat(np.cos(ang), 2, axis=1)
        s = np.repeat(np.sin(ang), 2, axis=1)
        s[:, 0::2] *= -1
        c[:, C_SIN + t * HD:C_SIN + (t + 1) * HD] = s
        c[:, C_IOTA + t * EXPERTS:C_IOTA + (t + 1) * EXPERTS] = np.where(p[:, None] < n, np.arange(EXPERTS)[None, :], -1)
        c[:, C_TOK + t] = a + p
    for j in range(4):
        c[:, C_HEAD + j] = (p // HD) % 4 == j
    for j in range(2):
        c[:, C_PAR + j] = (p // HD) % 2 == j
    c[:, C_PAD:C_PAD + SLOTS] = TOKENS + np.arange(SLOTS)[None, :]
    c[:, C_LNLA] = np.log(LA)
    return c


DENSE = [0, 1, 2, 3]
SCORE = [4, 6]


VALUE_STEPS = (-1, 0)
EARLY_VALUES = PAIRS // 2 - len(VALUE_STEPS)
PATCH_STEPS = range(-1, CH - 1)
EMBED_STEPS = (3, 5, 7)


def attention_steps(front):
    for s in range(-1, PAIRS + 3):
        if 0 <= s < PAIRS:
            yield ("score", s)
        if s in VALUE_STEPS:
            yield ("v", EARLY_VALUES + VALUE_STEPS.index(s))
        if front and s in PATCH_STEPS:
            for i in range(4 * (s + 1), 4 * (s + 2)):
                yield ("patch", i)
        if front and s in EMBED_STEPS:
            yield ("embed", EMBED_STEPS.index(s))
        if 2 <= s < PAIRS + 2:
            yield ("turn", 2 * (s - 2))
            yield ("turn", 2 * (s - 2) + 1)
        if s >= 3:
            yield ("out", 2 * (s - 3))
            yield ("out", 2 * (s - 3) + 1)


def each_tile(kind):
    return [(kind, t) for t in range(NT)]


def sum_steps(front):
    for t in range(NT):
        if t == NT - 1:
            for turned in BATCHES[0]:
                yield ("a2", turned)
        yield ("wo", t)
        if front and t == BATCHES[0][-1]:
            for i in range(len(EMBED_STEPS), 2 * DM):
                yield ("embed", i)


def back_jobs(front):
    def halves(turned, kinds, per):
        return [j for n in range(2) for j in [(turned, t) for t in BATCHES[n]] + [(k, n * per + f) for f in range(per) for k in kinds]]
    return (
        list(attention_steps(front)) + list(sum_steps(front)) + halves("a2", ("glu", "up"), len(GLU))[len(BATCHES[0]):] + each_tile("w2") + each_tile("token") * front + halves("y", ("gate",), FT) + each_tile("logit")
        + (each_tile("a1") + each_tile("qk") + [("v", i) for i in range(EARLY_VALUES)]) * front + [("pos", 0)] + each_tile("qkT") * front
    )


FIRST_JOBS = (
    [("patch", i) for i in range(2 * PK)] + [("embed", i) for i in range(2 * DM)] + each_tile("token") + each_tile("a1") + each_tile("qk")
    + [("v", i) for i in range(EARLY_VALUES)] + each_tile("qkT")
)
def expert_steps():
    yield from (("xT", 0), ("xT", 1), ("mid", 0), ("mid", 1), ("hid", 0))
    for e in range(EXPERTS):
        if e + 2 < EXPERTS:
            yield ("xT", e + 2)
        if e + 1 < EXPERTS:
            yield ("mid", 2 * e + 2)
            yield ("mid", 2 * e + 3)
        yield ("down", e)
        if e + 1 < EXPERTS:
            yield ("hid", e + 1)


SETUP_JOBS = [("wt", i) for i in range(PK)] + [("small", 0), ("posT", 0)]


class Banks:

    def __init__(self):
        self.uses = [0] * 8
        self.jobs = {}
        self.turn = 0
        self.scores = 0
        self.section("setup", SETUP_JOBS, 1)
        self.section("first", FIRST_JOBS, 1)
        self.section("loop", back_jobs(True), GROUPS - 1)
        self.section("last", back_jobs(False), 1)
        self.section("count", [("all", 0)], 1)
        self.section("expert", list(expert_steps()), 0)

    def section(self, name, jobs, times):
        base, count = list(self.uses), [0] * 8
        placed = {}
        for job in jobs:
            if job[0] in ("score", "small", "posT"):
                bank = SCORE[self.scores % 2]
                self.scores += 1
            else:
                if job[0] == "out" and job[1] % 2 == 0:
                    self.turn += self.turn % 2
                bank = self.turn % 8 if name == "expert" else DENSE[self.turn % len(DENSE)]
                self.turn += 1
            placed[job] = (bank, count[bank])
            count[bank] += 1
        for job, (bank, before) in placed.items():
            self.jobs[(name,) + job] = (bank, base[bank] + before, count[bank])
        self.uses = [u + times * c for u, c in zip(base, count)]

    def bank(self, name, *job):
        return self.jobs[(name,) + job][0]

    def vacant(self, name, *job, g=0):
        bank, before, per = self.jobs[(name,) + job]
        return g * per + before

    def filled(self, name, *job, g=0):
        return self.vacant(name, *job, g=g) + 1

    emptied = filled


def build(nc, x, tok_W, tok_b, cls_token, pos_enc, wq, wk, wv, wo, w1, w2, w3, ln1_g, ln1_b, ln2_g, ln2_b,
          gate_wi, gate_bi, gate_wo, gate_bo, exp_wi, exp_bi, exp_wo, exp_bo, const, out):
    banks = Banks()
    ctx = ExitStack()
    with ctx:
        def sb(name, shape, dt=F32):
            return ctx.enter_context(nc.sbuf_tensor(name, shape, dt))

        def sem(name):
            return ctx.enter_context(nc.semaphore(name))

        rows = nc.dram_tensor("token_rows", [TOKENS + SLOTS, ROW], F32, kind="Internal").ap()
        lists = nc.dram_tensor("expert_lists", [EXPERTS * TOKENS, 1], U32, kind="Internal").ap()

        con = sb("con", [P, C_ALL])
        ident = con[:, C_ID:C_ID + P]
        tri = con[:, C_TRI:C_TRI + P]
        ident_bf = sb("ident_bf", [P, P], BF16)
        mask_bf = sb("mask_bf", [P, 8 * SEQ], BF16)
        ones = sb("ones", [P, P])
        small_rows = sb("small_rows", [P, P])
        small = sb("small", [P, P])
        WT = sb("WT", [P, PK, D])
        posT = sb("posT", [P, DM, SEQ])
        wqk_s = sb("wqk_s", [P, DM, 2 * D])
        wv_s = sb("wv_s", [P, DM, D])
        wo_s = sb("wo_s", [P, DM, D])
        glu_area = sb("glu_area", [P, 2 * DM * HIDDEN + len(GLU) * D])
        w1_s, w3_s = (glu_area[:, i * DM * HIDDEN:(i + 1) * DM * HIDDEN].rearrange("p (k n) -> p k n", k=DM) for i in range(2))
        w2_s = glu_area[:, 2 * DM * HIDDEN:].rearrange("p (f n) -> p f n", n=D)
        gate_area = sb("gate_area", [P, DM * FF + FT * D])
        gwi_s = gate_area[:, 0:DM * FF].rearrange("p (k n) -> p k n", k=DM)
        gwo_s = gate_area[:, DM * FF:].rearrange("p (f n) -> p f n", f=FT)
        gbo_s = sb("gbo_s", [P, D])
        S_TB, S_CLS, S_G1, S_B1, S_G2, S_B2 = 0, 2, 4, 6, 8, 10
        S_GB = 12
        S_EB = S_GB + FT
        S_ROWS = S_EB + EXPERTS * FT
        gate_exp_bias = sb("gate_exp_bias", [P, FT])
        gate_lin_bias = sb("gate_lin_bias", [P, FT])

        XC = PATCH * SIDE
        EW = DM * FF
        VN, KN = PAIRS * D, 2 * DM * 4 * 2 * SEQ
        arena = sb("arena", [P, 2 * XC + VN + KN])
        xin = arena[:, 0:2 * XC].rearrange("p (c n) -> p c n", c=2)
        xin2 = arena[:, 2 * XC:3 * XC]
        V = arena[:, 2 * XC:2 * XC + VN].rearrange("p (i n) -> p i n", i=PAIRS)
        kx = arena[:, 2 * XC + VN:].rearrange("p (b m h n) -> p b m h n", b=2, m=DM, h=4)
        xp = sb("xp", [P, 2, GRID, P])
        hidT = sb("hidT", [P, FT, GT])
        gT = hidT[:, 0:len(GLU), :]
        patT = hidT[:, 0:PK, :]
        h0T = sb("h0T", [P, DM, GT])
        h0 = sb("h0", [P, NT, D])
        u = sb("u", [P, NT, D])
        z = sb("z", [P, NT, D])
        stats = sb("stats", [P, NT, 6])
        mv = sb("mv", [P, NT, 2])
        rstd = sb("rstd", [P, NT])
        var_eps = sb("var_eps", [P, NT])
        minus_half = sb("minus_half", [P, NT])
        a1T = sb("a1T", [P, DM, GT])
        qk = sb("qk", [P, NT, 2 * D])
        swapped = sb("swapped", [P, 2, 2 * D])
        qT = sb("qT", [P, DM, GT + PITCH - SEQ])
        kT = sb("kT", [P, DM, GT])
        top = sb("top", [P, 2, 16])
        total = sb("total", [P, 2, 16])
        share = sb("share", [P, 2, 16])
        shifted = sb("shifted", [P, 2, 16 * SEQ])
        probs = sb("probs", [P, 3, 16, PITCH])
        probsT = sb("probsT", [P, 2, 2, 4 * P])
        a1P = probsT[:].rearrange("p b r n -> p (b r n)").rearrange("p (m n) -> p m n", m=DM)
        even = sb("even", [P, 2, DM, 2 * SEQ])
        attnT = sb("attnT", [P, DM, GT])
        h1 = u
        res = h0
        a2T = a1T
        th = sb("th", [P, 4, HALF])
        H2 = sb("H2", [P, NT, D])
        y = sb("y", [P, NT, ROW])
        yT = a1T
        qk_area = qk[:].rearrange("p t n -> p (t n)")
        ex, lin = (qk_area[:, i * 3 * HALF:(i + 1) * 3 * HALF].rearrange("p (b n) -> p b n", b=3) for i in range(2))
        logits = sb("logits", [P, 2, D])
        v8 = sb("v8", [P, NT, 8])
        i8 = sb("i8", [P, NT, 8], U32)
        idxf = sb("idxf", [P, 2, NT])
        vsum = sb("vsum", [P, NT, 1])
        vinv = sb("vinv", [P, NT, 1])
        wts = sb("wts", [P, NT, 2])
        pick = sb("pick", [P, 2, NT, EXPERTS])
        sel = sb("sel", [P, NT, EXPERTS])
        selcum = sb("selcum", [P, EXPERTS])
        selsum = sb("selsum", [P, EXPERTS])
        part = sb("part", [P, 2, NT, EXPERTS])
        place = sb("place", [P, 2, NT])
        dest = sb("dest", [P, 2, NT], U32)
        tokf = sb("tokf", [P, NT])
        tok = sb("tok", [P, NT], U32)
        hid_area = hidT[:].rearrange("p f n -> p (f n)")
        expert_areas = (arena, glu_area, hid_area, gate_area)
        ewi = [a[:, 0:EW].rearrange("p (k n) -> p k n", k=DM) for a in expert_areas]
        ewo = [a[:, EW:2 * EW].rearrange("p (f n) -> p f n", f=FT) for a in expert_areas]
        most = sb("most", [P, 1])
        flag_u = sb("flag_u", [P, 1], U32)
        slot_tok = sb("slot_tok", [SLOTS, EXPERTS], U32)
        pad_row = sb("pad_row", [P, SLOTS], U32)
        zero_rows = sb("zero_rows", [SLOTS, ROW])
        xg = probs[:].rearrange("p a h n -> p (a h n)")[0:SLOTS, 0:EXPERTS * ROW].rearrange("p (b n) -> p b n", b=EXPERTS)
        turned = swapped[:].rearrange("p a n -> p (a n)")
        xT = turned[:, 0:2 * DM * SLOTS].rearrange("p (b m n) -> p b m n", b=2, m=DM)
        ye = turned[0:SLOTS, 2 * DM * SLOTS:2 * DM * SLOTS + 2 * D].rearrange("p (b n) -> p b n", b=2)
        raw = th[:].rearrange("p b n -> p (b n)")[0:SLOTS, 0:FF]
        ebo = probsT[:].rearrange("p a r n -> p (a r n)")[0:1, :].rearrange("p (e n) -> p e n", e=EXPERTS)
        pre, ee, el = (qk[:, i, :].rearrange("p (f n) -> p f n", f=FT) for i in range(3))
        ehT = qk[:, 3:5, :].rearrange("p b (f n) -> p b f n", f=FT)
        ps = ctx.enter_context(nc.psum_tensor("ps", [P, 8, 512], F32))

        full = [sem(f"bank_filled{b}") for b in range(8)]
        free = [sem(f"bank_emptied{b}") for b in range(8)]
        waits_passed = sem("waits_passed")
        con_in = sem("con_in")
        weight_in = sem("weight_in")
        tokw_in = sem("tokw_in")
        small_in = sem("small_in")
        x_in = [sem(f"x_in{c}") for c in range(CH)]
        const_ready = sem("const_ready")
        setup_done = sem("setup_done")
        vector_step = sem("vector_step")
        xp_ready = sem("xp_ready")
        var_ready = sem("var_ready")
        pool_step = sem("pool_step")
        rstd_ready = sem("rstd_ready")
        a1P_ready = sem("a1P_ready")
        z1_ready = sem("z1_ready")
        z2_ready = sem("z2_ready")
        y_ready = sem("y_ready")
        qk_ready = sem("qk_ready")
        kx_ready = sem("kx_ready")
        kT_ready = sem("kT_ready")
        exp_ready = sem("exp_ready")
        share_ready = sem("share_ready")
        probs_ready = sem("probs_ready")
        even_ready = sem("even_ready")
        res_ready = sem("res_ready")
        th_ready = sem("th_ready")
        hid_ready = sem("hid_ready")
        sel_ready = sem("sel_ready")
        weights_ready = sem("weights_ready")
        dest_ready = sem("dest_ready")
        h2_out = sem("h2_stored")
        row_out = sem("row_stored")
        list_out = sem("list_stored")
        flag_ready = sem("flag_ready")
        slots_in = sem("slots_in")
        gathered = [sem(f"rows_gathered{e}") for e in range(EXPERTS)]
        ew_in = [sem(f"expert_weights_in{b}") for b in range(EBUFS)]
        ebo_in = sem("expert_biases_in")
        pre_ready = sem("expert_pre_ready")
        act_ready = sem("expert_act_ready")
        added = [sem(f"expert_rows_added{e}") for e in range(EXPERTS)]

        def bank(*job):
            return ps[:, banks.bank(*job), :]

        def turns_of(job, g):
            return g if job[0] in ("loop", "expert") else 0

        def full_of(eng, *job, g=0):
            eng.wait_ge(full[banks.bank(*job)], banks.filled(*job, g=turns_of(job, g)))

        def read_of(eng, *job, g=0):
            eng.wait_ge(free[banks.bank(*job)], banks.emptied(*job, g=turns_of(job, g)))

        def all_read(eng, S, kind, indices, g=0):
            last = {banks.bank(S, kind, i): i for i in indices}
            alone(eng)
            for i in last.values():
                read_of(eng, S, kind, i, g=g)

        def vacant_for(eng, *job, g=0):
            eng.wait_ge(free[banks.bank(*job)], banks.vacant(*job, g=turns_of(job, g)))

        def alone(eng):
            eng.sem_inc(waits_passed, 1)

        def filled(ins, *job):
            ins.then_inc(full[banks.bank(*job)], 1)

        def emptied(ins, *job):
            ins.then_inc(free[banks.bank(*job)], 1)

        def expert_passes(eng, body):
            body(0)
            eng.wait_ge(flag_ready, 1)
            more = eng.value_load(flag_u[0:1, 0:1], min_val=0, max_val=1)
            with eng.If(more > 0):
                with eng.Fori(1, CHUNKS) as c:
                    body(c)

        E = "expert"
        LAST = GROUPS - 1

        x_rows = x.rearrange("b c (n r) w -> c b n (r w)", r=PATCH)

        block = ctx.enter_context(nc.Block())

        def store(eng, dst, src, g, done):
            whole = NT - 1
            a, n = TILES[whole]
            eng.dma_start(dst[bass.ds(g * GT, whole * P), :].rearrange("(t p) d -> p t d", p=P), src[:, 0:whole, :]).then_inc(done, 16)
            eng.dma_start(dst[bass.ds(g * GT + a, n), :], src[0:n, whole, :]).then_inc(done, 16)

        @block.sync
        def _(sp):
            sp.dma_start(con[:], const).then_inc(con_in, 16)
            sp.sem_inc(h2_out, PRIMED)
            wnat = patT.rearrange("p k n -> p (k n)")[:, 0:DM * PK * P].rearrange("p (m f) -> p m f", m=DM)
            sp.dma_start(wnat, tok_W.rearrange("(m p) f -> p m f", p=P)).then_inc(tokw_in, 16)
            for c, place in enumerate((xin[:, 0, :], xin[:, 1, :], xin2)):
                sp.dma_start(place[0:GI * GRID, :], x_rows[c, 0:GI]).then_inc(x_in[c], 16)
            pos_nat = h0[0:SEQ, 0, :]
            sp.dma_start(pos_nat, pos_enc[0]).then_inc(small_in, 16)
            for at, v in ((S_TB, tok_b), (S_G1, ln1_g), (S_B1, ln1_b), (S_G2, ln2_g), (S_B2, ln2_b), (S_GB, gate_bi)):
                n = v.shape[0] // P
                sp.dma_start(small_rows[at:at + n, :], v.rearrange("(n p) -> n p", p=P)).then_inc(small_in, 16)
            sp.dma_start(small_rows[S_CLS:S_CLS + DM, :], cls_token[0, 0, :].rearrange("(n p) -> n p", p=P)).then_inc(small_in, 16)
            sp.dma_start(small_rows[S_EB:S_EB + EXPERTS * FT, :], exp_bi.rearrange("e (n p) -> (e n) p", p=P)).then_inc(small_in, 16)
            sp.dma_start(wqk_s[:, :, 0:D], wq.rearrange("(k p) n -> p k n", p=P)).then_inc(weight_in, 16)
            sp.dma_start(wqk_s[:, :, D:2 * D], wk.rearrange("(k p) n -> p k n", p=P)).then_inc(weight_in, 16)
            sp.dma_start(wv_s[:], wv.rearrange("(k p) n -> p k n", p=P)).then_inc(weight_in, 16)
            sp.dma_start(wo_s[:], wo.rearrange("(k p) n -> p k n", p=P)).then_inc(weight_in, 16)
            sp.dma_start(w1_s, w1.rearrange("(k p) n -> p k n", p=P)).then_inc(weight_in, 16)
            sp.dma_start(w3_s, w3.rearrange("(k p) n -> p k n", p=P)).then_inc(weight_in, 16)
            whole = HIDDEN // P
            sp.dma_start(w2_s[:, 0:whole, :], w2[0:whole * P].rearrange("(k p) n -> p k n", p=P)).then_inc(weight_in, 16)
            sp.dma_start(w2_s[0:GLU[-1], whole, :], w2[whole * P:HIDDEN]).then_inc(weight_in, 16)
            sp.dma_start(gwi_s, gate_wi.rearrange("(k p) n -> p k n", p=P)).then_inc(weight_in, 16)
            sp.dma_start(gwo_s, gate_wo.rearrange("(k p) n -> p k n", p=P)).then_inc(weight_in, 16)
            sp.dma_start(gbo_s[:], gate_bo.rearrange("(a n) -> a n", a=1).to_broadcast([P, D])).then_inc(weight_in, 16)
            sp.wait_ge(const_ready, 3)
            sp.dma_start(rows[TOKENS:TOKENS + SLOTS, :], zero_rows[:]).then_inc(row_out, 16)
            def load_patches(g, more):
                sp.wait_ge(xp_ready, g * CH + 1)
                alone(sp)
                sp.dma_start(xin[0:GI * GRID, 0, :], x_rows[2, bass.ds(g * GI, GI)]).then_inc(x_in[2], 16)
                if more:
                    sp.wait_ge(xp_ready, g * CH + 2)
                    alone(sp)
                    sp.dma_start(xin[0:GI * GRID, 1, :], x_rows[1, bass.ds((g + 1) * GI, GI)]).then_inc(x_in[1], 16)
                    sp.wait_ge(xp_ready, g * CH + 3)
                    alone(sp)
                    sp.dma_start(xin[0:GI * GRID, 0, :], x_rows[0, bass.ds((g + 1) * GI, GI)]).then_inc(x_in[0], 16)

            def store_group(g):
                for t in range(NT):
                    read_of(sp, "loop", "w2", t, g=g)
                    alone(sp)
                store(sp, out, H2, g, h2_out)
                sp.wait_ge(weights_ready, g + 1)
                alone(sp)
                store(sp, rows, y, g, row_out)

            for c in range(2):
                sp.wait_ge(xp_ready, c + 1)
                sp.dma_start(xin[0:GI * GRID, c, :], x_rows[c, GI:2 * GI]).then_inc(x_in[c], 16)
            with sp.Fori(0, GROUPS - 2) as g:
                load_patches(g + 1, True)
                store_group(g)
            load_patches(LAST, False)
            store_group(LAST - 1)

            def load_expert(e):
                sp.dma_start(ewi[e % EBUFS], exp_wi[e].rearrange("(k p) n -> p k n", p=P)).then_inc(ew_in[e % EBUFS], 16)
                sp.dma_start(ewo[e % EBUFS], exp_wo[e].rearrange("(f p) n -> p f n", p=P)).then_inc(ew_in[e % EBUFS], 16)

            full_of(sp, "last", "out", 2 * PAIRS - 1)
            sp.dma_start(ebo, exp_bo.rearrange("(a e) n -> a e n", a=1)).then_inc(ebo_in, 16)
            load_expert(0)
            full_of(sp, "last", "w2", NT - 1)
            load_expert(1)
            full_of(sp, "last", "logit", NT - 1)
            load_expert(2)
            load_expert(3)
            sp.wait_ge(list_out, PRIMED + 16 * 2 * NT * (GROUPS + 1))

            def body(c):
                if not isinstance(c, int):
                    for e in range(EBUFS):
                        full_of(sp, E, "down", e + EBUFS, g=c - 1)
                        alone(sp)
                        load_expert(e)
                    for e in range(EXPERTS):
                        sp.wait_ge(added[e], PRIMED + 16 * c)
                        alone(sp)
                sp.dma_start(slot_tok[:], lists.rearrange("(e t) o -> t e o", e=EXPERTS)[bass.ds(c * SLOTS, SLOTS), :, 0],
                             allow_slow_non_contiguous=True).then_inc(slots_in, 16)
                for e in range(EBUFS, EXPERTS):
                    full_of(sp, E, "down", e - EBUFS, g=c)
                    alone(sp)
                    load_expert(e)
            expert_passes(sp, body)
            sp.wait_ge(h2_out, PRIMED + 16 * STORES * GROUPS)
            sp.wait_ge(row_out, PRIMED + 16 * STORES * GROUPS)

        @block.tensor
        def _(pe):
            def turn_tiles(S, job, src, g, f, tiles=range(NT)):
                for t in tiles:
                    a, n = TILES[t]
                    vacant_for(pe, S, job, t, g=g)
                    ready = {"a1": z1_ready, "a2": z2_ready, "y": y_ready}[job]
                    pe.wait_ge(ready, f * NT + t + 1)
                    for m in range(DM):
                        mm = pe.transpose(bank(S, job, t)[:, m * P:m * P + n], src[0:n, t, m * P:(m + 1) * P], ident[0:n, 0:n])
                    filled(mm, S, job, t)

            pe.wait_ge(con_in, 16)
            pe.wait_ge(tokw_in, 16)
            wnat = patT.rearrange("p k n -> p (k n)")[:, 0:DM * PK * P].rearrange("p (m f) -> p m f", m=DM)
            for k in range(PK):
                vacant_for(pe, "setup", "wt", k)
                for m in range(DM):
                    mm = pe.transpose(bank("setup", "wt", k)[:, m * P:(m + 1) * P], wnat[:, m, k * P:(k + 1) * P], ident)
                filled(mm, "setup", "wt", k)
            pe.wait_ge(small_in, 16 * 9)
            vacant_for(pe, "setup", "small", 0)
            filled(pe.transpose(bank("setup", "small", 0)[:, 0:S_ROWS], small_rows[0:S_ROWS, :], ident[0:S_ROWS, 0:S_ROWS]), "setup", "small", 0)
            vacant_for(pe, "setup", "posT", 0)
            for m in range(DM):
                mm = pe.transpose(bank("setup", "posT", 0)[:, m * SEQ:(m + 1) * SEQ], h0[0:SEQ, 0, m * P:(m + 1) * P], ident[0:SEQ, 0:SEQ])
            filled(mm, "setup", "posT", 0)
            pe.wait_ge(setup_done, 2)

            def patch(S, g, f, i):
                k, side = i // 2, i % 2
                c, upper = k // 2, k % 2
                if i % 4 == 0:
                    pe.wait_ge(xp_ready, f * CH + c + 1)
                vacant_for(pe, S, "patch", i, g=g)
                for j in range(3):
                    mm = pe.transpose(bank(S, "patch", i)[:, j * GI * GRID:(j + 1) * GI * GRID], xp[0:GI * GRID, upper, 3 * side + j, :],
                                      ident[0:GI * GRID, 0:GI * GRID])
                filled(mm, S, "patch", i)

            def embed(S, g, i):
                n, m = i // DM, i % DM
                vacant_for(pe, S, "embed", i, g=g)
                if i == 0:
                    all_read(pe, S, "patch", range(2 * PK), g)
                for k in range(PK):
                    mm = pe.matmul(bank(S, "embed", i)[:, 0:HALF], WT[:, k, m * P:(m + 1) * P], patT[:, k, n * HALF:(n + 1) * HALF],
                                   start=(k == 0), stop=(k == PK - 1))
                filled(mm, S, "embed", i)

            def tokens(S, g):
                for t, (a, n) in enumerate(TILES):
                    vacant_for(pe, S, "token", t, g=g)
                    if t in (0, 2):
                        all_read(pe, S, "embed", range(2 * DM if t else DM), g)
                    for m in range(DM):
                        mm = pe.transpose(bank(S, "token", t)[0:n, m * P:(m + 1) * P], h0T[:, m, a:a + n], ident)
                    filled(mm, S, "token", t)

            def values(S, g, f, i):
                vacant_for(pe, S, "v", i, g=g)
                pe.wait_ge(a1P_ready, f + 1)
                for j in range(2):
                    a = (2 * i + j) * P
                    for k in range(DM):
                        mm = pe.matmul(bank(S, "v", i)[:, j * D:(j + 1) * D], a1P[:, k, a:a + P], wv_s[:, k, :],
                                       start=(k == 0), stop=(k == DM - 1))
                filled(mm, S, "v", i)

            def project(S, g, f):
                turn_tiles(S, "a1", z, g, f)
                pe.wait_ge(weight_in, 16 * 11)
                for t, (a, n) in enumerate(TILES):
                    vacant_for(pe, S, "qk", t, g=g)
                    read_of(pe, S, "a1", t, g=g)
                    for k in range(DM):
                        mm = pe.matmul(bank(S, "qk", t)[0:n, :], a1T[:, k, a:a + n], wqk_s[:, k, :], start=(k == 0), stop=(k == DM - 1))
                    filled(mm, S, "qk", t)
                for i in range(EARLY_VALUES):
                    values(S, g, f, i)

            def turn_queries(S, g, f):
                for t, (a, n) in enumerate(TILES):
                    vacant_for(pe, S, "qkT", t, g=g)
                    pe.wait_ge(qk_ready, f * NT + t + 1)
                    for m in range(2 * DM):
                        mm = pe.transpose(bank(S, "qkT", t)[:, m * P:m * P + n], qk[0:n, t, m * P:(m + 1) * P], ident[0:n, 0:n])
                    filled(mm, S, "qkT", t)
                all_read(pe, S, "qkT", range(NT), g)

            def position(S, g):
                vacant_for(pe, S, "pos", 0, g=g)
                pe.wait_ge(sel_ready, g + 1)
                before = bank(S, "pos", 0)[:, 0:NT * EXPERTS].rearrange("p (t e) -> p t e", e=EXPERTS)
                pe.matmul(before, tri, sel[:], start=True, stop=False, skip_group_check=True)
                for back in range(1, NT):
                    pe.matmul(before[:, back:NT, :], ones[:], sel[:, 0:NT - back, :], start=False, stop=False, skip_group_check=True)
                filled(pe.matmul(before, ones[:], selcum[:].rearrange("p (a e) -> p a e", a=1).to_broadcast([P, NT, EXPERTS]),
                                 start=False, stop=True, skip_group_check=True), S, "pos", 0)

            def back(S, g, front):
                for kind, i in attention_steps(front):
                    if kind == "v":
                        values(S, g, g, i)
                        continue
                    if kind == "patch":
                        patch(S, g, g + 1, i)
                        continue
                    if kind == "embed":
                        embed(S, g, i)
                        continue
                    vacant_for(pe, S, kind, i, g=g)
                    if kind == "score":
                        pe.wait_ge(kx_ready, g * PAIRS + i + 1)
                        for r in range(2):
                            b = ps[:, banks.bank(S, "score", i) + r, 0:8 * SEQ]
                            pe.matmul(b, ident_bf[:], mask_bf[:], start=True, stop=False, skip_group_check=True)
                            for m in range(DM):
                                for j in range(2):
                                    a = (2 * i + j) * SEQ
                                    mm = pe.matmul(b.rearrange("p (h n) -> p h n", h=4)[PITCH * m:PITCH * (m + 1), :, j * SEQ:(j + 1) * SEQ],
                                                   qT[64 * r:64 * r + 64, m, a:a + PITCH], kx[64 * r:64 * r + 64, i % 2, m, :, j * SEQ:(j + 1) * SEQ],
                                                   start=False, stop=True, skip_group_check=True)
                    elif kind == "turn":
                        p, r = i // 2, i % 2
                        pe.wait_ge(probs_ready, g * PAIRS + p + 1)
                        for j in range(4):
                            src = probs[:, p % 3, (4 * r + j) * 2:(4 * r + j) * 2 + 2, :].rearrange("p a n -> p (a n)")
                            mm = pe.transpose(bank(S, kind, i)[:, j * P:(j + 1) * P], src, ident)
                    else:
                        pair, j = i // 2, i % 2
                        if i == 0:
                            all_read(pe, S, "v", range(EARLY_VALUES, PAIRS // 2), g)
                        if j == 0:
                            all_read(pe, S, "turn", (2 * pair, 2 * pair + 1), g)
                        alone(pe)
                        b = bank(S, kind, i)[:, 0:2 * 2 * SEQ].rearrange("p (m e c) -> p m e c", m=DM, e=2)
                        for m in range(DM):
                            for q in range(4):
                                r, s = q // 2, q % 2
                                pT = probsT[64 * j:64 * j + SEQ, pair % 2, r, :].rearrange("p (h n) -> p h n", h=4)
                                mm = pe.matmul(b[32 * q:32 * q + 32, m, :, :],
                                               V[64 * j:64 * j + SEQ, pair, m * P + 32 * q:m * P + 32 * q + 32],
                                               pT[:, 2 * s:2 * s + 2, PITCH * m:PITCH * m + SEQ], start=True, stop=True,
                                               skip_group_check=True)
                    filled(mm, S, kind, i)
                for kind, t in sum_steps(front):
                    if kind == "embed":
                        embed(S, g, t)
                        continue
                    if kind == "a2":
                        turn_tiles(S, "a2", z, g, g, (t,))
                        continue
                    a, n = TILES[t]
                    vacant_for(pe, S, "wo", t, g=g)
                    if t == 0:
                        all_read(pe, S, "out", range(2 * PAIRS), g)
                    for k in range(DM):
                        mm = pe.matmul(bank(S, "wo", t)[0:n, 0:D], attnT[:, k, a:a + n], wo_s[:, k, :], start=(k == 0), stop=(k == DM - 1))
                    filled(mm, S, "wo", t)
                for i in range(2 * len(GLU)):
                    n, f = i // len(GLU), i % len(GLU)
                    if i == len(GLU):
                        turn_tiles(S, "a2", z, g, g, BATCHES[n])
                    for kind, w in (("glu", w1_s), ("up", w3_s)):
                        vacant_for(pe, S, kind, i, g=g)
                        if kind == "glu" and f == 0:
                            all_read(pe, S, "a2", BATCHES[n], g)
                        for k in range(DM):
                            mm = pe.matmul(bank(S, kind, i)[0:GLU[f], 0:HALF], w[:, k, f * P:f * P + GLU[f]], a2T[:, k, n * HALF:(n + 1) * HALF],
                                           start=(k == 0), stop=(k == DM - 1))
                        filled(mm, S, kind, i)
                for t, (a, n) in enumerate(TILES):
                    vacant_for(pe, S, "w2", t, g=g)
                    if t in (0, 2):
                        all_read(pe, S, "up", range(len(GLU)) if t == 0 else range(len(GLU), 2 * len(GLU)), g)
                    for f, h in enumerate(GLU):
                        mm = pe.matmul(bank(S, "w2", t)[0:n, 0:D], gT[0:h, f, a:a + n], w2_s[0:h, f, :], start=(f == 0), stop=(f == len(GLU) - 1))
                    filled(mm, S, "w2", t)
                if front:
                    tokens(S, g)
                for i in range(2 * FT):
                    n, f = i // FT, i % FT
                    if f == 0:
                        turn_tiles(S, "y", y, g, g, BATCHES[n])
                    vacant_for(pe, S, "gate", i, g=g)
                    if f == 0:
                        all_read(pe, S, "y", BATCHES[n], g)
                    for k in range(DM):
                        mm = pe.matmul(bank(S, "gate", i)[:, 0:HALF], gwi_s[:, k, f * P:(f + 1) * P], yT[:, k, n * HALF:(n + 1) * HALF],
                                       start=(k == 0), stop=(k == DM - 1))
                    filled(mm, S, "gate", i)
                for t, (a, n) in enumerate(TILES):
                    vacant_for(pe, S, "logit", t, g=g)
                    if t in (0, 2):
                        pe.wait_ge(hid_ready, g * 2 * FT + (FT if t == 0 else 2 * FT))
                    for f in range(FT):
                        mm = pe.matmul(bank(S, "logit", t)[0:n, 0:D], hidT[:, f, a:a + n], gwo_s[:, f, :], start=(f == 0), stop=(f == FT - 1))
                    filled(mm, S, "logit", t)
                if front:
                    project(S, g, g + 1)
                position(S, g)
                if front:
                    turn_queries(S, g, g + 1)

            for i in range(2 * PK):
                patch("first", 0, 0, i)
            for i in range(2 * DM):
                embed("first", 0, i)
            tokens("first", 0)
            project("first", 0, 0)
            turn_queries("first", 0, 0)
            with pe.Fori(0, LAST) as g:
                back("loop", g, True)
            back("last", LAST, False)

            vacant_for(pe, "count", "all", 0)
            pe.wait_ge(dest_ready, GROUPS + 1)
            filled(pe.matmul(bank("count", "all", 0)[:, 0:EXPERTS], ones[:], selcum[:], start=True, stop=True), "count", "all", 0)

            def body(c):
                for kind, e in expert_steps():
                    vacant_for(pe, E, kind, e, g=c)
                    to = bank(E, kind, e)
                    if kind == "xT":
                        pe.wait_ge(gathered[e], 16 * (c + 1))
                        alone(pe)
                        for m in range(DM):
                            mm = pe.transpose(to[:, m * SLOTS:(m + 1) * SLOTS], xg[:, e, m * P:(m + 1) * P], ident[0:SLOTS, 0:SLOTS])
                    elif kind == "mid":
                        x, half = e // 2, e % 2
                        if half == 0:
                            pe.wait_ge(ew_in[x % EBUFS], 32 * (c * (EXPERTS // EBUFS) + x // EBUFS + 1))
                            alone(pe)
                            read_of(pe, E, "xT", x, g=c)
                        for k in range(DM):
                            mm = pe.matmul(to[0:SLOTS, :], xT[:, x % 2, k, :], ewi[x % EBUFS][:, k, half * FF // 2:(half + 1) * FF // 2],
                                           start=(k == 0), stop=(k == DM - 1))
                    elif kind == "hid":
                        all_read(pe, E, "mid", (2 * e, 2 * e + 1), c)
                        alone(pe)
                        for f in range(FT):
                            mm = pe.transpose(to[:, f * SLOTS:(f + 1) * SLOTS], raw[:, f * P:(f + 1) * P], ident[0:SLOTS, 0:SLOTS])
                    else:
                        pe.wait_ge(act_ready, c * EXPERTS + e + 1)
                        if e == 0:
                            pe.wait_ge(ebo_in, 16)
                        alone(pe)
                        pe.matmul(to[0:SLOTS, 0:D], ones[0:1, 0:SLOTS], ebo[:, e, :], start=True, stop=False)
                        for f in range(FT):
                            mm = pe.matmul(to[0:SLOTS, 0:D], ehT[:, e % 2, f, :], ewo[e % EBUFS][:, f, :], start=False, stop=(f == FT - 1))
                    filled(mm, E, kind, e)
            expert_passes(pe, body)

        @block.scalar
        def _(act):
            def turned(S, job, dst, g, scale=None, bias=None, tiles=range(NT)):
                for t in tiles:
                    a, n = TILES[t]
                    full_of(act, S, job, t, g=g)
                    if scale is None:
                        last = act.activation(dst[:, :, a:a + n], bank(S, job, t)[:, 0:DM * P].rearrange("p (m n) -> p m n", m=DM)[:, :, 0:n], ACT.Copy)
                    else:
                        for m in range(DM):
                            last = act.activation(dst[:, m, a:a + n], bank(S, job, t)[:, m * P:m * P + n], ACT.Identity,
                                                  scale=small[:, scale + m:scale + m + 1], bias=small[:, bias + m:bias + m + 1])
                    emptied(last, S, job, t)

            for k in range(PK):
                full_of(act, "setup", "wt", k)
                emptied(act.activation(WT[:, k, :], bank("setup", "wt", k)[:, 0:D], ACT.Copy), "setup", "wt", k)

            def patch(S, g, i):
                k, side = i // 2, i % 2
                full_of(act, S, "patch", i, g=g)
                dst = patT[:, k, :].rearrange("p (b s) -> p b s", s=SEQ)[:, :, 1:SEQ].rearrange("p b (n w) -> p b n w", w=GRID)
                src = bank(S, "patch", i)[:, 0:3 * GI * GRID].rearrange("p (w b n) -> p w b n", w=3, b=GI)
                for j in range(3):
                    last = act.activation(dst[:, :, :, 3 * side + j], src[:, j, :, :], ACT.Copy)
                emptied(last, S, "patch", i)

            def tokens(S, g):
                for t, (a, n) in enumerate(TILES):
                    full_of(act, S, "token", t, g=g)
                    if S == "loop":
                        read_of(act, S, "w2", t, g=g)
                    emptied(act.activation(h0[0:n, t, :], bank(S, "token", t)[0:n, 0:D], ACT.Copy), S, "token", t)

            def values(S, g, i):
                full_of(act, S, "v", i, g=g)
                emptied(act.activation(V[:, 2 * i:2 * i + 2, :].rearrange("p a n -> p (a n)"), bank(S, "v", i), ACT.Copy), S, "v", i)

            def project(S, g):
                turned(S, "a1", a1T, g, S_G1, S_B1)
                for i in range(EARLY_VALUES):
                    values(S, g, i)
                for t, (a, n) in enumerate(TILES):
                    full_of(act, S, "qkT", t, g=g)
                    src = bank(S, "qkT", t).rearrange("p (m n) -> p m n", m=2 * DM)
                    act.activation(kT[:, :, a:a + n], src[:, DM:2 * DM, 0:n], ACT.Copy).then_inc(kT_ready, 1)
                    emptied(act.activation(qT[:, :, a:a + n], src[:, 0:DM, 0:n], ACT.Copy, scale=float(HD) ** -0.5), S, "qkT", t)

            def back(S, g, front):
                for s in range(-1, PAIRS + 3):
                    if 0 <= s < PAIRS:
                        read_of(act, S, "score", s, g=g)
                        if s >= 3:
                            full_of(act, S, "turn", 2 * (s - 3) + 1, g=g)
                        act.activation(probs[:, s % 3, :, 0:SEQ], shifted[:, s % 2, :].rearrange("p (h n) -> p h n", n=SEQ),
                                       ACT.Exp).then_inc(exp_ready, 1)
                    if s in VALUE_STEPS:
                        values(S, g, EARLY_VALUES + VALUE_STEPS.index(s))
                    if front and s in PATCH_STEPS:
                        for i in range(4 * (s + 1), 4 * (s + 2)):
                            patch(S, g, i)
                    if 2 <= s < PAIRS + 2:
                        for r in range(2):
                            i = 2 * (s - 2) + r
                            full_of(act, S, "turn", i, g=g)
                            emptied(act.activation(probsT[:, (s - 2) % 2, r, :], bank(S, "turn", i), ACT.Copy), S, "turn", i)
                    if s >= 3:
                        i = s - 3
                        full_of(act, S, "out", 2 * i + 1, g=g)
                        if i >= 2:
                            read_of(act, S, "out", 2 * (i - 2) + 1, g=g)
                        b = banks.bank(S, "out", 2 * i)
                        assert banks.bank(S, "out", 2 * i + 1) == b + 1
                        src = ps[:, b:b + 2, 0:2 * 2 * SEQ].rearrange("p j (m e c) -> p m j e c", m=DM, e=2)
                        act.activation(even[:, i % 2, :, :].rearrange("p m (j c) -> p m j c", j=2), src[:, :, :, 0, :], ACT.Copy, scale=con[:, C_PAR:C_PAR + 1]).then_inc(even_ready, 1)
                for i in range(2 * len(GLU)):
                    f = i % len(GLU)
                    if f == 0:
                        turned(S, "a2", a2T, g, S_G2, S_B2, BATCHES[i // len(GLU)])
                    full_of(act, S, "glu", i, g=g)
                    if i >= 4:
                        read_of(act, S, "up", i - 4, g=g)
                    act.activation(th[0:GLU[f], i % 4, :], bank(S, "glu", i)[0:GLU[f], 0:HALF], ACT.Tanh, scale=0.5).then_inc(th_ready, 1)
                if front:
                    tokens(S, g)
                for i in range(2 * FT):
                    f = i % FT
                    if f == 0:
                        turned(S, "y", yT, g, tiles=BATCHES[i // FT])
                    full_of(act, S, "gate", i, g=g)
                    if i >= 3:
                        act.wait_ge(hid_ready, g * 2 * FT + i - 2)
                    act.activation(ex[:, i % 3, :], bank(S, "gate", i)[:, 0:HALF], ACT.Exp, bias=gate_exp_bias[:, f:f + 1])
                    act.activation(lin[:, i % 3, :], bank(S, "gate", i)[:, 0:HALF], ACT.Relu, scale=LAMBDA,
                                   bias=gate_lin_bias[:, f:f + 1]).then_inc(free[banks.bank(S, "gate", i)], 1)
                if front:
                    project(S, g)

            act.wait_ge(setup_done, 2)
            for c in range(CH):
                for i in range(4 * c, 4 * c + 4):
                    patch("first", 0, i)
            tokens("first", 0)
            project("first", 0)
            with act.Fori(0, LAST) as g:
                back("loop", g, True)
            back("last", LAST, False)

            for t in range(NT):
                read_of(act, "last", "w2", t)
            store(act, out, H2, LAST, h2_out)
            act.wait_ge(weights_ready, GROUPS)
            store(act, rows, y, LAST, row_out)

            def body(c):
                for kind, e in expert_steps():
                    if kind == "xT":
                        full_of(act, E, "xT", e, g=c)
                        emptied(act.activation(xT[:, e % 2, :, :].rearrange("p m n -> p (m n)"), bank(E, "xT", e)[:, 0:DM * SLOTS], ACT.Copy), E, "xT", e)
                    elif kind == "mid":
                        full_of(act, E, "mid", e, g=c)
                        half = slice(e % 2 * FF // 2, (e % 2 + 1) * FF // 2)
                        emptied(act.activation(raw[:, half], bank(E, "mid", e)[0:SLOTS, :], ACT.Copy), E, "mid", e)
                    elif kind == "hid":
                        read_of(act, E, "hid", e, g=c)
                        act.activation(ee, pre, ACT.Exp, bias=con[:, C_LNLA:C_LNLA + 1])
                        act.activation(el, pre, ACT.Relu, scale=LAMBDA).then_inc(pre_ready, 1)
            expert_passes(act, body)

        @block.gpsimd
        def _(pool):
            pool.memset(ones[:], 1.0).then_inc(const_ready, 1)
            pool.memset(zero_rows[:], 0.0).then_inc(const_ready, 1)
            pool.memset(probs[:], 0.0)
            pool.memset(probsT[:], 0.0)
            pool.memset(qT[:, :, GT:], 0.0)
            pool.memset(selcum[:], 0.0)
            pool.memset(minus_half[:], -0.5)
            pool.memset(v8[:], 1.0)
            pool.memset(i8[:], 0)
            pool.wait_ge(con_in, 16)
            pool.tensor_copy(ident_bf[:], ident)
            pool.tensor_copy(mask_bf[:], con[:, C_MASK:C_MASK + 8 * SEQ]).then_inc(setup_done, 1)
            pool.wait_ge(const_ready, 3)
            quarter = EXPERTS * CHUNKS // 4
            pool.dma_start(lists.rearrange("(q c s) o -> q c (s o)", s=SLOTS, c=4),
                           pad_row[0:quarter, :].rearrange("q (a s) -> q a s", a=1).to_broadcast([quarter, 4, SLOTS])).then_inc(list_out, 16)
            pad = SLOTS // EXPERTS
            for b in range(EXPERTS):
                pool.dma_start(out[TOKENS + b * pad:TOKENS + (b + 1) * pad, :], zero_rows[0:pad, 0:D]).then_inc(added[b], 16)

            def inverse_deviation(which, g):
                for b, tiles in enumerate(BATCHES):
                    done = (g * 4 + which) * 2 + b + 1
                    own = slice(tiles[0], tiles[-1] + 1)
                    pool.wait_ge(var_ready, done)
                    alone(pool)
                    pool.tensor_scalar(var_eps[:, own], mv[:, own, 1], EPS, None, ALU.add).then_inc(pool_step, 1)
                    pool.wait_ge(pool_step, done)
                    pool.tensor_tensor(rstd[:, own], var_eps[:, own], minus_half[:, own], ALU.pow).then_inc(rstd_ready, 1)

            def project(S, g, f):
                for t in range(NT):
                    read_of(pool, S, "a1", t, g=g)
                alone(pool)
                pool.tensor_copy(a1P.rearrange("p m (i n) -> p m i n", n=PITCH)[:, :, :, 0:SEQ],
                                 a1T[:].rearrange("p m (i n) -> p m i n", n=SEQ)).then_inc(a1P_ready, 1)
                for t, (a, n) in enumerate(TILES):
                    read_of(pool, S, "qk", t, g=g)
                    pool.tensor_tensor(qk[0:n, t, :], qk[0:n, t, :], swapped[0:n, t % 2, :], ALU.add).then_inc(qk_ready, 1)

            def spread_keys(S, g, i):
                last_tile = min(NT - 1, ((i + 1) * 2 * SEQ - 1) // P)
                pool.wait_ge(kT_ready, g * NT + last_tile + 1)
                if i >= 2:
                    full_of(pool, S, "score", i - 2, g=g)
                for m in range(DM):
                    last = pool.tensor_tensor(
                        kx[:, i % 2, m, :, :],
                        kT[:, m:m + 1, i * 2 * SEQ:(i + 1) * 2 * SEQ].to_broadcast([P, 4, 2 * SEQ]),
                        con[:, C_HEAD:C_HEAD + 4].rearrange("p (h a) -> p h a", a=1).to_broadcast([P, 4, 2 * SEQ]), ALU.mult)
                last.then_inc(kx_ready, 1)

            def list_tile(t):
                n = TILES[t][1]
                for k in range(2):
                    pool.indirect_dma_start(out=lists, out_offset=bass.IndirectOffsetOnAxis(ap=dest[0:n, k, t:t + 1], axis=0),
                                            in_=tok[0:n, t:t + 1], in_offset=None, bounds_check=EXPERTS * TOKENS - 1,
                                            oob_is_err=False).then_inc(list_out, 16)

            def back(S, g, front):
                spread_keys(S, g, 0)
                spread_keys(S, g, 1)
                for s in range(PAIRS):
                    pool.wait_ge(share_ready, g * PAIRS + s + 1)
                    pool.tensor_tensor(probs[:, s % 3, :, 0:SEQ], probs[:, s % 3, :, 0:SEQ],
                                       share[:, s % 2, :].rearrange("p (h a) -> p h a", a=1).to_broadcast([P, 16, SEQ]),
                                       ALU.mult).then_inc(probs_ready, 1)
                    if s + 2 < PAIRS:
                        spread_keys(S, g, s + 2)
                    if s == 2:
                        pool.wait_ge(dest_ready, g + 1)
                        alone(pool)
                        pool.wait_ge(list_out, PRIMED)
                    if 2 <= s < 2 + NT:
                        list_tile(s - 2)
                inverse_deviation(2, g)
                for t, (a, n) in enumerate(TILES):
                    read_of(pool, S, "wo", t, g=g)
                    pool.tensor_tensor(res[0:n, t, :], h0[0:n, t, :], h1[0:n, t, :], ALU.add).then_inc(res_ready, 1)
                inverse_deviation(3, g)
                if front:
                    inverse_deviation(4, g)
                    inverse_deviation(5, g)
                    project(S, g, g + 1)

            inverse_deviation(0, 0)
            inverse_deviation(1, 0)
            project("first", 0, 0)
            with pool.Fori(0, LAST) as g:
                back("loop", g, True)
            back("last", LAST, False)
            pool.wait_ge(dest_ready, GROUPS + 1)
            for t in range(NT):
                list_tile(t)

            pool.wait_ge(row_out, PRIMED + 16 * STORES * GROUPS)
            pool.wait_ge(h2_out, PRIMED + 16 * STORES * GROUPS)

            def body(c):
                pool.wait_ge(slots_in, 16 * (c + 1))
                alone(pool)
                for e in range(EXPERTS):
                    pool.indirect_dma_start(out=xg[:, e, :], out_offset=None, in_=rows,
                                            in_offset=bass.IndirectOffsetOnAxis(ap=slot_tok[:, e:e + 1], axis=0)).then_inc(gathered[e], 16)
                for e in range(EXPERTS):
                    read_of(pool, E, "down", e, g=c)
                    if e:
                        pool.wait_ge(added[e - 1], PRIMED + 16 * (c + 1))
                    alone(pool)
                    pool.indirect_dma_start(out=out, out_offset=bass.IndirectOffsetOnAxis(ap=slot_tok[:, e:e + 1], axis=0),
                                            in_=ye[:, e % 2, :], in_offset=None, compute_op=ALU.add).then_inc(added[e], 16)
                pool.wait_ge(added[EXPERTS - 1], PRIMED + 16 * (c + 1))
            expert_passes(pool, body)

        @block.vector
        def _(dve):
            class Chain:
                def __init__(self, before):
                    self.before, self.n = before, 0

                def step(self, ins):
                    ins.then_inc(vector_step, 1)
                    self.n += 1

                def wait(self):
                    dve.wait_ge(vector_step, self.before + self.n)

            FIRST_STEPS, LOOP_STEPS = 5, 39

            def norm(which, dst, src, chain, ready, g, product=None, meanwhile=None):
                def statistics(t):
                    n = TILES[t][1]
                    return dve.bn_stats(stats[0:n, t, :], src[0:n, t, :])

                def variances(tiles):
                    for t in tiles:
                        if product is None:
                            last = statistics(t)
                            continue
                        product[0](t)
                        if t > tiles[0]:
                            product[1](t - 1)
                            statistics(t - 1)
                    if product is not None:
                        product[1](t)
                        last = statistics(t)
                    chain.step(last)
                    chain.wait()
                    alone(dve)
                    for t in tiles:
                        n = TILES[t][1]
                        last = dve.bn_aggr(mv[0:n, t, :], stats[0:n, t, :])
                    last.then_inc(var_ready, 1)

                for b, tiles in enumerate(BATCHES):
                    if product is None:
                        if b == 0:
                            variances(BATCHES[0])
                            variances(BATCHES[1])
                    else:
                        variances(tiles)
                    if b == 0 and meanwhile is not None:
                        meanwhile()
                    dve.wait_ge(rstd_ready, (g * 4 + which) * 2 + b + 1)
                    for t in tiles:
                        n = TILES[t][1]
                        ins = dve.tensor_scalar(dst[0:n, t, 0:D], src[0:n, t, :], mv[0:n, t, 0:1], rstd[0:n, t:t + 1], ALU.subtract, ALU.mult)
                        if ready is not None:
                            ins.then_inc(ready, 1)
                if ready is None:
                    chain.step(ins)
                    chain.wait()

            dve.memset(mv[:], 1.0)
            dve.memset(tok[:], 0)
            dve.memset(dest[:], EXPERTS * TOKENS).then_inc(dest_ready, 1)
            dve.wait_ge(con_in, 16)
            dve.tensor_copy(tokf[:], con[:, C_TOK:C_TOK + NT])
            dve.tensor_copy(pad_row[:], con[:, C_PAD:C_PAD + SLOTS]).then_inc(const_ready, 1)
            full_of(dve, "setup", "small", 0)
            dve.tensor_copy(small[:, 0:S_ROWS], bank("setup", "small", 0)[:, 0:S_ROWS]).then_inc(free[banks.bank("setup", "small", 0)], 1)
            read_of(dve, "setup", "small", 0)
            dve.tensor_scalar(gate_exp_bias[:], small[:, S_GB:S_GB + FT], con[:, C_LNLA:C_LNLA + 1], None, ALU.add)
            dve.tensor_scalar(gate_lin_bias[:], small[:, S_GB:S_GB + FT], LAMBDA, None, ALU.mult)
            full_of(dve, "setup", "posT", 0)
            for m in range(DM):
                src = bank("setup", "posT", 0)[:, m * SEQ:(m + 1) * SEQ]
                dve.tensor_scalar(posT[:, m, 1:SEQ], src[:, 1:SEQ], small[:, S_TB + m:S_TB + m + 1], None, ALU.add)
                last = dve.tensor_scalar(posT[:, m, 0:1], src[:, 0:1], small[:, S_CLS + m:S_CLS + m + 1], None, ALU.add)
            emptied(last, "setup", "posT", 0)
            read_of(dve, "setup", "wt", PK - 1)
            dve.memset(patT.rearrange("p k (b s) -> p k b s", s=SEQ)[:, :, :, 0], 0.0).then_inc(setup_done, 1)

            def take_pixels(S, g, f, c):
                dve.wait_ge(x_in[c], 16 * (f + 1))
                if c:
                    full_of(dve, S, "patch", 4 * c - 1, g=g)
                source = xin2 if S == "first" and c == 2 else xin[:, c % 2, :]
                for upper in range(2):
                    last = dve.tensor_copy(xp[0:GI * GRID, upper, :, :].rearrange("p w (r x) -> p r w x", x=PATCH),
                                          source[0:GI * GRID, upper * 8 * SIDE:(upper + 1) * 8 * SIDE].rearrange("p (r w x) -> p r w x", w=GRID, x=PATCH))
                last.then_inc(xp_ready, 1)

            def embed(S, g, i):
                n, m = i // DM, i % DM
                full_of(dve, S, "embed", i, g=g)
                dst = h0T[:, m, n * HALF:(n + 1) * HALF].rearrange("p (b s) -> p b s", s=SEQ)
                src = bank(S, "embed", i)[:, 0:HALF].rearrange("p (b s) -> p b s", s=SEQ)
                dve.tensor_copy(dst[:, :, 0:1], posT[:, m:m + 1, 0:1].to_broadcast([P, GI // 2, 1]))
                emptied(dve.tensor_tensor(dst[:, :, 1:SEQ], src[:, :, 1:SEQ],
                                          posT[:, m:m + 1, 1:SEQ].to_broadcast([P, GI // 2, SEQ - 1]), ALU.add), S, "embed", i)

            def rotate(S, g, f):
                for t, (a, n) in enumerate(TILES):
                    full_of(dve, S, "qk", t, g=g)
                    if t >= 2:
                        dve.wait_ge(qk_ready, f * NT + t - 1)
                    src = bank(S, "qk", t)[0:n, :].rearrange("p (h c) -> p h c", c=HD)
                    heads = 2 * HEADS

                    def table(at):
                        return con[0:n, at + t * HD:at + (t + 1) * HD].rearrange("p (a c) -> p a c", a=1)
                    dve.tensor_tensor(qk[0:n, t, :].rearrange("p (h c) -> p h c", c=HD), src, table(C_COS).to_broadcast([n, heads, HD]), ALU.mult)
                    for e in range(2):
                        ins = dve.tensor_tensor(swapped[0:n, t % 2, :].rearrange("p (h c) -> p h c", c=HD)[:, :, e::2], src[:, :, 1 - e::2],
                                                table(C_SIN)[:, :, e::2].to_broadcast([n, heads, HD // 2]), ALU.mult)
                    emptied(ins, S, "qk", t)

            def hidden(S, g, half):
                for i in range(half * FT, (half + 1) * FT):
                    n, f = i // FT, i % FT
                    read_of(dve, S, "gate", i, g=g)
                    dve.scalar_tensor_tensor(hidT[:, f, n * HALF:(n + 1) * HALF], ex[:, i % 3, :], LA, lin[:, i % 3, :], ALU.subtract, ALU.min).then_inc(hid_ready, 1)

            def back(S, g, front):
                ch = Chain(FIRST_STEPS + g * LOOP_STEPS)
                if front:
                    take_pixels(S, g, g + 1, 0)
                    take_pixels(S, g, g + 1, 1)
                for s in range(PAIRS + 3):
                    if s < PAIRS:
                        full_of(dve, S, "score", s, g=g)
                        b = banks.bank(S, "score", s)
                        src = ps[:, b:b + 2, 0:8 * SEQ].rearrange("p r (h n) -> p r h n", n=SEQ)
                        mx = top[:, s % 2, :].rearrange("p (r h) -> p r h", r=2)
                        ch.step(dve.tensor_reduce(mx, src, AX.X, ALU.max))
                        ch.wait()
                        emptied(dve.tensor_tensor(shifted[:, s % 2, :].rearrange("p (r h n) -> p r h n", r=2, n=SEQ), src,
                                                  mx.rearrange("p r (h a) -> p r h a", a=1).to_broadcast([P, 2, 8, SEQ]), ALU.subtract),
                                S, "score", s)
                        dve.wait_ge(exp_ready, g * PAIRS + s + 1)
                        ch.step(dve.tensor_reduce(total[:, s % 2, :], probs[:, s % 3, :, 0:SEQ], AX.X, ALU.add))
                        ch.wait()
                        dve.reciprocal(share[:, s % 2, :], total[:, s % 2, :]).then_inc(share_ready, 1)
                    if front and s == 0:
                        take_pixels(S, g, g + 1, 2)
                    if front and s in EMBED_STEPS:
                        embed(S, g, EMBED_STEPS.index(s))
                    if s >= 3:
                        i = s - 3
                        dve.wait_ge(even_ready, g * PAIRS + i + 1)
                        for j in range(2):
                            src = bank(S, "out", 2 * i + j)[:, 0:2 * 2 * SEQ].rearrange("p (m e c) -> p m e c", m=DM, e=2)
                            a = (2 * i + j) * SEQ
                            emptied(dve.scalar_tensor_tensor(attnT[:, :, a:a + SEQ], src[:, :, 1, :], con[:, C_PAR + 1:C_PAR + 2],
                                                             even[:, i % 2, :, j * SEQ:(j + 1) * SEQ], ALU.mult, ALU.add), S, "out", 2 * i + j)
                def attention_sum(t):
                    n = TILES[t][1]
                    full_of(dve, S, "wo", t, g=g)
                    emptied(dve.tensor_tensor(h1[0:n, t, :], bank(S, "wo", t)[0:n, 0:D], u[0:n, t, :], ALU.add), S, "wo", t)

                def last_embeds():
                    if front:
                        for i in range(len(EMBED_STEPS), 2 * DM):
                            embed(S, g, i)
                norm(2, z, h1, ch, z2_ready, g, (attention_sum, lambda t: read_of(dve, S, "wo", t, g=g)), last_embeds)
                for i in range(2 * len(GLU)):
                    n, f = i // len(GLU), i % len(GLU)
                    h = GLU[f]
                    dve.wait_ge(th_ready, g * 2 * len(GLU) + i + 1)
                    full_of(dve, S, "up", i, g=g)
                    emptied(dve.scalar_tensor_tensor(th[0:h, i % 4, :], th[0:h, i % 4, :], 1.0, bank(S, "glu", i)[0:h, 0:HALF], ALU.add, ALU.mult), S, "glu", i)
                    read_of(dve, S, "glu", i, g=g)
                    emptied(dve.scalar_tensor_tensor(gT[0:h, f, n * HALF:(n + 1) * HALF], th[0:h, i % 4, :], 0.5, bank(S, "up", i)[0:h, 0:HALF], ALU.mult, ALU.mult), S, "up", i)
                dve.wait_ge(h2_out, PRIMED + g * STORES * 16)
                dve.wait_ge(row_out, PRIMED + g * STORES * 16)

                def unit_sum(t):
                    n = TILES[t][1]
                    dve.wait_ge(res_ready, g * NT + t + 1)
                    full_of(dve, S, "w2", t, g=g)
                    emptied(dve.tensor_tensor(H2[0:n, t, :], bank(S, "w2", t)[0:n, 0:D], res[0:n, t, :], ALU.add), S, "w2", t)
                norm(3, y, H2, ch, y_ready, g, (unit_sum, lambda t: read_of(dve, S, "w2", t, g=g)))
                if front:
                    for t in range(NT):
                        read_of(dve, S, "token", t, g=g)
                    norm(4, u, h0, ch, None, g)
                hidden(S, g, 0)
                if front:
                    norm(5, z, u, ch, z1_ready, g)
                hidden(S, g, 1)
                for t, (a, n) in enumerate(TILES):
                    full_of(dve, S, "logit", t, g=g)
                    emptied(dve.tensor_tensor(logits[0:n, t % 2, :], bank(S, "logit", t)[0:n, 0:D], gbo_s[0:n, :], ALU.add), S, "logit", t)
                    read_of(dve, S, "logit", t, g=g)
                    alone(dve)
                    ch.step(dve.max(v8[0:n, t, :], logits[0:n, t % 2, :]))
                    ch.wait()
                    alone(dve)
                    ins = dve.max_index(i8[0:n, t, :], v8[0:n, t, :], logits[0:n, t % 2, :])
                ch.step(ins)
                ch.wait()
                if front:
                    rotate(S, g, g + 1)
                dve.tensor_copy(idxf[:].rearrange("p k t -> p t k"), i8[:, :, 0:2])
                ch.step(dve.tensor_tensor(vsum[:], v8[:, :, 0:1], v8[:, :, 1:2], ALU.add))
                ch.wait()
                ch.step(dve.reciprocal(vinv[:], vsum[:]))
                iota = con[:, C_IOTA:C_IOTA + NT * EXPERTS].rearrange("p (t e) -> p t e", e=EXPERTS)
                for k in range(2):
                    ins = dve.tensor_tensor(pick[:, k, :, :], iota, idxf[:, k, :].rearrange("p (t a) -> p t a", a=1).to_broadcast([P, NT, EXPERTS]), ALU.is_equal)
                ch.step(ins)
                ch.wait()
                ch.step(dve.tensor_tensor(wts[:], v8[:, :, 0:2], vinv[:].to_broadcast([P, NT, 2]), ALU.mult))
                dve.tensor_tensor(sel[:], pick[:, 0, :, :], pick[:, 1, :, :], ALU.add).then_inc(sel_ready, 1)
                ch.wait()
                for k in range(2):
                    ins = dve.tensor_tensor(part[:, k, :, :], pick[:, k, :, :], wts[:, :, k:k + 1].to_broadcast([P, NT, EXPERTS]), ALU.mult)
                ch.step(ins)
                ch.wait()
                dve.tensor_tensor(y[:, :, D:ROW], part[:, 0, :, :], part[:, 1, :, :], ALU.add).then_inc(weights_ready, 1)
                dve.wait_ge(weights_ready, g + 1)
                full_of(dve, S, "pos", 0, g=g)
                before = bank(S, "pos", 0)[:, 0:NT * EXPERTS].rearrange("p (t e) -> p t e", e=EXPERTS)
                for k in range(2):
                    ins = dve.tensor_tensor(part[:, k, :, :], pick[:, k, :, :], before, ALU.mult)
                emptied(ins, S, "pos", 0)
                read_of(dve, S, "pos", 0, g=g)
                ch.step(dve.tensor_reduce(place[:], part[:], AX.X, ALU.add))
                ch.step(dve.tensor_reduce(selsum[:], sel[:].rearrange("p t e -> p e t"), AX.X, ALU.add))
                ch.wait()
                dve.wait_ge(list_out, PRIMED + (g + 1) * 2 * NT * 16)
                dve.tensor_tensor(selcum[:], selcum[:], selsum[:], ALU.add)
                dve.tensor_copy(tok[:], tokf[:])
                ch.step(dve.scalar_tensor_tensor(dest[:], idxf[:], float(TOKENS), place[:], ALU.mult, ALU.add))
                ch.wait()
                dve.tensor_scalar(tokf[:], tokf[:], float(GT), None, ALU.add).then_inc(dest_ready, 1)
                assert not front or ch.n == LOOP_STEPS, ch.n

            for c in range(CH):
                take_pixels("first", 0, 0, c)
            for i in range(2 * DM):
                embed("first", 0, i)
            for t in range(NT):
                read_of(dve, "first", "token", t)
            ch = Chain(0)
            norm(0, u, h0, ch, None, 0)
            norm(1, z, u, ch, z1_ready, 0)
            assert ch.n == FIRST_STEPS, ch.n
            rotate("first", 0, 0)
            with dve.Fori(0, LAST) as g:
                back("loop", g, True)
            back("last", LAST, False)

            full_of(dve, "count", "all", 0)
            dve.tensor_reduce(most[:], bank("count", "all", 0)[:, 0:EXPERTS], AX.X, ALU.max).then_inc(free[banks.bank("count", "all", 0)], 1)
            read_of(dve, "count", "all", 0)
            dve.tensor_scalar(flag_u[:], most[:], float(SLOTS), None, ALU.is_gt).then_inc(flag_ready, 1)

            def body(c):
                for kind, e in expert_steps():
                    if kind not in ("hid", "down"):
                        continue
                    full_of(dve, E, kind, e, g=c)
                    if kind == "hid":
                        bias = small[:, S_EB + e * FT:S_EB + (e + 1) * FT].rearrange("p (f a) -> p f a", a=1)
                        emptied(dve.tensor_tensor(pre, bank(E, "hid", e).rearrange("p (f n) -> p f n", f=FT),
                                                  bias.to_broadcast([P, FT, SLOTS]), ALU.add), E, "hid", e)
                        dve.wait_ge(pre_ready, c * EXPERTS + e + 1)
                        dve.scalar_tensor_tensor(ehT[:, e % 2, :, :], ee, LA, el, ALU.subtract, ALU.min).then_inc(act_ready, 1)
                    else:
                        if e >= 2:
                            dve.wait_ge(added[e - 2], PRIMED + 16 * (c + 1))
                        elif not isinstance(c, int):
                            dve.wait_ge(added[EXPERTS - 2 + e], PRIMED + 16 * c)
                        emptied(dve.tensor_scalar(ye[:, e % 2, :], bank(E, "down", e)[0:SLOTS, 0:D],
                                                  xg[:, e, D + e:D + e + 1], None, ALU.mult), E, "down", e)
            expert_passes(dve, body)


_INS = ['x', 'L0_tok_W', 'L0_tok_b', 'L0_tok_cls_token', 'L0_tok_pos_enc', 'L0_attn_wq', 'L0_attn_wk', 'L0_attn_wv', 'L0_attn_wo',
        'L0_attn_w1', 'L0_attn_w2', 'L0_attn_w3', 'L0_attn_ln1_g', 'L0_attn_ln1_b', 'L0_attn_ln2_g', 'L0_attn_ln2_b',
        'L0_ffn_gate_wi', 'L0_ffn_gate_bi', 'L0_ffn_gate_wo', 'L0_ffn_gate_bo', 'L0_ffn_exp_wi', 'L0_ffn_exp_bi', 'L0_ffn_exp_wo', 'L0_ffn_exp_bo']


def kernel(**inputs):
    import numpy as _np
    import concourse.bacc as _bacc
    from concourse import mybir as _mybir
    from concourse.bass_utils import run_bass_kernel_spmd as _run

    nc = _bacc.Bacc("TRN2", target_bir_lowering=False, num_devices=1)
    arrays, args = {}, []
    for name in _INS:
        a = _np.ascontiguousarray(inputs[name])
        arrays[f"in_{name}"] = a
        args.append(nc.dram_tensor(f"in_{name}", a.shape, _mybir.dt.from_np(a.dtype), kind="ExternalInput").ap())
    arrays["const"] = constants()
    args.append(nc.dram_tensor("const", arrays["const"].shape, F32, kind="ExternalInput").ap())
    args.append(nc.dram_tensor("out_0", (TOKENS + SLOTS, D), F32, kind="ExternalOutput").ap())
    build(nc, *args)
    r = _run(nc, [arrays], core_ids=[0])
    return r.results[0]["out_0"][:TOKENS].reshape(IMAGES, SEQ, D)
```
